# Optimizing a Trainium2 kernel written in Bass

```python
import numpy as np
import jax
import jax.numpy as jnp

def _softmax(x, axis=-1):
    return jax.nn.softmax(x, axis=axis)

def _gelu(x):
    return jax.nn.gelu(x, approximate=True)

def _silu(x):
    return jax.nn.silu(x)

def _sigmoid(x):
    return jax.nn.sigmoid(x)

def _layernorm(x, axis=-1, eps=1e-05):
    m = jnp.mean(x, axis=axis, keepdims=True)
    v = jnp.var(x, axis=axis, keepdims=True)
    return (x - m) / jnp.sqrt(v + eps)

def _scatter_add(tgt, idx, src, axis=0):
    return tgt.at[idx].add(src)

def _segment_sum(src, seg, n):
    return jax.ops.segment_sum(src, seg, n)
kernel_name = 'mk_gnn_ffn_d2_gnn_r32_b5c84f'

def setup_inputs(seed: int=0):
    np.random.seed(seed)
    _w = jnp.asarray

    def _rec_inputs():
        import jax
        import jax.numpy as jnp
        _gk = jax.random.key(seed)
        x = -8.776e-05 + 1 * jax.random.normal(jax.random.fold_in(_gk, 1), (10000, 512), jnp.float32)
        src = jax.random.randint(jax.random.fold_in(_gk, 2), (5000,), 0, 10000, jnp.int32)
        dst = jax.random.randint(jax.random.fold_in(_gk, 3), (5000,), 0, 10000, jnp.int32)
        _o = jnp.argsort(dst, stable=True)
        src = src[_o]
        dst = dst[_o]
        edge_type_2 = jax.random.randint(jax.random.fold_in(_gk, 12), (5000,), 0, 2, jnp.int32)
        edge_weight1 = -0.00598325 + 0.997157 * jax.random.normal(jax.random.fold_in(_gk, 13), (5000, 1), jnp.float32)
        return (x, src, dst, edge_type_2, edge_weight1)
    x, src, dst, edge_type_2, edge_weight1 = _rec_inputs()

    def _L0_gnn_setup():
        import jax, jax.numpy as jnp
        import numpy as np
        NUM_RELATIONS = 2
        NUM_BASES = 30
        HIDDEN = 512
        N_NODES = 10000
        N_EDGES = 5000

        def rgcn_gate_layer(x, row, col, edge_type, basis, att, gate_w, root, bias):
            H = x.shape[1]
            w = jnp.einsum('rb,bio->rio', att, basis)
            x_j = x[col]
            msgs = []
            for r in range(NUM_RELATIONS):
                gate = jax.nn.sigmoid(x_j @ gate_w[r, :, 0])
                msgs.append(gate[:, None] * x_j @ w[r])
            msg = jnp.where((edge_type == 0)[:, None], msgs[0], msgs[1])
            agg = jax.ops.segment_sum(msg, row, num_segments=x.shape[0])
            return agg + x @ root + bias
        key = jax.random.key(seed)
        ks = jax.random.split(key, 16)
        H, R, B = (HIDDEN, NUM_RELATIONS, NUM_BASES)
        bound = 1.0 / np.sqrt(B * H)
        u = lambda k, shape: jax.random.uniform(k, shape, jnp.float32, -bound, bound)
        inp = {'x': jax.random.normal(ks[0], (N_NODES, H), jnp.float32), 'edge_index': jax.random.randint(ks[1], (2, N_EDGES), 0, N_NODES, jnp.int32), 'edge_type': jax.random.randint(ks[2], (N_EDGES,), 0, R, jnp.int32), 'basis1': u(ks[3], (B, H, H)), 'att1': u(ks[4], (R, B)), 'gate_w1': u(ks[5], (R, H, 1)), 'root1': u(ks[6], (H, H)), 'bias1': u(ks[7], (H,)), 'basis2': u(ks[8], (B, H, H)), 'att2': u(ks[9], (R, B)), 'gate_w2': u(ks[10], (R, H, 1)), 'root2': u(ks[11], (H, H)), 'bias2': u(ks[12], (H,))}
        return inp
    _L0_gnn_all = _L0_gnn_setup()
    _L0_gnn_in = {k: v for k, v in _L0_gnn_all.items() if k in ('basis1', 'att1', 'gate_w1', 'root1', 'bias1', 'basis2', 'att2', 'gate_w2', 'root2', 'bias2')}
    del _L0_gnn_all

    def _L0_ffn_setup():
        import jax, jax.numpy as jnp
        import numpy as np
        D, H, E, B, S = (512, 64, 16, 8, 256)
        MAX_GROUP_SIZE = 128
        MIN_CAPACITY = 8
        CAPACITY_FACTOR = 1.0

        def _group_dims(num_tokens, num_experts):
            num_groups = -(-num_tokens // MAX_GROUP_SIZE)
            while num_tokens % num_groups != 0 or num_groups % num_experts != 0:
                num_groups += 1
            return (num_tokens // num_groups, num_groups)
        key = jax.random.key(seed)
        ks = jax.random.split(key, 6)
        s = 0.02
        return {'x': jax.random.normal(ks[0], (B, S, D), jnp.float32), 'gate_w': jax.random.normal(ks[1], (D, E), jnp.float32) * s, 'w1': jax.random.normal(ks[2], (E, D, H), jnp.float32) * s, 'b1': jnp.zeros((E, H), jnp.float32), 'w2': jax.random.normal(ks[3], (E, H, D), jnp.float32) * s, 'b2': jnp.zeros((E, D), jnp.float32), 'sw1': jax.random.normal(ks[4], (D, H), jnp.float32) * s, 'sb1': jnp.zeros((H,), jnp.float32), 'sw2': jax.random.normal(ks[5], (H, D), jnp.float32) * s, 'sb2': jnp.zeros((D,), jnp.float32)}
    _L0_ffn_all = _L0_ffn_setup()
    _L0_ffn_in = {k: v for k, v in _L0_ffn_all.items() if k in ('gate_w', 'w1', 'b1', 'w2', 'b2', 'sw1', 'sb1', 'sw2', 'sb2')}
    del _L0_ffn_all

    def _L1_gnn_setup():
        import jax, jax.numpy as jnp
        import numpy as np
        N, D, E, L = (625, 512, 5000, 4)
        BN_EPS = 1e-05

        def _gine_layer(x, src, dst, edge_attr, eps, We, be, W1, b1, gamma, beta, W2, b2):
            e = edge_attr @ We + be
            m = jax.nn.relu(x[src] + e)
            agg = jax.ops.segment_sum(m, dst, num_segments=x.shape[0])
            h = ((1.0 + eps) * x + agg) @ W1 + b1
            mu = jnp.mean(h, axis=0)
            var = jnp.mean(jnp.square(h - mu), axis=0)
            h = (h - mu) * jax.lax.rsqrt(var + BN_EPS) * gamma + beta
            h = jax.nn.relu(h)
            return jax.nn.relu(h @ W2 + b2)
        key = jax.random.key(seed)
        ks = jax.random.split(key, 10)
        x = jax.random.normal(ks[0], (N, D), dtype=jnp.float32)
        edge_index = jax.random.randint(ks[1], (2, E), 0, N, dtype=jnp.int64)
        edge_attr = jax.random.normal(ks[2], (E, 1), dtype=jnp.float32)
        s1 = 1.0 / np.sqrt(D)
        params = {'eps': jnp.zeros((L,), jnp.float32), 'We': jax.random.normal(ks[3], (L, 1, D), jnp.float32) * 1.0, 'be': jnp.zeros((L, D), jnp.float32), 'W1': jax.random.normal(ks[4], (L, D, D), jnp.float32) * s1, 'b1': jnp.zeros((L, D), jnp.float32), 'gamma': jnp.ones((L, D), jnp.float32), 'beta': jnp.zeros((L, D), jnp.float32), 'W2': jax.random.normal(ks[5], (L, D, D), jnp.float32) * s1, 'b2': jnp.zeros((L, D), jnp.float32)}
        return {'x': x, 'edge_index': edge_index, 'edge_attr': edge_attr, **params}
    _L1_gnn_all = _L1_gnn_setup()
    _L1_gnn_in = {k: v for k, v in _L1_gnn_all.items() if k in ('eps', 'We', 'be', 'W1', 'b1', 'gamma', 'beta', 'W2', 'b2')}
    del _L1_gnn_all

    def _L1_ffn_setup():
        import jax, jax.numpy as jnp
        import numpy as np
        EPS = 1e-05

        def _bitlinear(x, w):
            w_scale = jnp.clip(jnp.mean(jnp.abs(w)), EPS, None)
            w_q = jnp.clip(jnp.round(w / w_scale), -1.0, 1.0) * w_scale
            w_eff = w + jax.lax.stop_gradient(w_q - w)
            x_scale = 127.0 / jnp.clip(jnp.max(jnp.abs(x), axis=-1, keepdims=True), EPS, None)
            x_q = jnp.clip(jnp.round(x * x_scale), -128.0, 127.0) / x_scale
            x_eff = x + jax.lax.stop_gradient(x_q - x)
            return jnp.einsum('bsi,oi->bso', x_eff, w_eff)

        def _ste_round_clamp_int8(h):
            h_q = jnp.clip(jnp.round(h), -128.0, 127.0)
            return h + jax.lax.stop_gradient(h_q - h)
        key = jax.random.key(seed)
        k1, k2, k3 = jax.random.split(key, 3)
        B, S, D, F = (8, 256, 512, 64)
        x = jax.random.normal(k1, (B, S, D), dtype=jnp.float32)
        w_up = jax.random.normal(k2, (F, D), dtype=jnp.float32) * (1.0 / np.sqrt(D))
        w_down = jax.random.normal(k3, (D, F), dtype=jnp.float32) * (1.0 / np.sqrt(F))
        return {'x': x, 'w_up': w_up, 'w_down': w_down}
    _L1_ffn_all = _L1_ffn_setup()
    _L1_ffn_in = {k: v for k, v in _L1_ffn_all.items() if k in ('w_up', 'w_down')}
    del _L1_ffn_all
    return {'x': x, 'src': src, 'dst': dst, 'edge_type_2': edge_type_2, 'edge_weight1': edge_weight1, 'L0_gnn_basis1': _L0_gnn_in['basis1'], 'L0_gnn_att1': _L0_gnn_in['att1'], 'L0_gnn_gate_w1': _L0_gnn_in['gate_w1'], 'L0_gnn_root1': _L0_gnn_in['root1'], 'L0_gnn_bias1': _L0_gnn_in['bias1'], 'L0_gnn_basis2': _L0_gnn_in['basis2'], 'L0_gnn_att2': _L0_gnn_in['att2'], 'L0_gnn_gate_w2': _L0_gnn_in['gate_w2'], 'L0_gnn_root2': _L0_gnn_in['root2'], 'L0_gnn_bias2': _L0_gnn_in['bias2'], 'L0_ffn_gate_w': _L0_ffn_in['gate_w'], 'L0_ffn_w1': _L0_ffn_in['w1'], 'L0_ffn_b1': _L0_ffn_in['b1'], 'L0_ffn_w2': _L0_ffn_in['w2'], 'L0_ffn_b2': _L0_ffn_in['b2'], 'L0_ffn_sw1': _L0_ffn_in['sw1'], 'L0_ffn_sb1': _L0_ffn_in['sb1'], 'L0_ffn_sw2': _L0_ffn_in['sw2'], 'L0_ffn_sb2': _L0_ffn_in['sb2'], 'L1_gnn_eps': _L1_gnn_in['eps'], 'L1_gnn_We': _L1_gnn_in['We'], 'L1_gnn_be': _L1_gnn_in['be'], 'L1_gnn_W1': _L1_gnn_in['W1'], 'L1_gnn_b1': _L1_gnn_in['b1'], 'L1_gnn_gamma': _L1_gnn_in['gamma'], 'L1_gnn_beta': _L1_gnn_in['beta'], 'L1_gnn_W2': _L1_gnn_in['W2'], 'L1_gnn_b2': _L1_gnn_in['b2'], 'L1_ffn_w_up': _L1_ffn_in['w_up'], 'L1_ffn_w_down': _L1_ffn_in['w_down']}

def reference(x, src, dst, edge_type_2, edge_weight1, L0_gnn_basis1, L0_gnn_att1, L0_gnn_gate_w1, L0_gnn_root1, L0_gnn_bias1, L0_gnn_basis2, L0_gnn_att2, L0_gnn_gate_w2, L0_gnn_root2, L0_gnn_bias2, L0_ffn_gate_w, L0_ffn_w1, L0_ffn_b1, L0_ffn_w2, L0_ffn_b2, L0_ffn_sw1, L0_ffn_sb1, L0_ffn_sw2, L0_ffn_sb2, L1_gnn_eps, L1_gnn_We, L1_gnn_be, L1_gnn_W1, L1_gnn_b1, L1_gnn_gamma, L1_gnn_beta, L1_gnn_W2, L1_gnn_b2, L1_ffn_w_up, L1_ffn_w_down):
    import jax
    import jax.numpy as jnp

    def _L0_gnn_ref(x, edge_index, edge_type, basis1, att1, gate_w1, root1, bias1, basis2, att2, gate_w2, root2, bias2):
        import jax, jax.numpy as jnp
        import numpy as np
        NUM_RELATIONS = 2
        NUM_BASES = 30
        HIDDEN = 512
        N_NODES = 10000
        N_EDGES = 5000

        def rgcn_gate_layer(x, row, col, edge_type, basis, att, gate_w, root, bias):
            H = x.shape[1]
            w = jnp.einsum('rb,bio->rio', att, basis)
            x_j = x[col]
            msgs = []
            for r in range(NUM_RELATIONS):
                gate = jax.nn.sigmoid(x_j @ gate_w[r, :, 0])
                msgs.append(gate[:, None] * x_j @ w[r])
            msg = jnp.where((edge_type == 0)[:, None], msgs[0], msgs[1])
            agg = jax.ops.segment_sum(msg, row, num_segments=x.shape[0])
            return agg + x @ root + bias
        row, col = (edge_index[0], edge_index[1])
        h = jax.nn.relu(rgcn_gate_layer(x, row, col, edge_type, basis1, att1, gate_w1, root1, bias1))
        out = rgcn_gate_layer(h, row, col, edge_type, basis2, att2, gate_w2, root2, bias2)
        return out

    def _L0_ffn_ref(x, gate_w, w1, b1, w2, b2, sw1, sb1, sw2, sb2):
        import jax, jax.numpy as jnp
        import numpy as np
        D, H, E, B, S = (512, 64, 16, 8, 256)
        MAX_GROUP_SIZE = 128
        MIN_CAPACITY = 8
        CAPACITY_FACTOR = 1.0

        def _group_dims(num_tokens, num_experts):
            num_groups = -(-num_tokens // MAX_GROUP_SIZE)
            while num_tokens % num_groups != 0 or num_groups % num_experts != 0:
                num_groups += 1
            return (num_tokens // num_groups, num_groups)
        Bn, Sn, Dn = x.shape
        En = gate_w.shape[1]
        T = Bn * Sn
        group_size, num_groups = _group_dims(T, En)
        cap = max(int(round(CAPACITY_FACTOR * group_size * num_groups / En)), MIN_CAPACITY)
        xg = x.reshape(num_groups, group_size, Dn)
        logits = jnp.einsum('gsd,de->gse', xg, gate_w)
        probs = jax.nn.softmax(logits, axis=-1)
        flat_probs = probs.transpose(2, 0, 1).reshape(En, T)
        scores, tok_idx = jax.lax.top_k(flat_probs, cap)
        xf = x.reshape(T, Dn)
        toks = xf[tok_idx]
        h = jax.nn.gelu(jnp.einsum('ecd,edh->ech', toks, w1) + b1[:, None, :])
        y = jnp.einsum('ech,ehd->ecd', h, w2) + b2[:, None, :]
        y = y * scores[..., None]
        routed = jnp.zeros_like(xf).at[tok_idx.reshape(-1)].add(y.reshape(-1, Dn))
        shared = jax.nn.gelu(xf @ sw1 + sb1) @ sw2 + sb2
        out = (routed + shared).reshape(Bn, Sn, Dn)
        return out

    def _L1_gnn_ref(x, edge_index, edge_attr, eps, We, be, W1, b1, gamma, beta, W2, b2):
        import jax, jax.numpy as jnp
        import numpy as np
        N, D, E, L = (625, 512, 5000, 4)
        BN_EPS = 1e-05

        def _gine_layer(x, src, dst, edge_attr, eps, We, be, W1, b1, gamma, beta, W2, b2):
            e = edge_attr @ We + be
            m = jax.nn.relu(x[src] + e)
            agg = jax.ops.segment_sum(m, dst, num_segments=x.shape[0])
            h = ((1.0 + eps) * x + agg) @ W1 + b1
            mu = jnp.mean(h, axis=0)
            var = jnp.mean(jnp.square(h - mu), axis=0)
            h = (h - mu) * jax.lax.rsqrt(var + BN_EPS) * gamma + beta
            h = jax.nn.relu(h)
            return jax.nn.relu(h @ W2 + b2)
        src, dst = (edge_index[0], edge_index[1])
        for l in range(L):
            x = _gine_layer(x, src, dst, edge_attr, eps[l], We[l], be[l], W1[l], b1[l], gamma[l], beta[l], W2[l], b2[l])
        return x

    def _L1_ffn_ref(x, w_up, w_down):
        import jax, jax.numpy as jnp
        import numpy as np
        EPS = 1e-05

        def _bitlinear(x, w):
            w_scale = jnp.clip(jnp.mean(jnp.abs(w)), EPS, None)
            w_q = jnp.clip(jnp.round(w / w_scale), -1.0, 1.0) * w_scale
            w_eff = w + jax.lax.stop_gradient(w_q - w)
            x_scale = 127.0 / jnp.clip(jnp.max(jnp.abs(x), axis=-1, keepdims=True), EPS, None)
            x_q = jnp.clip(jnp.round(x * x_scale), -128.0, 127.0) / x_scale
            x_eff = x + jax.lax.stop_gradient(x_q - x)
            return jnp.einsum('bsi,oi->bso', x_eff, w_eff)

        def _ste_round_clamp_int8(h):
            h_q = jnp.clip(jnp.round(h), -128.0, 127.0)
            return h + jax.lax.stop_gradient(h_q - h)
        h = _bitlinear(x, w_up)
        h = jax.nn.relu(h)
        h = _ste_round_clamp_int8(h)
        return _bitlinear(h, w_down)
    edge_index = jnp.stack([src, dst])
    x = x + _L0_gnn_ref(_layernorm(x, axis=-1), edge_index, edge_type_2, L0_gnn_basis1, L0_gnn_att1, L0_gnn_gate_w1, L0_gnn_root1, L0_gnn_bias1, L0_gnn_basis2, L0_gnn_att2, L0_gnn_gate_w2, L0_gnn_root2, L0_gnn_bias2)
    x = x + _L0_ffn_ref(_layernorm(x, axis=-1)[None], L0_ffn_gate_w, L0_ffn_w1, L0_ffn_b1, L0_ffn_w2, L0_ffn_b2, L0_ffn_sw1, L0_ffn_sb1, L0_ffn_sw2, L0_ffn_sb2)[0]
    x = x + _L1_gnn_ref(_layernorm(x, axis=-1), edge_index, edge_weight1, L1_gnn_eps, L1_gnn_We, L1_gnn_be, L1_gnn_W1, L1_gnn_b1, L1_gnn_gamma, L1_gnn_beta, L1_gnn_W2, L1_gnn_b2)
    x = x + _L1_ffn_ref(_layernorm(x, axis=-1)[None], L1_ffn_w_up, L1_ffn_w_down)[0]
    return x

_drawn_inputs = setup_inputs


def setup_inputs(seed=0):
    import zlib

    import numpy as np

    out = dict(_drawn_inputs(seed))
    spreads = {'L0_ffn_b1': (0.0, 1.121),
     'L0_ffn_b2': (0.0, 0.1),
     'L0_ffn_sb1': (0.0, 0.1),
     'L0_ffn_sb2': (0.0, 0.1),
     'L1_gnn_eps': (0.0, 0.1),
     'L1_gnn_be': (0.0, 0.1),
     'L1_gnn_b1': (0.0, 2.0),
     'L1_gnn_gamma': (1.0, 0.2),
     'L1_gnn_beta': (0.0, 0.1),
     'L1_gnn_b2': (0.0, 0.1)}
    factors = {'L0_gnn_basis1': 22.44,
     'L0_gnn_att1': 21.812,
     'L0_gnn_gate_w1': 30.989,
     'L0_gnn_bias1': 14.627,
     'L0_gnn_basis2': 7.74,
     'L0_gnn_att2': 7.698,
     'L0_gnn_gate_w2': 58.807}
    for name, (base, spread) in spreads.items():
        noise = np.random.default_rng([zlib.crc32(name.encode()), seed]).standard_normal(out[name].shape)
        drawn = base * np.exp(spread * noise) if base else spread * noise
        out[name] = jnp.asarray(drawn.astype(out[name].dtype))
    for name, factor in factors.items():
        out[name] = (out[name] * factor).astype(out[name].dtype)
    return out
```

```python
import concourse.bass as bass
from concourse import mybir
from concourse.alu_op_type import AluOpType as ALU
from contextlib import ExitStack, contextmanager

F32, F32R, BF16 = mybir.dt.float32, mybir.dt.float32r, mybir.dt.bfloat16
I32, U32 = mybir.dt.int32, mybir.dt.uint32
ACT = mybir.ActivationFunctionType
AX = mybir.AxisListType

P = 128
N, D, E = 10000, 512, 5000
KC = D // P
RELATIONS, BASES = 2, 30
EXPERTS, HID = 16, 64
CAP = 625
LAYERS = 4
GROUP = 256
TILES = GROUP // P
NG = -(-N // GROUP)
REST = N - (NG - 1) * GROUP
ET = -(-E // P)
EP = ET * P
EPS = 1e-5
MAGIC = 1.5 * 2.0 ** 23
NO_ROW = float(1 << 20)


def wait(eng, sem, value):
    if not isinstance(value, int) or value > 0:
        eng.wait_ge(sem, value)


def pipeline(eng, stages, count=NG, short_last=True, ways=2):
    deepest = max(lag for lag, _ in stages)
    first = deepest + ways
    turns = (count - int(short_last) - first) // ways

    def peeled(r):
        for lag, step in stages:
            g = r - lag
            if 0 <= g < count:
                step(g, g // ways, g % ways, short_last and g == count - 1)

    for r in range(first):
        peeled(r)
    with eng.Fori(0, turns) as i:
        for u in range(ways):
            for lag, step in stages:
                b = first + u - lag
                step(i * ways + b, i + b // ways, b % ways, False)
    for r in range(first + ways * turns, count + deepest):
        peeled(r)


def wait_apart(eng, sem, value):
    wait(eng, sem, value)
    if not isinstance(value, int):
        eng.nop(nofuse=True)


def tiles_of(last):
    return [(0, REST)] if last else [(t, P) for t in range(TILES)]


def width_of(last):
    return REST if last else GROUP


def rows(dram, g, last):
    if last:
        return dram[g * GROUP:g * GROUP + REST, :].rearrange("(t p) d -> p t d", t=1)
    return dram[bass.ds(g * GROUP, GROUP), :].rearrange("(t p) d -> p t d", p=P)


def part(tile, last):
    return tile[0:REST, 0:1, :] if last else tile[:, :, :]


class Core:

    BANK, INDEXED = 48, 8

    def __init__(self, nc):
        self.nc = nc
        self.sems = [nc.alloc_semaphore(name=f"phase_sem{i}") for i in range(self.BANK)]
        self.indexed = [nc.alloc_semaphore(name=f"indexed_sem{i}") for i in range(self.INDEXED)]
        self.phases = 0

    @contextmanager
    def phase(self, name, sem_names):
        names = sem_names.split()
        own = [n for n in names if not n.startswith("sw")]
        indexed = [n for n in names if n.startswith("sw")]
        assert len(own) <= self.BANK and len(indexed) <= self.INDEXED and len(set(names)) == len(names), name
        sems = {**dict(zip(own, self.sems)), **dict(zip(indexed, self.indexed))}
        self.phases += 1
        name = f"{name}{self.phases}"
        with ExitStack() as memory:
            def sbuf(n, shape, dt=F32):
                return memory.enter_context(self.nc.sbuf_tensor(f"{name}_{n}", shape, dt))

            def psum(n, shape, dt=F32):
                return memory.enter_context(self.nc.psum_tensor(f"{name}_{n}", shape, dt))

            yield sems, sbuf, psum
            self.nc.all_engine_barrier()
            if indexed:
                nums = [sems[n].num for n in indexed]
                self.nc.gpsimd.dma_reset(range(min(nums), max(nums) + 1))
            for n in names:
                self.nc.gpsimd.sem_clear(sems[n])
            self.nc.all_engine_barrier()


def norm_phase(core, src, dst, half):
    nc = core.nc
    W = 4
    with core.phase("norm", "ld0 ld1 ld2 ld3 stats aggr var rstd norm st0 st1 st2 st3") as (s, sbuf, psum):
        x = [sbuf(f"x{q}", [P, TILES, D]) for q in range(W)]
        y = [sbuf(f"y{q}", [P, TILES, D]) for q in range(W)]
        bn = [sbuf(f"bn{q}", [P, TILES, 6]) for q in range(W)]
        mv = [sbuf(f"mv{q}", [P, TILES, 2]) for q in range(W)]
        rs = [sbuf(f"rs{q}", [P, TILES]) for q in range(W)]
        ld, st = [s[f"ld{q}"] for q in range(W)], [s[f"st{q}"] for q in range(W)]
        with nc.Block() as block:
            @block.sync
            def _(eng):
                def load(g, h, q, last):
                    wait(eng, s["norm"], g - W + 1)
                    eng.dma_start(part(x[q], last), rows(src, g, last)).then_inc(ld[q], 16)
                pipeline(eng, [(0, load)], ways=W)

            @block.vector
            def _(eng):
                def stats(g, h, q, last):
                    eng.wait_ge(ld[q], (h + 1) * 16)
                    row_stats(eng, s, g, x[q], bn[q], mv[q], last)

                def norm(g, h, q, last):
                    eng.wait_ge(s["rstd"], g + 1)
                    wait(eng, st[q], h * 16)
                    row_norm(eng, x[q], y[q], mv[q], rs[q], last).then_inc(s["norm"], 1)
                pipeline(eng, [(0, stats), (1, norm)], ways=W)

            @block.gpsimd
            def _(eng):
                pipeline(eng, [(0, lambda g, h, q, last: row_rstd(eng, s, g, mv[q], half, rs[q], last))], ways=W)

            @block.scalar
            def _(eng):
                def store(g, h, q, last):
                    eng.wait_ge(s["norm"], g + 1)
                    eng.dma_start(rows(dst, g, last), part(y[q], last)).then_inc(st[q], 16)
                pipeline(eng, [(0, store)], ways=W)
                for q in range(W):
                    eng.wait_ge(st[q], 16 * (NG // W))


def row_norm(eng, x, y, mv, rs, last):
    for t, n in tiles_of(last):
        done = eng.tensor_scalar(y[0:n, t, :], x[0:n, t, :], mv[0:n, t, 0:1], rs[0:n, t:t + 1],
                                 ALU.subtract, ALU.mult)
    return done


def row_stats(eng, s, g, x, bn, mv, last, negated=None):
    for t, n in tiles_of(last):
        done = eng.bn_stats(bn[0:n, t, :], x[0:n, t, :])
    done.then_inc(s["stats"], 1)
    wait_apart(eng, s["stats"], g + 1)
    for t, n in tiles_of(last):
        done = eng.bn_aggr(mv[0:n, t, :], bn[0:n, t, :])
    done.then_inc(s["aggr"], 1)
    eng.wait_ge(s["aggr"], g + 1)
    n = REST if last else P
    k = 1 if last else TILES
    if negated is not None:
        eng.tensor_scalar(negated[0:n, 0:k], mv[0:n, 0:k, 0], -1.0, None, ALU.mult)
    eng.tensor_scalar(mv[0:n, 0:k, 1], mv[0:n, 0:k, 1], EPS, None, ALU.add).then_inc(s["var"], 1)


def row_rstd(eng, s, g, mv, half, rs, last):
    eng.wait_ge(s["var"], g + 1)
    n = REST if last else P
    k = 1 if last else TILES
    eng.tensor_tensor(rs[0:n, 0:k], mv[0:n, 0:k, 1], half[0:n, 0:k], ALU.pow).then_inc(s["rstd"], 1)


HI = 80
KEYS = 2
PAD_NODE = N
ROWS = NG * GROUP


def ds1(i):
    return slice(i, i + 1) if isinstance(i, int) else bass.ds(i, 1)


class Edges:

    def __init__(self, nc):
        def sbuf(n, dt=F32):
            return [nc.alloc_sbuf_tensor(f"edge_{n}{k}", [P, ET], dt) for k in range(KEYS)]

        self.key, self.carried, self.kind, self.weight = sbuf("key"), sbuf("carried"), sbuf("kind"), sbuf("weight")
        self.partner, self.target = sbuf("partner", U32), sbuf("target", U32)
        self.table = [nc.dram_tensor(f"edge_table{k}", (EP, 4), F32).ap() for k in range(KEYS)]
        self.key_row = [nc.dram_tensor(f"edge_key_row{k}", (EP + P,), F32).ap() for k in range(KEYS)]
        self.weight_row = nc.dram_tensor("edge_weight_row", (EP,), F32).ap()
        self.sums = [nc.dram_tensor(f"edge_sums{k}", (ROWS, D), F32).ap() for k in range(KEYS)]


def order_phase(core, ed, cst, src, dst, kind, weight):
    nc = core.nc
    W = 4
    names = ("ints rows colf hilo shift keyrow hirow hot hist histc scan roll off base put "
             "count look bsb ohT val rank made zero zdone fin1 fin2 fin3 wide "
             "pk0 pk1 pk2 pk3 sw0 sw1 sw2 sw3 sw4 sw5 sw6 sw7")
    with core.phase("order", names) as (s, sbuf, psum):
        load_i = sbuf("load_i", [P, 5, ET], I32)
        col = sbuf("col", [P, 5, ET])
        hl_i = sbuf("hl_i", [P, KEYS, 2, ET], I32)
        hl = sbuf("hl", [P, KEYS, 2, ET])
        wt = sbuf("wt", [P, ET])
        packed = sbuf("packed", [P, KEYS, ET, 4])
        row_i = [sbuf(f"row_i{k}", [P, EP], I32) for k in range(KEYS)]
        key_row = [sbuf(f"key_row{k}", [P, EP]) for k in range(KEYS)]
        hi_row = [sbuf(f"hi_row{k}", [HI, EP]) for k in range(KEYS)]
        hot_hi = [sbuf(f"hot_hi{k}", [P, ET, HI], BF16) for k in range(KEYS)]
        hot_lo = [sbuf(f"hot_lo{k}", [P, ET, P], BF16) for k in range(KEYS)]
        cnt = sbuf("cnt", [HI, KEYS, P])
        incl = sbuf("incl", [HI, KEYS, P])
        ohT = [sbuf(f"ohT{q}", [HI, KEYS, P]) for q in range(2)]
        place = [sbuf(f"place{q}", [HI, KEYS, P]) for q in range(2)]
        junk = [sbuf(f"junk{q}", [P, KEYS, 2, P]) for q in range(2)]
        part_n = [sbuf(f"part_n{q}", [P, KEYS, 2]) for q in range(2)]
        rank = sbuf("rank", [P, KEYS, ET])
        rank_i = sbuf("rank_i", [P, KEYS, ET], I32)
        rr_i = sbuf("rr_i", [P, 2, KEYS, ET], I32)
        rr = sbuf("rr", [P, 2, KEYS, ET])
        slot = sbuf("slot", [P, KEYS, ET], U32)
        pk = [sbuf(f"pk{q}", [P, KEYS, 4]) for q in range(W)]
        ix = [sbuf(f"ix{q}", [P, KEYS], U32) for q in range(W)]
        zeros = sbuf("zeros", [P, 2, D])
        tab = sbuf("tab", [P, KEYS, ET, 4])
        lineT = sbuf("lineT", [ET, KEYS + 1, P])
        nextT = sbuf("nextT", [ET, KEYS, P])
        same = sbuf("same", [P, KEYS, ET])
        minus = sbuf("minus", [1, P])
        h_ps = psum("h_ps", [HI, KEYS, P])
        o_ps = psum("o_ps", [HI, KEYS])
        c_ps = [psum(f"c_ps{q}", [HI, KEYS, P]) for q in range(2)]
        l_ps = [psum(f"l_ps{q}", [P, KEYS, P]) for q in range(2)]
        t_ps = psum("t_ps", [P, 3, P])
        key_in = (src, dst)
        pk_s, sc_s = [s[f"pk{q}"] for q in range(W)], [[s[f"sw{q * KEYS + k}"] for k in range(KEYS)] for q in range(W)]
        USED = E // ET
        assert USED * ET == E

        with nc.Block() as block:
            @block.gpsimd
            def _(eng):
                eng.memset(load_i[:, 0:2, :], PAD_NODE)
                eng.memset(load_i[:, 2, :], RELATIONS)
                eng.memset(load_i[:, 3:5, :], 0)
                eng.memset(wt[:, :], 0.0)
                for k in range(KEYS):
                    eng.memset(row_i[k][:, E:EP], PAD_NODE)
                eng.memset(minus[:, :], -1.0)
                eng.memset(zeros[:, :, :], 0.0).then_inc(s["made"], 1)

                def scatter(t, h, q, last):
                    wait_apart(eng, pk_s[q], h + 1)
                    for k in range(KEYS):
                        eng.indirect_dma_start(ed.table[k], bass.IndirectOffsetOnAxis(ap=ix[q][:, k:k + 1], axis=0),
                                               pk[q][:, k, :], None).then_inc(sc_s[q][k], 16)
                pipeline(eng, [(0, scatter)], count=ET, short_last=False, ways=W)

            @block.sync
            def _(eng):
                eng.wait_ge(s["made"], 1)
                for j, a in enumerate((src, dst, kind, src, dst)):
                    eng.dma_start(load_i[0:USED, j, :], a.rearrange("(p t) -> p t", t=ET)).then_inc(s["ints"], 16)
                eng.dma_start(wt[0:USED, :], weight.rearrange("(p t) one -> p (t one)", t=ET)).then_inc(s["ints"], 16)
                for k in range(KEYS):
                    eng.dma_start(row_i[k][:, 0:E], key_in[k].partition_broadcast(P)).then_inc(s["rows"], 16)
                for k in range(KEYS):
                    eng.dma_start(ed.key_row[k].rearrange("(a n) -> a n", a=1)[:, EP:EP + P], minus[:, :]).then_inc(s["fin1"], 16)

                def clear(g, h, q, last):
                    for k in range(KEYS):
                        eng.dma_start(ed.sums[k][bass.ds(g * GROUP, GROUP), :].rearrange("(t p) d -> p t d", p=P),
                                      zeros[:, :, :]).then_inc(s["zdone"], 16)
                with eng.Fori(0, NG) as g:
                    clear(g, 0, 0, False)
                for q in range(W):
                    for k in range(KEYS):
                        eng.wait_ge(sc_s[q][k], 16 * (ET // W))
                for k in range(KEYS):
                    eng.dma_start(tab[:, k, :, :], ed.table[k].rearrange("(p t) c -> p t c", t=ET)).then_inc(s["fin2"], 16)
                eng.wait_ge(s["wide"], 1)
                for k in range(KEYS):
                    eng.dma_start(ed.key_row[k].rearrange("(t p) -> t p", p=P)[0:ET, :], lineT[:, k, :]).then_inc(s["fin1"], 16)
                eng.dma_start(ed.weight_row.rearrange("(t p) -> t p", p=P), lineT[:, KEYS, :]).then_inc(s["fin1"], 16)
                eng.wait_ge(s["fin1"], 16 * (2 * KEYS + 1))
                for k in range(KEYS):
                    eng.dma_start(nextT[:, k, :], ed.key_row[k][1:EP + 1].rearrange("(t p) -> t p", p=P)).then_inc(s["fin3"], 16)
                eng.wait_ge(s["zdone"], 16 * KEYS * NG)

            @block.vector
            def _(eng):
                eng.wait_ge(s["ints"], 96)
                eng.tensor_copy(col[:, :, :], load_i[:, :, :]).then_inc(s["colf"], 1)
                for k in range(KEYS):
                    eng.tensor_scalar(hl_i[:, k, 0, :], load_i[:, k, :], 7, None, ALU.logical_shift_right)
                    m = eng.tensor_scalar(hl_i[:, k, 1, :], load_i[:, k, :], P - 1, None, ALU.bitwise_and)
                m.then_inc(s["hilo"], 1)
                eng.wait_ge(s["hilo"], 1)
                eng.tensor_copy(hl[:, :, :, :], hl_i[:, :, :, :]).then_inc(s["hilo"], 1)
                eng.wait_ge(s["hilo"], 2)
                for k in range(KEYS):
                    for t0 in range(0, ET, ET // 2):
                        ts = slice(t0, t0 + ET // 2)
                        for hot, part_, w in ((hot_hi, 0, HI), (hot_lo, 1, P)):
                            m = eng.tensor_tensor(hot[k][:, ts, :], cst.iota[:, 0:w].unsqueeze(1).to_broadcast([P, ET // 2, w]),
                                                  hl[:, k, part_, ts].unsqueeze(2).to_broadcast([P, ET // 2, w]), ALU.is_equal)
                m.then_inc(s["hot"], 1)
                for k in range(KEYS):
                    for c, j in ((0, k), (1, 4 - k), (2, 2)):
                        eng.tensor_copy(packed[:, k, :, c], col[:, j, :])
                    eng.tensor_copy(packed[:, k, :, 3], wt[:, :])
                eng.wait_ge(s["rows"], 32)
                for k in range(KEYS):
                    eng.tensor_copy(key_row[k][:, :], row_i[k][:, :]).then_inc(s["keyrow"], 1)
                eng.wait_ge(s["keyrow"], 2)
                for k in range(KEYS):
                    eng.tensor_scalar(row_i[k][0:HI, :], row_i[k][0:HI, :], 7, None, ALU.logical_shift_right).then_inc(s["shift"], 1)
                    eng.wait_ge(s["shift"], k + 1)
                    eng.tensor_copy(hi_row[k][:, :], row_i[k][0:HI, :]).then_inc(s["hirow"], 1)
                eng.wait_ge(s["hist"], 1)
                eng.tensor_copy(cnt[:, :, :], h_ps[:, :, :]).then_inc(s["histc"], 1)
                eng.wait_ge(s["histc"], 1)
                for k in range(KEYS):
                    m = eng.tensor_tensor_scan(incl[:, k, :], cnt[:, k, :], cnt[:, k, :], 0.0, ALU.add, ALU.bypass)
                m.then_inc(s["scan"], 1)
                eng.wait_ge(s["scan"], 1)
                eng.wait_ge(s["off"], 1)
                eng.tensor_tensor(incl[:, :, :], incl[:, :, :], cnt[:, :, :], ALU.subtract).then_inc(s["base"], 1)
                eng.wait_ge(s["base"], 1)
                eng.tensor_tensor(place[0][:, :, :], incl[:, :, :], o_ps[:, :].unsqueeze(2).to_broadcast([HI, KEYS, P]),
                                  ALU.add).then_inc(s["put"], 1)
                eng.wait_ge(s["hirow"], 2)

                def columns(t, k):
                    return key_row[k].ap().rearrange("a (p t) -> a t p", t=ET)[:, ds1(t), :].rearrange("a one p -> a (one p)")

                def spread(t, h, q, last):
                    wait(eng, s["look"], t - 1)
                    for k in range(KEYS):
                        v = hi_row[k].ap().rearrange("a (p t) -> a t p", t=ET)[:, ds1(t), :].rearrange("a one p -> a (one p)")
                        m = eng.tensor_scalar(ohT[q][:, k, :], v, cst.index[0:HI, :], None, ALU.is_equal)
                    m.then_inc(s["ohT"], 1)

                def ranks(t, h, q, last):
                    eng.wait_ge(s["look"], t + 1)
                    for k in range(KEYS):
                        eng.scalar_tensor_tensor(junk[q][:, k, 0, :], l_ps[q][:, k, :], 1.0,
                                                 hot_lo[k].ap()[:, ds1(t), :].rearrange("a one p -> a (one p)"),
                                                 ALU.mult, ALU.mult, accum_out=part_n[q][:, k, 0:1])
                        m = eng.scalar_tensor_tensor(junk[q][:, k, 1, :], columns(t, k), col[:, k, ds1(t)], cst.before[:, :],
                                                     ALU.is_equal, ALU.mult, accum_out=part_n[q][:, k, 1:2])
                    m.then_inc(s["val"], 1)
                    eng.wait_ge(s["put"], t + 1)
                    eng.tensor_tensor(place[1 - q][:, :, :], place[q][:, :, :], c_ps[q][:, :, :], ALU.add).then_inc(s["put"], 1)
                    eng.wait_ge(s["val"], t + 1)
                    eng.tensor_tensor(rank[:, :, ds1(t)], part_n[q][:, :, 0:1], part_n[q][:, :, 1:2], ALU.add).then_inc(s["rank"], 1)
                pipeline(eng, [(0, spread), (1, ranks)], count=ET, short_last=False)
                eng.wait_ge(s["rank"], ET)
                eng.tensor_copy(rank_i[:, :, :], rank[:, :, :]).then_inc(s["rank"], 1)
                eng.wait_ge(s["rank"], ET + 1)
                eng.tensor_scalar(rr_i[:, 0, :, :], rank_i[:, :, :], 7, None, ALU.logical_shift_right)
                eng.tensor_scalar(rr_i[:, 1, :, :], rank_i[:, :, :], P - 1, None, ALU.bitwise_and).then_inc(s["rank"], 1)
                eng.wait_ge(s["rank"], ET + 2)
                eng.tensor_copy(rr[:, :, :, :], rr_i[:, :, :, :]).then_inc(s["rank"], 1)
                eng.wait_ge(s["rank"], ET + 3)
                eng.scalar_tensor_tensor(slot[:, :, :], rr[:, 1, :, :], float(ET), rr[:, 0, :, :], ALU.mult, ALU.add).then_inc(s["rank"], 1)
                eng.wait_ge(s["rank"], ET + 4)

                def pack(t, h, q, last):
                    for k in range(KEYS):
                        wait(eng, sc_s[q][k], h * 16)
                    eng.tensor_copy(pk[q][:, :, :], packed[:, :, ds1(t), :].rearrange("a k one c -> a (k one) c"))
                    eng.tensor_copy(ix[q][:, :], slot[:, :, ds1(t)].rearrange("a k one -> a (k one)")).then_inc(pk_s[q], 1)
                pipeline(eng, [(0, pack)], count=ET, short_last=False, ways=W)
                eng.wait_ge(s["fin2"], 32)
                for k in range(KEYS):
                    for c, dst_ in enumerate((ed.key[k], ed.partner[k], ed.kind[k], ed.weight[k])):
                        m = eng.tensor_copy(dst_[:, :], tab[:, k, :, c])
                m.then_inc(s["count"], 1)
                eng.wait_ge(s["count"], 2)
                eng.tensor_copy(lineT[:, :, :], t_ps[0:ET, :, :]).then_inc(s["wide"], 1)
                for k in range(KEYS):
                    eng.memset(ed.carried[k][:, 0:1], 0.0)
                    m = eng.tensor_scalar(ed.carried[k][:, 1:ET], ed.key[k][:, 0:ET - 1], 1.0, cst.last_row[:, :], ALU.add, ALU.mult)
                m.then_inc(s["roll"], 1)
                eng.wait_ge(s["roll"], 1)
                for k in range(KEYS):
                    eng.tensor_scalar(ed.carried[k][:, :], ed.carried[k][:, :], -1.0, None, ALU.add)
                eng.wait_ge(s["count"], 3)
                for k in range(KEYS):
                    m = eng.tensor_tensor(same[:, k, :], ed.key[k][:, :], t_ps[:, k, 0:ET], ALU.is_equal)
                m.then_inc(s["roll"], 1)
                eng.wait_ge(s["roll"], 2)
                for k in range(KEYS):
                    eng.scalar_tensor_tensor(ed.target[k][:, :], same[:, k, :], NO_ROW, ed.key[k][:, :], ALU.mult, ALU.add)

            @block.tensor
            def _(eng):
                eng.wait_ge(s["hot"], 1)
                for k in range(KEYS):
                    def hist(t, start, stop):
                        return eng.matmul(h_ps[:, k, :], hot_hi[k].ap()[:, ds1(t), :].rearrange("a one p -> a (one p)"),
                                          hot_lo[k].ap()[:, ds1(t), :].rearrange("a one p -> a (one p)"), start=start, stop=stop)
                    hist(0, True, False)
                    with eng.Fori(1, ET - 1) as t:
                        hist(t, False, False)
                    m = hist(ET - 1, False, True)
                m.then_inc(s["hist"], 1)
                eng.wait_ge(s["scan"], 1)
                for k in range(KEYS):
                    m = eng.matmul(o_ps[:, k:k + 1], cst.after[0:HI, 0:HI], incl[:, k, P - 1:P], start=True, stop=True)
                m.then_inc(s["off"], 1)

                def look(t, h, q, last):
                    wait(eng, s["put"], t)
                    wait(eng, s["val"], t - 1)
                    for k in range(KEYS):
                        eng.matmul(c_ps[q][:, k, :], hot_hi[k].ap()[:, ds1(t), :].rearrange("a one p -> a (one p)"),
                                   hot_lo[k].ap()[:, ds1(t), :].rearrange("a one p -> a (one p)"), start=True, stop=True)
                    eng.wait_ge(s["ohT"], t + 1)
                    eng.wait_ge(s["put"], t + 1)
                    for k in range(KEYS):
                        m = eng.matmul(l_ps[q][:, k, :], ohT[q][:, k, :], place[q][:, k, :], start=True, stop=True)
                    m.then_inc(s["look"], 1)
                pipeline(eng, [(0, look)], count=ET, short_last=False)
                eng.wait_ge(s["count"], 1)
                for k in range(KEYS):
                    eng.transpose(t_ps[0:ET, k, :], ed.key[k][:, :], cst.ident[:, :])
                eng.transpose(t_ps[0:ET, KEYS, :], ed.weight[1][:, :], cst.ident[:, :]).then_inc(s["count"], 1)
                eng.wait_ge(s["fin3"], 32)
                eng.wait_ge(s["wide"], 1)
                for k in range(KEYS):
                    m = eng.transpose(t_ps[:, k, 0:ET], nextT[:, k, :], cst.ident[0:ET, 0:ET])
                m.then_inc(s["count"], 1)


class Constants:

    def __init__(self, core, early):
        nc = core.nc

        def early_sbuf(n, shape, dt=F32):
            return early.enter_context(nc.sbuf_tensor(f"cst_{n}", shape, dt))

        def sbuf(n, shape, dt=F32):
            return nc.alloc_sbuf_tensor(f"cst_{n}", shape, dt)

        self.half = sbuf("half", [P, KC])
        self.ident = sbuf("ident", [P, P])
        self.ident_b = sbuf("ident_b", [P, P], BF16)
        self.last_row = sbuf("last_row", [P, 1])
        self.iota = early_sbuf("iota", [P, P])
        self.index = early_sbuf("index", [P, 1])
        self.before = early_sbuf("before", [P, P])
        self.after = early_sbuf("after", [P, P])
        with core.phase("const", "a b") as (s, _, _), nc.Block() as block:
            @block.gpsimd
            def _(eng):
                eng.memset(self.half[:, :], -0.5)
                eng.iota(self.iota[:, :], [[1, P]], base=0, channel_multiplier=0, allow_small_or_imprecise_dtypes=True)
                eng.iota(self.index[:, :], [[1, 1]], base=0, channel_multiplier=1, allow_small_or_imprecise_dtypes=True).then_inc(s["a"], 1)

            @block.vector
            def _(eng):
                eng.wait_ge(s["a"], 1)
                for m, op in ((self.before, ALU.is_lt), (self.after, ALU.is_gt), (self.ident, ALU.is_equal),
                              (self.ident_b, ALU.is_equal)):
                    eng.tensor_scalar(m[:, :], self.iota[:, :], self.index[:, :], None, op)
                eng.tensor_scalar(self.last_row[:, :], self.index[:, :], float(P - 1), None, ALU.is_equal)


def split_phase(core, name, items):
    nc = core.nc
    with core.phase(name, "load hi lo") as (s, sbuf, _):
        stage = [sbuf(f"stage{j}", list(hi.shape)) for j, (_, hi, _) in enumerate(items)]
        with nc.Block() as block:
            @block.sync
            def _(eng):
                for st, (value, _, _) in zip(stage, items):
                    eng.dma_start(st.ap(), value).then_inc(s["load"], 16)

            @block.scalar
            def _(eng):
                eng.wait_ge(s["load"], 16 * len(items))
                for st, (_, hi, _) in zip(stage, items):
                    eng.activation(hi, st.ap(), ACT.Copy).then_inc(s["hi"], 1)

            @block.vector
            def _(eng):
                for j, (st, (_, hi, lo)) in enumerate(zip(stage, items)):
                    eng.wait_ge(s["hi"], j + 1)
                    eng.tensor_tensor(lo, st.ap(), hi.bitcast(F32), ALU.subtract)


def chunked(w):
    return w.rearrange("(c p) n -> p c n", p=P)


def combine_phase(core, cst, basis, att, w_hi, w_lo):
    nc = core.nc
    W = 4
    TE = KC - 1
    with core.phase("combine", "att ld0 ld1 ld2 ld3 diag te ve hi lo") as (s, sbuf, psum):
        b_t = [sbuf(f"basis{q}", [P, KC, D]) for q in range(W)]
        att_t = sbuf("att", [P, RELATIONS * BASES])
        diag = [sbuf(f"diag{q}", [P, P]) for q in range(W)]
        acc = sbuf("acc", [P, KC + 1, D])
        rest = psum("rest", [P, TE, D])
        ld = [s[f"ld{q}"] for q in range(W)]
        with nc.Block() as block:
            @block.sync
            def _(eng):
                eng.dma_start(att_t[:, :], att.rearrange("r b -> (r b)").partition_broadcast(P)).then_inc(s["att"], 16)

                def load(b, h, q, last):
                    wait(eng, s["te"], b - W + 1)
                    wait(eng, s["ve"], b - W + 1)
                    eng.dma_start(b_t[q][:, :, :], chunked(basis[ds1(b), :, :].rearrange("one i o -> (one i) o"))).then_inc(ld[q], 16)
                pipeline(eng, [(0, load)], count=BASES, short_last=False, ways=W)

            @block.scalar
            def _(eng):
                eng.wait_ge(s["att"], 16)

                def diagonal(b, h, q, last):
                    wait(eng, s["te"], b - W + 1)
                    a = BASES + b
                    eng.activation(diag[q][:, :], cst.ident[:, :], ACT.Copy, scale=att_t[:, ds1(a)]).then_inc(s["diag"], 1)
                pipeline(eng, [(0, diagonal)], count=BASES, short_last=False, ways=W)
                eng.wait_ge(s["ve"], BASES)
                eng.activation(w_hi[:, 0:KC, :], acc[:, 0:KC, :], ACT.Copy)
                eng.activation(w_hi[:, 2 * KC - 1, :], acc[:, KC, :], ACT.Copy)
                eng.wait_ge(s["te"], BASES)
                eng.activation(w_hi[:, KC:KC + TE, :], rest[:, :, :], ACT.Copy).then_inc(s["hi"], 1)

            @block.vector
            def _(eng):
                eng.memset(acc[:, :, :], 0.0).then_inc(s["lo"], 1)
                eng.wait_ge(s["lo"], 1)
                eng.wait_ge(s["att"], 16)

                def add(b, h, q, last):
                    eng.wait_ge(ld[q], (h + 1) * 16)
                    wait(eng, s["ve"], b)
                    eng.scalar_tensor_tensor(acc[:, 0:KC, :], b_t[q][:, :, :], att_t[:, ds1(b)], acc[:, 0:KC, :], ALU.mult, ALU.add)
                    a = BASES + b
                    eng.scalar_tensor_tensor(acc[:, KC, :], b_t[q][:, TE, :], att_t[:, ds1(a)], acc[:, KC, :],
                                             ALU.mult, ALU.add).then_inc(s["ve"], 1)
                pipeline(eng, [(0, add)], count=BASES, short_last=False, ways=W)
                eng.wait_ge(s["hi"], 1)
                eng.tensor_tensor(w_lo[:, 0:KC, :], acc[:, 0:KC, :], w_hi[:, 0:KC, :].bitcast(F32), ALU.subtract)
                eng.tensor_tensor(w_lo[:, 2 * KC - 1, :], acc[:, KC, :], w_hi[:, 2 * KC - 1, :].bitcast(F32), ALU.subtract)
                eng.tensor_tensor(w_lo[:, KC:KC + TE, :], rest[:, :, :], w_hi[:, KC:KC + TE, :].bitcast(F32), ALU.subtract)

            @block.tensor
            def _(eng):
                def term(b, h, q, last):
                    eng.wait_ge(ld[q], (h + 1) * 16)
                    eng.wait_ge(s["diag"], b + 1)
                    for c in range(TE):
                        m = eng.matmul(rest[:, c, :], diag[q][:, :], b_t[q][:, c, :],
                                       start=isinstance(b, int) and b == 0, stop=isinstance(b, int) and b == BASES - 1)
                    m.then_inc(s["te"], 1)
                pipeline(eng, [(0, term)], count=BASES, short_last=False, ways=W)


def three(eng, out, a_hi, a_lo, b_hi, b_lo, start, stop):
    eng.matmul(out, a_hi, b_hi, start=start, stop=False)
    eng.matmul(out, a_lo, b_hi, start=False, stop=False)
    return eng.matmul(out, a_hi, b_lo, start=False, stop=stop)


def relation_phase(core, cst, ed, table, gate_w, w_hi, w_lo):
    nc = core.nc
    W = 4
    names = ("gw krow mask hk hix ends ix swg0 swg1 swg2 swg3 z sig copy lo coef ch sel A pth ptl B res tix hd H hres "
             "sws0 sws1 sws2 sws3")
    with core.phase("relation", names) as (s, sbuf, psum):
        gw = sbuf("gw", [P, RELATIONS, D])
        krow = sbuf("krow", [P, EP])
        mask = sbuf("mask", [P, RELATIONS, ET])
        ix = [sbuf(f"ix{q}", [P, 1], U32) for q in range(W)]
        tix = [sbuf(f"tix{q}", [P, 1], U32) for q in range(W)]
        x = [sbuf(f"x{q}", [P, D]) for q in range(W)]
        xh = [sbuf(f"xh{q}", [P, D], F32R) for q in range(W)]
        xl = [sbuf(f"xl{q}", [P, D], F32R) for q in range(W)]
        junk = [sbuf(f"junk{q}", [P, RELATIONS, D]) for q in range(W)]
        z = [sbuf(f"z{q}", [P, RELATIONS]) for q in range(W)]
        sig = [sbuf(f"sig{q}", [P, RELATIONS]) for q in range(W)]
        cf = [sbuf(f"cf{q}", [P, RELATIONS]) for q in range(W)]
        ch = [sbuf(f"ch{q}", [P, RELATIONS], F32R) for q in range(W)]
        cl = [sbuf(f"cl{q}", [P, RELATIONS]) for q in range(W)]
        sh = [sbuf(f"sh{q}", [P, RELATIONS, P], F32R) for q in range(W)]
        sl = [sbuf(f"sl{q}", [P, RELATIONS, P], F32R) for q in range(W)]
        hd = [sbuf(f"hd{q}", [P, ET]) for q in range(W)]
        ends = sbuf("ends", [P, ET])
        hkey = sbuf("hkey", [ET, 2])
        hsame = sbuf("hsame", [ET, 1])
        hix = sbuf("hix", [ET, 1], U32)
        hres = sbuf("hres", [ET, D])
        pth = [sbuf(f"pth{q}", [P, KC, RELATIONS, P], F32R) for q in range(2)]
        ptl = [sbuf(f"ptl{q}", [P, KC, RELATIONS, P], F32R) for q in range(2)]
        res = [sbuf(f"res{q}", [P, D]) for q in range(W)]
        A = [psum(f"A{q}", [P, KC, RELATIONS, P]) for q in range(2)]
        B = [psum(f"B{q}", [P, D]) for q in range(2)]
        H = psum("H", [ET, D])
        heads = krow.ap().rearrange("a (t p) -> a p t", p=P)[:, 0, :]
        ga, sc = [s[f"swg{q}"] for q in range(W)], [s[f"sws{q}"] for q in range(W)]

        def run(eng, *stages):
            pipeline(eng, stages, count=ET, short_last=False, ways=W)

        with nc.Block() as block:
            @block.sync
            def _(eng):
                eng.dma_start(krow[:, :], ed.key_row[0][0:EP].partition_broadcast(P)).then_inc(s["krow"], 16)
                eng.dma_start(gw[:, :, :], gate_w.rearrange("r i one -> (r i one)").partition_broadcast(P)
                              .rearrange("a (r i) -> a r i", r=RELATIONS)).then_inc(s["gw"], 16)
                for j in range(2):
                    eng.dma_start(hkey[:, j:j + 1], ed.key_row[0][j * P:j * P + EP].rearrange("(t p) -> t p", p=P)[:, 0:1],
                                  allow_slow_non_contiguous=True).then_inc(s["hk"], 16)

            @block.gpsimd
            def _(eng):
                def gather(t, h, q, last):
                    wait(eng, s["lo"], t - W + 1)
                    wait(eng, s["z"], t - W + 1)
                    wait_apart(eng, s["ix"], t + 1)
                    eng.indirect_dma_start(x[q][:, :], None, table, bass.IndirectOffsetOnAxis(ap=ix[q][:, :], axis=0)).then_inc(ga[q], 16)

                def scatter(t, h, q, last):
                    eng.wait_ge(s["tix"], t + 1)
                    wait_apart(eng, s["res"], t + 1)
                    eng.indirect_dma_start(ed.sums[0], bass.IndirectOffsetOnAxis(ap=tix[q][:, :], axis=0), res[q][:, :], None,
                                           bounds_check=ROWS - 1, oob_is_err=False).then_inc(sc[q], 16)
                run(eng, (0, gather), (4, scatter))
                for q in range(W):
                    eng.wait_ge(sc[q], 16 * (ET // W))
                eng.wait_ge(s["hres"], 1)
                eng.indirect_dma_start(ed.sums[0], bass.IndirectOffsetOnAxis(ap=hix[:, :], axis=0), hres[:, :], None,
                                       bounds_check=ROWS - 1, oob_is_err=False).then_inc(sc[0], 16)
                eng.wait_ge(sc[0], 16 * (ET // W) + 16)

            @block.vector
            def _(eng):
                for r in range(RELATIONS):
                    if r == 0:
                        m = eng.tensor_scalar(mask[:, 0, :], ed.kind[0][:, :], 0.0, None, ALU.is_equal)
                    else:
                        m = eng.tensor_scalar(mask[:, 1, :], ed.kind[0][:, :], 0.0, None, ALU.not_equal)
                m.then_inc(s["mask"], 1)
                eng.wait_ge(s["hk"], 32)
                eng.tensor_tensor(hsame[:, :], hkey[:, 0:1], hkey[:, 1:2], ALU.is_equal).then_inc(s["hix"], 1)
                eng.wait_ge(s["hix"], 1)
                eng.scalar_tensor_tensor(hix[:, :], hsame[:, :], NO_ROW, hkey[:, 0:1], ALU.mult, ALU.add).then_inc(s["hix"], 1)
                eng.tensor_scalar(ends[:, :], ed.target[0][:, :], NO_ROW, cst.last_row[:, :], ALU.is_lt, ALU.max).then_inc(s["ends"], 1)

                def index(t, h, q, last):
                    wait(eng, ga[q], h * 16)
                    eng.tensor_copy(ix[q][:, :], ed.partner[0][:, ds1(t)]).then_inc(s["ix"], 1)

                def gates(t, h, q, last):
                    eng.wait_ge(ga[q], (h + 1) * 16)
                    wait(eng, s["sig"], t - W + 1)
                    for r in range(RELATIONS):
                        m = eng.scalar_tensor_tensor(junk[q][:, r, :], x[q][:, :], 1.0, gw[:, r, :], ALU.mult, ALU.mult,
                                                     accum_out=z[q][:, r:r + 1])
                    m.then_inc(s["z"], 1)
                    eng.wait_ge(s["copy"], t + 1)
                    wait(eng, s["A"], t - W + 1)
                    eng.tensor_tensor(xl[q][:, :], x[q][:, :], xh[q][:, :].bitcast(F32), ALU.subtract).then_inc(s["lo"], 1)

                def select(t, h, q, last):
                    eng.wait_ge(s["sig"], t + 1)
                    eng.tensor_tensor(cf[q][:, :], sig[q][:, :], mask[:, :, ds1(t)].rearrange("a r one -> a (r one)"),
                                      ALU.mult).then_inc(s["coef"], 1)
                    wait(eng, s["H"], t - W + 1)
                    eng.tensor_scalar(hd[q][:, :], heads, ed.key[0][:, ds1(t)], ends[:, ds1(t)], ALU.is_equal, ALU.mult).then_inc(s["hd"], 1)
                    wait(eng, sc[q], h * 16)
                    eng.tensor_copy(tix[q][:, :], ed.target[0][:, ds1(t)]).then_inc(s["tix"], 1)
                    eng.wait_ge(s["coef"], t + 1)
                    eng.tensor_copy(ch[q][:, :], cf[q][:, :]).then_inc(s["ch"], 1)
                    eng.wait_ge(s["ch"], t * 2 + 1)
                    eng.tensor_tensor(cl[q][:, :], cf[q][:, :], ch[q][:, :].bitcast(F32), ALU.subtract).then_inc(s["ch"], 1)
                    eng.wait_ge(s["ch"], t * 2 + 2)
                    for r in range(RELATIONS):
                        eng.tensor_scalar(sh[q][:, r, :], krow[:, bass.ts(t, P)], ed.key[0][:, ds1(t)],
                                          ch[q][:, r:r + 1].bitcast(F32), ALU.is_equal, ALU.mult)
                        m = eng.tensor_scalar(sl[q][:, r, :], krow[:, bass.ts(t, P)], ed.key[0][:, ds1(t)],
                                              cl[q][:, r:r + 1], ALU.is_equal, ALU.mult)
                    m.then_inc(s["sel"], 1)

                def low(t, h, q, last):
                    eng.wait_ge(s["pth"], t + 1)
                    eng.tensor_tensor(ptl[q % 2][:, :, :, :], A[q % 2][:, :, :, :], pth[q % 2][:, :, :, :].bitcast(F32),
                                      ALU.subtract).then_inc(s["ptl"], 1)
                eng.wait_ge(s["krow"], 16)
                eng.wait_ge(s["gw"], 16)
                eng.wait_ge(s["mask"], 1)
                eng.wait_ge(s["ends"], 1)
                run(eng, (0, index), (1, gates), (2, select), (3, low))
                eng.wait_ge(s["H"], ET)
                eng.wait_ge(s["hix"], 2)
                eng.tensor_copy(hres[:, :], H[:, :]).then_inc(s["hres"], 1)

            @block.scalar
            def _(eng):
                def copy(t, h, q, last):
                    eng.wait_ge(ga[q], (h + 1) * 16)
                    wait(eng, s["A"], t - W + 1)
                    eng.activation(xh[q][:, :], x[q][:, :], ACT.Copy).then_inc(s["copy"], 1)
                    eng.wait_ge(s["z"], t + 1)
                    wait(eng, s["coef"], t - W + 1)
                    eng.activation(sig[q][:, :], z[q][:, :], ACT.Sigmoid).then_inc(s["sig"], 1)

                def high(t, h, q, last):
                    eng.wait_ge(s["A"], t + 1)
                    wait(eng, s["B"], t - 1)
                    eng.activation(pth[q % 2][:, :, :, :], A[q % 2][:, :, :, :], ACT.Copy).then_inc(s["pth"], 1)

                def result(t, h, q, last):
                    eng.wait_ge(s["B"], t + 1)
                    wait(eng, sc[q], h * 16)
                    wait(eng, s["H"], t - W + 1)
                    eng.activation(res[q][:, :], B[q % 2][:, :], ACT.Copy).then_inc(s["res"], 1)
                run(eng, (1, copy), (3, high), (4, result))

            @block.tensor
            def _(eng):
                def sums(t, h, q, last):
                    eng.wait_ge(s["lo"], t + 1)
                    eng.wait_ge(s["sel"], t + 1)
                    wait(eng, s["ptl"], t - 1)
                    for c in range(KC):
                        cs = slice(c * P, (c + 1) * P)
                        m = three(eng, A[q % 2][:, c, :, :], xh[q][:, cs], xl[q][:, cs], sh[q][:, :, :], sl[q][:, :, :], True, True)
                    m.then_inc(s["A"], 1)

                def product(t, h, q, last):
                    eng.wait_ge(s["ptl"], t + 1)
                    wait(eng, s["res"], t - 1)
                    for r in range(RELATIONS):
                        for c in range(KC):
                            m = three(eng, B[q % 2][:, :], pth[q % 2][:, c, r, :], ptl[q % 2][:, c, r, :], w_hi[:, r * KC + c, :],
                                      w_lo[:, r * KC + c, :], r == 0 and c == 0, r == RELATIONS - 1 and c == KC - 1)
                    m.then_inc(s["B"], 1)

                def head(t, h, q, last):
                    eng.wait_ge(s["res"], t + 1)
                    eng.wait_ge(s["hd"], t + 1)
                    eng.matmul(H[:, :], hd[q][:, :], res[q][:, :], start=isinstance(t, int) and t == 0,
                               stop=isinstance(t, int) and t == ET - 1).then_inc(s["H"], 1)
                run(eng, (2, sums), (3, product), (4, head))


def root_phase(core, cst, ed, rows_in, root, bias, half, rows_out, skip=None, normed=None):
    nc = core.nc
    fin = skip is not None
    root_hi, root_lo = root
    names = ("bias ld0 ld1 la0 la1 lx0 lx1 T hi lo M pa pb pc y r st0 st1 sn0 sn1 stats aggr var rstd norm")
    with core.phase("root", names) as (s, sbuf, psum):
        bt = sbuf("bias", [P, D])
        xin = [sbuf(f"xin{q}", [P, TILES, D]) for q in range(2)]
        agg = [sbuf(f"agg{q}", [P, TILES, D]) for q in range(2)]
        skp = [sbuf(f"skp{q}", [P, TILES, D]) for q in range(2)] if fin else None
        xh = [sbuf(f"xh{q}", [P, KC, GROUP], F32R) for q in range(2)]
        xl = [sbuf(f"xl{q}", [P, KC, GROUP], F32R) for q in range(2)]
        y = [sbuf(f"y{q}", [P, TILES, D]) for q in range(2)]
        nrm = [sbuf(f"nrm{q}", [P, TILES, D]) for q in range(2)] if fin else None
        bn = [sbuf(f"bn{q}", [P, TILES, 6]) for q in range(2)]
        mv = [sbuf(f"mv{q}", [P, TILES, 2]) for q in range(2)]
        rs = [sbuf(f"rs{q}", [P, TILES]) for q in range(2)]
        T = [psum(f"T{q}", [P, KC, GROUP]) for q in range(2)]
        O = [psum(f"O{q}", [P, TILES, D]) for q in range(2)]
        ld, la, lx = (s["ld0"], s["ld1"]), (s["la0"], s["la1"]), (s["lx0"], s["lx1"])
        st, sn = (s["st0"], s["st1"]), (s["sn0"], s["sn1"])
        with nc.Block() as block:
            @block.sync
            def _(eng):
                eng.dma_start(bt[:, :], bias.partition_broadcast(P)).then_inc(s["bias"], 16)

                def load(g, h, q, last):
                    wait(eng, s["T"], g - 1)
                    eng.dma_start(part(xin[q], last), rows(rows_in, g, last)).then_inc(ld[q], 16)
                    wait(eng, s["y"], g - 1)
                    eng.dma_start(part(agg[q], last), rows(ed.sums[0], g, last)).then_inc(la[q], 16)
                    if fin:
                        eng.dma_start(part(skp[q], last), rows(skip, g, last)).then_inc(lx[q], 16)
                pipeline(eng, [(0, load)])

            @block.tensor
            def _(eng):
                root_T = lambda g, h, q, last: turn(eng, s, g, h, q, last, ld, xin, T, cst.ident)

                def product(g, h, q, last):
                    eng.wait_ge(s["lo"], g + 1)
                    wait(eng, s["y"], g - 1)
                    for t, n in tiles_of(last):
                        ts = slice(t * P, t * P + n)
                        for c in range(KC):
                            m = three(eng, O[q][0:n, t, :], xh[q][:, c, ts], xl[q][:, c, ts], root_hi[:, c, :], root_lo[:, c, :],
                                      c == 0, c == KC - 1)
                    m.then_inc(s["M"], 1)
                pipeline(eng, [(0, root_T), (1, product)])

            @block.gpsimd
            def _(eng):
                def add_bias(g, h, q, last):
                    n = REST if last else P
                    eng.wait_ge(la[q], (h + 1) * 16)
                    k = 1 if last else TILES
                    eng.tensor_tensor(agg[q][0:n, 0:k, :], agg[q][0:n, 0:k, :], bt[0:n, :].unsqueeze(1).to_broadcast([n, k, D]),
                                      ALU.add).then_inc(s["pa"], 1)
                    if fin:
                        eng.wait_ge(lx[q], (h + 1) * 16)
                        eng.wait_ge(s["pa"], g + 1)
                        eng.tensor_tensor(agg[q][0:n, 0:k, :], agg[q][0:n, 0:k, :], skp[q][0:n, 0:k, :], ALU.add).then_inc(s["pb"], 1)
                eng.wait_ge(s["bias"], 16)
                stages = [(0, add_bias)]
                if fin:
                    stages.append((2, lambda g, h, q, last: row_rstd(eng, s, g, mv[q], half, rs[q], last)))
                pipeline(eng, stages)

            @block.scalar
            def _(eng):
                def high(g, h, q, last):
                    split_hi(eng, s, g, q, last, T, xh)

                def finish(g, h, q, last):
                    eng.wait_ge(s["y"], g + 1)
                    if not fin:
                        eng.activation(part(y[q], last), part(y[q], last), ACT.Relu).then_inc(s["r"], 1)
                        eng.wait_ge(s["r"], g + 1)
                    eng.dma_start(rows(rows_out, g, last), part(y[q], last)).then_inc(st[q], 16)
                    if fin:
                        eng.wait_ge(s["norm"], g + 1)
                        eng.dma_start(rows(normed, g, last), part(nrm[q], last)).then_inc(sn[q], 16)
                pipeline(eng, [(0, high), (2, finish)])
                for q in range(2):
                    eng.wait_ge(st[q], 16 * (NG // 2))
                    if fin:
                        eng.wait_ge(sn[q], 16 * (NG // 2))

            @block.vector
            def _(eng):
                def low(g, h, q, last):
                    split_lo(eng, s, g, q, last, T, xh, xl)

                def total(g, h, q, last):
                    eng.wait_ge(s["M"], g + 1)
                    eng.wait_ge(s["pb" if fin else "pa"], g + 1)
                    wait(eng, st[q], h * 16)
                    if fin:
                        wait(eng, s["norm"], g - 1)
                    eng.tensor_tensor(part(y[q], last), part(O[q], last), part(agg[q], last), ALU.add).then_inc(s["y"], 1)
                    if fin:
                        eng.wait_ge(s["y"], g + 1)
                        row_stats(eng, s, g, y[q], bn[q], mv[q], last)

                def norm(g, h, q, last):
                    eng.wait_ge(s["rstd"], g + 1)
                    wait(eng, sn[q], h * 16)
                    row_norm(eng, y[q], nrm[q], mv[q], rs[q], last).then_inc(s["norm"], 1)
                pipeline(eng, [(0, low), (1, total)] + ([(2, norm)] if fin else []))


def turn(eng, s, g, h, q, last, ready, x, T, ident, value=None):
    if ready is None:
        eng.wait_ge(s["pre"], g + 1)
    else:
        eng.wait_ge(ready[q], (h + 1) * 16)
    wait(eng, s["lo"], g - 1)
    for t, n in tiles_of(last):
        for c in range(KC):
            m = eng.transpose(T[q][:, c, t * P:t * P + n], x[q][0:n, t, c * P:(c + 1) * P], ident[0:n, 0:n])
    m.then_inc(s["T"], 1)


def split_hi(eng, s, g, q, last, T, xh):
    w = width_of(last)
    eng.wait_ge(s["T"], g + 1)
    wait(eng, s["M"], g - 1)
    eng.activation(xh[q][:, :, 0:w], T[q][:, :, 0:w], ACT.Copy).then_inc(s["hi"], 1)


def split_lo(eng, s, g, q, last, T, xh, xl):
    w = width_of(last)
    eng.wait_ge(s["hi"], g + 1)
    eng.tensor_tensor(xl[q][:, :, 0:w], T[q][:, :, 0:w], xh[q][:, :, 0:w].bitcast(F32), ALU.subtract).then_inc(s["lo"], 1)


SUB = P // EXPERTS
LINE = N // SUB
BITS = 30


def route_phase(core, cst, rows_in, gate_w, probs):
    nc = core.nc
    names = "gw gwh gwl ld0 ld1 T hi lo M mx sub exp sum rec pr pt ptc st"
    with core.phase("route", names) as (s, sbuf, psum):
        gw = sbuf("gw", [P, KC, EXPERTS])
        gh = sbuf("gh", [P, KC, EXPERTS], F32R)
        gl = sbuf("gl", [P, KC, EXPERTS], F32R)
        xin = [sbuf(f"xin{q}", [P, TILES, D]) for q in range(2)]
        xh = [sbuf(f"xh{q}", [P, KC, GROUP], F32R) for q in range(2)]
        xl = [sbuf(f"xl{q}", [P, KC, GROUP], F32R) for q in range(2)]
        mx = [sbuf(f"mx{q}", [P, TILES]) for q in range(2)]
        sm = [sbuf(f"sm{q}", [P, TILES]) for q in range(2)]
        rc = [sbuf(f"rc{q}", [P, TILES]) for q in range(2)]
        lg = [sbuf(f"lg{q}", [P, TILES, EXPERTS]) for q in range(2)]
        ex = [sbuf(f"ex{q}", [P, TILES, EXPERTS]) for q in range(2)]
        pr = [sbuf(f"pr{q}", [P, TILES, EXPERTS]) for q in range(2)]
        pT = sbuf("pT", [EXPERTS, NG * GROUP])
        T = [psum(f"T{q}", [P, KC, GROUP]) for q in range(2)]
        L = [psum(f"L{q}", [P, TILES, EXPERTS]) for q in range(2)]
        Q = [psum(f"Q{q}", [EXPERTS, GROUP]) for q in range(2)]
        ld = (s["ld0"], s["ld1"])
        with nc.Block() as block:
            @block.sync
            def _(eng):
                eng.dma_start(gw[:, :, :], chunked(gate_w)).then_inc(s["gw"], 16)

                def load(g, h, q, last):
                    wait(eng, s["T"], g - 1)
                    eng.dma_start(part(xin[q], last), rows(rows_in, g, last)).then_inc(ld[q], 16)
                pipeline(eng, [(0, load)])
                eng.wait_ge(s["ptc"], NG)
                eng.dma_start(probs, pT[:, 0:N]).then_inc(s["st"], 16)
                eng.wait_ge(s["st"], 16)

            @block.tensor
            def _(eng):
                def product(g, h, q, last):
                    eng.wait_ge(s["lo"], g + 1)
                    wait(eng, s["sub"], g - 1)
                    for t, n in tiles_of(last):
                        ts = slice(t * P, t * P + n)
                        for c in range(KC):
                            m = three(eng, L[q][0:n, t, :], xh[q][:, c, ts], xl[q][:, c, ts], gh[:, c, :], gl[:, c, :],
                                      c == 0, c == KC - 1)
                    m.then_inc(s["M"], 1)

                def turn_probs(g, h, q, last):
                    eng.wait_ge(s["pr"], g + 1)
                    wait(eng, s["ptc"], g - 1)
                    for t, n in tiles_of(last):
                        m = eng.transpose(Q[q][:, t * P:t * P + n], pr[q][0:n, t, :], cst.ident[0:n, 0:n])
                    m.then_inc(s["pt"], 1)
                eng.wait_ge(s["gwl"], 1)
                pipeline(eng, [(0, lambda g, h, q, last: turn(eng, s, g, h, q, last, ld, xin, T, cst.ident)),
                               (1, product), (3, turn_probs)])

            @block.scalar
            def _(eng):
                eng.wait_ge(s["gw"], 16)
                eng.activation(gh[:, :, :], gw[:, :, :], ACT.Copy).then_inc(s["gwh"], 1)

                def exps(g, h, q, last):
                    n, k = (REST, 1) if last else (P, TILES)
                    eng.wait_ge(s["sub"], g + 1)
                    wait(eng, s["pr"], g - 1)
                    eng.activation(ex[q][0:n, 0:k, :], lg[q][0:n, 0:k, :], ACT.Exp).then_inc(s["exp"], 1)

                def out(g, h, q, last):
                    wait_apart(eng, s["pt"], g + 1)
                    w = width_of(last)
                    at = slice(g * GROUP, g * GROUP + w) if isinstance(g, int) else bass.ds(g * GROUP, w)
                    eng.activation(pT[:, at], Q[q][:, 0:w], ACT.Copy).then_inc(s["ptc"], 1)
                pipeline(eng, [(0, lambda g, h, q, last: split_hi(eng, s, g, q, last, T, xh)), (1, exps), (3, out)])

            @block.vector
            def _(eng):
                eng.wait_ge(s["gwh"], 1)
                eng.tensor_tensor(gl[:, :, :], gw[:, :, :], gh[:, :, :].bitcast(F32), ALU.subtract).then_inc(s["gwl"], 1)

                def shift(g, h, q, last):
                    n, k = (REST, 1) if last else (P, TILES)
                    eng.wait_ge(s["M"], g + 1)
                    eng.tensor_reduce(mx[q][0:n, 0:k], L[q][0:n, 0:k, :], AX.X, ALU.max).then_inc(s["mx"], 1)
                    eng.wait_ge(s["mx"], g + 1)
                    wait(eng, s["exp"], g - 1)
                    eng.tensor_tensor(lg[q][0:n, 0:k, :], L[q][0:n, 0:k, :], mx[q][0:n, 0:k].unsqueeze(2).to_broadcast([n, k, EXPERTS]),
                                      ALU.subtract).then_inc(s["sub"], 1)

                def divide(g, h, q, last):
                    n, k = (REST, 1) if last else (P, TILES)
                    eng.wait_ge(s["exp"], g + 1)
                    eng.tensor_reduce(sm[q][0:n, 0:k], ex[q][0:n, 0:k, :], AX.X, ALU.add).then_inc(s["sum"], 1)
                    eng.wait_ge(s["sum"], g + 1)
                    eng.reciprocal(rc[q][0:n, 0:k], sm[q][0:n, 0:k]).then_inc(s["rec"], 1)
                    eng.wait_ge(s["rec"], g + 1)
                    wait(eng, s["pt"], g - 1)
                    eng.tensor_tensor(pr[q][0:n, 0:k, :], ex[q][0:n, 0:k, :], rc[q][0:n, 0:k].unsqueeze(2).to_broadcast([n, k, EXPERTS]),
                                      ALU.mult).then_inc(s["pr"], 1)
                pipeline(eng, [(0, lambda g, h, q, last: split_lo(eng, s, g, q, last, T, xh, xl)), (1, shift), (2, divide)])


def select_phase(core, cst, probs, chosen):
    nc = core.nc
    names = "ld blk ibit cand cnt tot keep th gt eq sc tg off need okr pick out st one"
    with core.phase("select", names) as (s, sbuf, psum):
        p = sbuf("p", [P, LINE])
        same = sbuf("same", [P, P])
        prior = sbuf("prior", [P, P])
        grp = sbuf("grp", [P, P])
        grp_i = sbuf("grp_i", [P, P], I32)
        own_i = sbuf("own_i", [P, 1], I32)
        own = sbuf("own", [P, 1])
        thr = [sbuf(f"thr{q}", [P, 1], I32) for q in range(2)]
        cand = [sbuf(f"cand{q}", [P, 1], I32) for q in range(2)]
        cnt = [sbuf(f"cnt{q}", [P, 1]) for q in range(2)]
        junk = [sbuf(f"junk{q}", [P, LINE]) for q in range(2)]
        gt = sbuf("gt", [P, LINE])
        eq = sbuf("eq", [P, LINE])
        scan = sbuf("scan", [P, LINE])
        need = sbuf("need", [P, 2])
        two = sbuf("two", [P, 2])
        tot = [psum(f"tot{q}", [P, 1]) for q in range(2)]
        off = psum("off", [P, 2])
        sums = psum("sums", [P, 1])
        with nc.Block() as block:
            @block.sync
            def _(eng):
                eng.dma_start(p[:, :], probs.rearrange("e (k n) -> (e k) n", k=SUB)).then_inc(s["ld"], 16)
                eng.wait_ge(s["out"], 1)
                eng.dma_start(chosen.rearrange("e (k n) -> (e k) n", k=SUB), gt[:, :]).then_inc(s["st"], 16)
                eng.wait_ge(s["st"], 16)

            @block.gpsimd
            def _(eng):
                eng.iota(grp_i[:, :], [[1, P]], base=0, channel_multiplier=0)
                eng.iota(own_i[:, :], [[1, 1]], base=0, channel_multiplier=1).then_inc(s["ibit"], 1)

            @block.tensor
            def _(eng):
                eng.wait_ge(s["blk"], 1)
                for b in range(BITS):
                    q = b % 2
                    eng.wait_ge(s["cnt"], b + 1)
                    eng.matmul(tot[q][:, :], same[:, :], cnt[q][:, :], start=True, stop=True).then_inc(s["tot"], 1)
                eng.wait_ge(s["tg"], 1)
                eng.matmul(sums[:, :], same[:, :], two[:, 0:1], start=True, stop=True)
                eng.matmul(off[:, 0:1], prior[:, :], two[:, 1:2], start=True, stop=True).then_inc(s["off"], 1)

            @block.vector
            def _(eng):
                eng.wait_ge(s["ibit"], 1)
                eng.tensor_scalar(grp_i[:, :], grp_i[:, :], 3, None, ALU.logical_shift_right)
                eng.tensor_scalar(own_i[:, :], own_i[:, :], 3, None, ALU.logical_shift_right)
                eng.memset(thr[0][:, :], 0).then_inc(s["one"], 1)
                eng.wait_ge(s["one"], 1)
                eng.tensor_copy(grp[:, :], grp_i[:, :])
                eng.tensor_copy(own[:, :], own_i[:, :]).then_inc(s["one"], 1)
                eng.wait_ge(s["one"], 2)
                eng.tensor_scalar(same[:, :], grp[:, :], own[:, :], None, ALU.is_equal).then_inc(s["one"], 1)
                eng.wait_ge(s["one"], 3)
                eng.tensor_tensor(prior[:, :], same[:, :], cst.after[:, :], ALU.mult).then_inc(s["blk"], 1)
                eng.wait_ge(s["ld"], 16)
                assert 1 << SUB.bit_length() - 1 == SUB == 8
                for b in range(BITS):
                    q = b % 2
                    wait(eng, s["th"], b)
                    eng.tensor_scalar(cand[q][:, :], thr[q][:, :], 1 << (BITS - 1 - b), None, ALU.bitwise_or).then_inc(s["cand"], 1)
                    eng.wait_ge(s["cand"], b + 1)
                    eng.tensor_scalar(junk[q][:, :], p[:, :], cand[q][:, :].bitcast(F32), 0.0, ALU.is_ge, ALU.add,
                                      accum_out=cnt[q][:, :]).then_inc(s["cnt"], 1)
                    eng.wait_ge(s["tot"], b + 1)
                    eng.scalar_tensor_tensor(two[:, 0:1], tot[q][:, :], float(CAP), cand[q][:, :].bitcast(F32),
                                             ALU.is_ge, ALU.mult).then_inc(s["keep"], 1)
                    eng.wait_ge(s["keep"], b + 1)
                    eng.tensor_tensor(thr[1 - q][:, :].bitcast(F32), two[:, 0:1], thr[q][:, :].bitcast(F32), ALU.max).then_inc(s["th"], 1)
                border = thr[BITS % 2][:, :].bitcast(F32)
                eng.wait_ge(s["th"], BITS)
                eng.tensor_scalar(gt[:, :], p[:, :], border, 0.0, ALU.is_gt, ALU.add, accum_out=two[:, 0:1])
                eng.tensor_scalar(eq[:, :], p[:, :], border, None, ALU.is_equal).then_inc(s["gt"], 1)
                eng.wait_ge(s["gt"], 1)
                eng.tensor_tensor_scan(scan[:, :], eq[:, :], eq[:, :], 0.0, ALU.add, ALU.bypass).then_inc(s["sc"], 1)
                eng.wait_ge(s["sc"], 1)
                eng.tensor_copy(two[:, 1:2], scan[:, LINE - 1:LINE]).then_inc(s["tg"], 1)
                eng.wait_ge(s["off"], 1)
                eng.tensor_scalar(need[:, 0:1], sums[:, :], -1.0, float(CAP), ALU.mult, ALU.add).then_inc(s["need"], 1)
                eng.wait_ge(s["need"], 1)
                eng.tensor_tensor(need[:, 1:2], need[:, 0:1], off[:, 0:1], ALU.subtract).then_inc(s["need"], 1)
                eng.wait_ge(s["need"], 2)
                eng.scalar_tensor_tensor(eq[:, :], scan[:, :], need[:, 1:2], eq[:, :], ALU.is_le, ALU.mult).then_inc(s["okr"], 1)
                eng.wait_ge(s["okr"], 1)
                eng.tensor_tensor(gt[:, :], gt[:, :], eq[:, :], ALU.add).then_inc(s["pick"], 1)
                eng.wait_ge(s["pick"], 1)
                eng.tensor_tensor(gt[:, :], gt[:, :], p[:, :], ALU.mult).then_inc(s["out"], 1)


def experts_phase(core, cst, rows_in, residual, chosen, w, half, rows_out, normed):
    nc = core.nc
    MC = EXPERTS * HID // P
    (w1h, w1l), (w2h, w2l), (s1h, s1l), (s2h, s2l), (b2h, b2l), b1, sb1, sb2 = w
    names = ("ld0 ld1 lr0 lr1 lc0 lc1 bias T hi lo sel ch cl cw hm act gate gh gl M pa y stats aggr var rstd "
             "norm st0 st1 sn0 sn1 self cn")
    with core.phase("experts", names) as (s, sbuf, psum):
        xin = [sbuf(f"xin{q}", [P, TILES, D]) for q in range(2)]
        rsd = [sbuf(f"rsd{q}", [P, TILES, D]) for q in range(2)]
        y = [sbuf(f"y{q}", [P, TILES, D]) for q in range(2)]
        nrm = [sbuf(f"nrm{q}", [P, TILES, D]) for q in range(2)]
        bn = [sbuf(f"bn{q}", [P, TILES, 6]) for q in range(2)]
        mv = [sbuf(f"mv{q}", [P, TILES, 2]) for q in range(2)]
        rs = [sbuf(f"rs{q}", [P, TILES]) for q in range(2)]
        xh = [sbuf(f"xh{q}", [P, KC, GROUP], F32R) for q in range(2)]
        xl = [sbuf(f"xl{q}", [P, KC, GROUP], F32R) for q in range(2)]
        cf = [sbuf(f"cf{q}", [EXPERTS, GROUP]) for q in range(2)]
        ch = [sbuf(f"ch{q}", [EXPERTS, GROUP], F32R) for q in range(2)]
        cl = [sbuf(f"cl{q}", [EXPERTS, GROUP], F32R) for q in range(2)]
        act = [sbuf(f"act{m}", [P, GROUP]) for m in range(2)]
        gat = [sbuf(f"gat{m}", [P, GROUP]) for m in range(2)]
        gh = [sbuf(f"gh{m}", [P, GROUP], F32R) for m in range(MC + 1)]
        gl = [sbuf(f"gl{m}", [P, GROUP], F32R) for m in range(MC + 1)]
        sel_f = sbuf("sel_f", [EXPERTS, MC, 2, HID])
        sel = sbuf("sel", [EXPERTS, MC, P], F32R)
        sb2t = sbuf("sb2t", [P, D])
        T = psum("T", [P, KC, GROUP])
        Hp = [psum(f"Hp{m}", [P, 512]) for m in range(2)]
        Cp = [psum(f"Cp{m}", [P, 512]) for m in range(2)]
        O = psum("O", [P, TILES, D])
        ld, lr, lc = (s["ld0"], s["ld1"]), (s["lr0"], s["lr1"]), (s["lc0"], s["lc1"])
        st, sn = (s["st0"], s["st1"]), (s["sn0"], s["sn1"])
        A = MC + 1

        with nc.Block() as block:
            @block.sync
            def _(eng):
                eng.dma_start(sb2t[:, :], sb2.partition_broadcast(P)).then_inc(s["bias"], 16)

                def load(g, h, q, last):
                    w_ = width_of(last)
                    wait(eng, s["T"], g - 1)
                    eng.dma_start(part(xin[q], last), rows(rows_in, g, last)).then_inc(ld[q], 16)
                    wait_apart(eng, s["cl"], g - 1)
                    at = slice(g * GROUP, g * GROUP + w_) if isinstance(g, int) else bass.ds(g * GROUP, w_)
                    eng.dma_start(cf[q][:, 0:w_], chosen[:, at]).then_inc(lc[q], 16)
                    wait(eng, s["y"], g - 1)
                    eng.dma_start(part(rsd[q], last), rows(residual, g, last)).then_inc(lr[q], 16)
                pipeline(eng, [(0, load)])

            @block.gpsimd
            def _(eng):
                eng.memset(sel_f[:, :, :, :], 0.0).then_inc(s["self"], 1)
                eng.wait_ge(s["self"], 1)
                eng.affine_select(out=sel_f[:, :, :, :], in_=sel_f[:, :, :, :], compare_op=ALU.not_equal, fill=1.0, base=0,
                                  pattern=[[-2, MC], [-1, 2], [0, HID]], channel_multiplier=1).then_inc(s["self"], 1)
                eng.wait_ge(s["bias"], 16)

                def add_bias(g, h, q, last):
                    n, k = (REST, 1) if last else (P, TILES)
                    eng.wait_ge(lr[q], (h + 1) * 16)
                    eng.tensor_tensor(rsd[q][0:n, 0:k, :], rsd[q][0:n, 0:k, :], sb2t[0:n, :].unsqueeze(1).to_broadcast([n, k, D]),
                                      ALU.add).then_inc(s["pa"], 1)
                pipeline(eng, [(0, add_bias), (2, lambda g, h, q, last: row_rstd(eng, s, g, mv[q], half, rs[q], last))])

            @block.tensor
            def _(eng):
                def turn_rows(g, h, q, last):
                    eng.wait_ge(ld[q], (h + 1) * 16)
                    wait(eng, s["lo"], g)
                    for t, n in tiles_of(last):
                        for c in range(KC):
                            m = eng.transpose(T[:, c, t * P:t * P + n], xin[q][0:n, t, c * P:(c + 1) * P], cst.ident[0:n, 0:n])
                    m.then_inc(s["T"], 1)

                def product(g, h, q, last):
                    w_ = width_of(last)
                    eng.wait_ge(s["lo"], g + 1)
                    eng.wait_ge(s["cl"], g + 1)
                    for m in range(A):
                        k = P if m < MC else HID
                        b = m % 2
                        n = g * A + m
                        wait(eng, s["act"], n - 1)
                        for c in range(KC):
                            if m < MC:
                                w_hi, w_lo = w1h[:, c, m * P:(m + 1) * P], w1l[:, c, m * P:(m + 1) * P]
                            else:
                                w_hi, w_lo = s1h[:, c, :], s1l[:, c, :]
                            d = three(eng, Hp[b][0:k, 0:w_], w_hi, w_lo, xh[q][:, c, 0:w_], xl[q][:, c, 0:w_], c == 0, c == KC - 1)
                        if m < MC:
                            nc_ = g * MC + m
                            wait(eng, s["gate"], nc_ - 1)
                            eng.matmul(Cp[b][:, 0:w_], sel[:, m, :], ch[q][:, 0:w_], start=True, stop=False)
                            d = eng.matmul(Cp[b][:, 0:w_], sel[:, m, :], cl[q][:, 0:w_], start=False, stop=True)
                        d.then_inc(s["hm"], 1)

                def down(g, h, q, last):
                    eng.wait_ge(s["gl"], g * A + A)
                    wait(eng, s["y"], g)
                    for t, n in tiles_of(last):
                        ts = slice(t * P, t * P + n)
                        for m in range(A):
                            k = P if m < MC else HID
                            r_hi, r_lo = (w2h[:, m, :], w2l[:, m, :]) if m < MC else (s2h[:, :], s2l[:, :])
                            three(eng, O[0:n, t, :], gh[m][0:k, ts], gl[m][0:k, ts], r_hi, r_lo, m == 0, False)
                        d = three(eng, O[0:n, t, :], ch[q][:, ts], cl[q][:, ts], b2h[:, :], b2l[:, :], False, True)
                    d.then_inc(s["M"], 1)
                eng.wait_ge(s["sel"], 1)
                pipeline(eng, [(0, turn_rows), (1, product), (1, down)])

            @block.scalar
            def _(eng):
                def high(g, h, q, last):
                    w_ = width_of(last)
                    eng.wait_ge(s["T"], g + 1)
                    wait(eng, s["M"], g - 1)
                    eng.activation(xh[q][:, :, 0:w_], T[:, :, 0:w_], ACT.Copy).then_inc(s["hi"], 1)
                    eng.wait_ge(lc[q], (h + 1) * 16)
                    eng.activation(ch[q][:, 0:w_], cf[q][:, 0:w_], ACT.Copy).then_inc(s["ch"], 1)

                def acts(g, h, q, last):
                    w_ = width_of(last)
                    for m in range(A):
                        k = P if m < MC else HID
                        n = g * A + m
                        eng.wait_ge(s["hm"], n + 1)
                        wait(eng, s["gl"], n - 1)
                        bias = b1[:, m:m + 1] if m < MC else sb1[:, :]
                        eng.activation(act[m % 2][0:k, 0:w_], Hp[m % 2][0:k, 0:w_], ACT.Gelu_apprx_tanh, bias=bias).then_inc(s["act"], 1)
                        if m == 0:
                            wait(eng, s["M"], g)
                        if m < MC:
                            eng.wait_ge(s["gate"], g * MC + m + 1)
                            eng.activation(gh[m][:, 0:w_], gat[m % 2][:, 0:w_], ACT.Copy).then_inc(s["gh"], 1)
                        else:
                            eng.wait_ge(s["act"], n + 1)
                            eng.activation(gh[m][0:k, 0:w_], act[m % 2][0:k, 0:w_], ACT.Copy).then_inc(s["gh"], 1)

                def store(g, h, q, last):
                    eng.wait_ge(s["y"], g + 1)
                    eng.dma_start(rows(rows_out, g, last), part(y[q], last)).then_inc(st[q], 16)
                    eng.wait_ge(s["norm"], g + 1)
                    eng.dma_start(rows(normed, g, last), part(nrm[q], last)).then_inc(sn[q], 16)
                eng.wait_ge(s["self"], 2)
                eng.activation(sel[:, :, :], sel_f.ap().rearrange("e m a h -> e m (a h)"), ACT.Copy).then_inc(s["sel"], 1)
                pipeline(eng, [(0, high), (1, acts), (3, store)])
                for q in range(2):
                    eng.wait_ge(st[q], 16 * (NG // 2))
                    eng.wait_ge(sn[q], 16 * (NG // 2))

            @block.vector
            def _(eng):
                def low(g, h, q, last):
                    w_ = width_of(last)
                    eng.wait_ge(s["hi"], g + 1)
                    eng.tensor_tensor(xl[q][:, :, 0:w_], T[:, :, 0:w_], xh[q][:, :, 0:w_].bitcast(F32), ALU.subtract).then_inc(s["lo"], 1)
                    eng.wait_ge(s["ch"], g + 1)
                    eng.tensor_tensor(cl[q][:, 0:w_], cf[q][:, 0:w_], ch[q][:, 0:w_].bitcast(F32), ALU.subtract).then_inc(s["cl"], 1)

                def gates(g, h, q, last):
                    w_ = width_of(last)
                    for m in range(A):
                        n = g * A + m
                        if m < MC:
                            eng.wait_ge(s["act"], n + 1)
                            eng.tensor_tensor(gat[m % 2][:, 0:w_], act[m % 2][:, 0:w_], Cp[m % 2][:, 0:w_], ALU.mult).then_inc(s["gate"], 1)
                            eng.wait_ge(s["gh"], n + 1)
                            eng.tensor_tensor(gl[m][:, 0:w_], gat[m % 2][:, 0:w_], gh[m][:, 0:w_].bitcast(F32), ALU.subtract).then_inc(s["gl"], 1)
                        else:
                            eng.wait_ge(s["gh"], n + 1)
                            eng.tensor_tensor(gl[m][0:HID, 0:w_], act[m % 2][0:HID, 0:w_], gh[m][0:HID, 0:w_].bitcast(F32), ALU.subtract).then_inc(s["gl"], 1)

                def total(g, h, q, last):
                    eng.wait_ge(s["M"], g + 1)
                    eng.wait_ge(s["pa"], g + 1)
                    wait(eng, st[q], h * 16)
                    wait(eng, s["norm"], g - 1)
                    eng.tensor_tensor(part(y[q], last), part(O, last), part(rsd[q], last), ALU.add).then_inc(s["y"], 1)
                    eng.wait_ge(s["y"], g + 1)
                    row_stats(eng, s, g, y[q], bn[q], mv[q], last)

                def norm(g, h, q, last):
                    eng.wait_ge(s["rstd"], g + 1)
                    wait(eng, sn[q], h * 16)
                    row_norm(eng, y[q], nrm[q], mv[q], rs[q], last).then_inc(s["norm"], 1)
                pipeline(eng, [(0, low), (1, gates), (2, total), (3, norm)])


def layer_of(a, layer):
    v = a[bass.ds(layer, 1)]
    names = " ".join("abc"[:len(a.shape) - 1])
    return v.rearrange(f"one {names} -> (one {names.split()[0]}) {' '.join(names.split()[1:])}")


def message_phase(core, cst, ed, table, We, be, layer):
    nc = core.nc
    W = 4
    names = ("krow we hk hix ix swg0 swg1 swg2 swg3 mix sum mh ml sel tix B res hres head sws0 sws1 sws2 sws3")
    with core.phase("message", names) as (s, sbuf, psum):
        krow = sbuf("krow", [P, EP])
        We_b = sbuf("We", [P, D])
        be_b = sbuf("be", [P, D])
        ix = [sbuf(f"ix{q}", [P, 1], U32) for q in range(W)]
        tix = [sbuf(f"tix{q}", [P, 1], U32) for q in range(W)]
        x = [sbuf(f"x{q}", [P, D]) for q in range(W)]
        y = [sbuf(f"y{q}", [P, D]) for q in range(W)]
        z = [sbuf(f"z{q}", [P, D]) for q in range(W)]
        mh = [sbuf(f"mh{q}", [P, D], F32R) for q in range(W)]
        ml = [sbuf(f"ml{q}", [P, D], F32R) for q in range(W)]
        sel = [sbuf(f"sel{q}", [P, P], F32R) for q in range(W)]
        hd = [sbuf(f"hd{q}", [P, ET], F32R) for q in range(W)]
        hkey = sbuf("hkey", [ET, 2])
        hsame = sbuf("hsame", [ET, 1])
        hix = sbuf("hix", [ET, 1], U32)
        hres = sbuf("hres", [ET, D])
        res = [sbuf(f"res{q}", [P, D]) for q in range(W)]
        B = [psum(f"B{q}", [P, D]) for q in range(2)]
        H = psum("H", [ET, D])
        ga, sc = [s[f"swg{q}"] for q in range(W)], [s[f"sws{q}"] for q in range(W)]

        heads = krow.ap().rearrange("a (t p) -> a p t", p=P)[:, 0, :]

        def run(eng, *stages):
            pipeline(eng, stages, count=ET, short_last=False, ways=W)

        with nc.Block() as block:
            @block.sync
            def _(eng):
                eng.dma_start(krow[:, :], ed.key_row[1][0:EP].partition_broadcast(P)).then_inc(s["krow"], 16)
                eng.dma_start(We_b[:, :], layer_of(We, layer).rearrange("one d -> (one d)").partition_broadcast(P)).then_inc(s["we"], 16)
                eng.dma_start(be_b[:, :], be[bass.ds(layer, 1), :].rearrange("one d -> (one d)").partition_broadcast(P)).then_inc(s["we"], 16)
                for j in range(2):
                    eng.dma_start(hkey[:, j:j + 1], ed.key_row[1][j * P:j * P + EP].rearrange("(t p) -> t p", p=P)[:, 0:1],
                                  allow_slow_non_contiguous=True).then_inc(s["hk"], 16)

            @block.gpsimd
            def _(eng):
                def gather(t, h, q, last):
                    wait(eng, s["mix"], t - W + 1)
                    wait_apart(eng, s["ix"], t + 1)
                    eng.indirect_dma_start(x[q][:, :], None, table, bass.IndirectOffsetOnAxis(ap=ix[q][:, :], axis=0)).then_inc(ga[q], 16)

                def scatter(t, h, q, last):
                    eng.wait_ge(s["tix"], t + 1)
                    wait_apart(eng, s["res"], t + 1)
                    eng.indirect_dma_start(ed.sums[1], bass.IndirectOffsetOnAxis(ap=tix[q][:, :], axis=0), res[q][:, :], None,
                                           bounds_check=ROWS - 1, oob_is_err=False).then_inc(sc[q], 16)
                run(eng, (0, gather), (5, scatter))
                for q in range(W):
                    eng.wait_ge(sc[q], 16 * (ET // W))
                eng.wait_ge(s["hres"], 1)
                eng.indirect_dma_start(ed.sums[1], bass.IndirectOffsetOnAxis(ap=hix[:, :], axis=0), hres[:, :], None,
                                       bounds_check=ROWS - 1, oob_is_err=False).then_inc(sc[0], 16)
                eng.wait_ge(sc[0], 16 * (ET // W) + 16)

            @block.vector
            def _(eng):
                eng.wait_ge(s["krow"], 16)
                eng.wait_ge(s["we"], 32)
                eng.wait_ge(s["hk"], 32)
                eng.tensor_tensor(hsame[:, :], hkey[:, 0:1], hkey[:, 1:2], ALU.is_equal).then_inc(s["hix"], 1)
                eng.wait_ge(s["hix"], 1)
                eng.scalar_tensor_tensor(hix[:, :], hsame[:, :], NO_ROW, hkey[:, 0:1], ALU.mult, ALU.add).then_inc(s["hix"], 1)

                def index(t, h, q, last):
                    wait(eng, ga[q], h * 16)
                    eng.tensor_copy(ix[q][:, :], ed.partner[1][:, ds1(t)]).then_inc(s["ix"], 1)

                def select(t, h, q, last):
                    wait(eng, s["B"], t - W + 1)
                    eng.tensor_scalar(hd[q][:, :], heads, ed.key[1][:, ds1(t)], None, ALU.is_equal).then_inc(s["head"], 1)
                    eng.tensor_scalar(sel[q][:, :], krow[:, bass.ts(t, P)], ed.key[1][:, ds1(t)], None, ALU.is_equal).then_inc(s["sel"], 1)

                def target(t, h, q, last):
                    wait(eng, sc[q], h * 16)
                    eng.tensor_copy(tix[q][:, :], ed.target[1][:, ds1(t)]).then_inc(s["tix"], 1)

                def add(t, h, q, last):
                    eng.wait_ge(ga[q], (h + 1) * 16)
                    eng.scalar_tensor_tensor(y[q][:, :], We_b[:, :], ed.weight[1][:, ds1(t)], x[q][:, :], ALU.mult, ALU.add).then_inc(s["mix"], 1)
                    eng.wait_ge(s["mix"], t + 1)
                    wait(eng, s["ml"], t - W + 1)
                    eng.tensor_tensor(z[q][:, :], y[q][:, :], be_b[:, :], ALU.add).then_inc(s["sum"], 1)

                def low(t, h, q, last):
                    eng.wait_ge(s["mh"], t + 1)
                    wait(eng, s["B"], t - W + 1)
                    eng.scalar_tensor_tensor(ml[q][:, :], z[q][:, :], 0.0, mh[q][:, :].bitcast(F32), ALU.max, ALU.subtract).then_inc(s["ml"], 1)
                run(eng, (0, index), (3, add), (4, low), (3, select), (4, target))
                eng.wait_ge(s["B"], ET)
                eng.wait_ge(s["hix"], 2)
                eng.tensor_copy(hres[:, :], H[:, :]).then_inc(s["hres"], 1)

            @block.scalar
            def _(eng):
                def high(t, h, q, last):
                    eng.wait_ge(s["sum"], t + 1)
                    wait(eng, s["B"], t - W + 1)
                    eng.activation(mh[q][:, :], z[q][:, :], ACT.Relu).then_inc(s["mh"], 1)

                def result(t, h, q, last):
                    eng.wait_ge(s["B"], t + 1)
                    wait(eng, sc[q], h * 16)
                    eng.activation(res[q][:, :], B[q % 2][:, :], ACT.Copy).then_inc(s["res"], 1)
                run(eng, (3, high), (5, result))

            @block.tensor
            def _(eng):
                def sums(t, h, q, last):
                    eng.wait_ge(s["ml"], t + 1)
                    eng.wait_ge(s["sel"], t + 1)
                    wait(eng, s["res"], t - 1)
                    eng.matmul(B[q % 2][:, :], sel[q][:, :], mh[q][:, :], start=True, stop=False)
                    eng.matmul(B[q % 2][:, :], sel[q][:, :], ml[q][:, :], start=False, stop=True)
                    eng.wait_ge(s["head"], t + 1)
                    first, end = (isinstance(t, int) and t == 0), (isinstance(t, int) and t == ET - 1)
                    eng.matmul(H[:, :], hd[q][:, :], mh[q][:, :], start=first, stop=False)
                    eng.matmul(H[:, :], hd[q][:, :], ml[q][:, :], start=False, stop=end).then_inc(s["B"], 1)
                run(eng, (4, sums))


def hidden_phase(core, cst, ed, table, eps, b1, w, layer, hT, stats):
    nc = core.nc
    wh, wl = w
    names = "eps eps1 b1 ld0 ld1 la pre T hi lo M ev bn"
    with core.phase("hidden", names) as (s, sbuf, psum):
        e_t = sbuf("eps", [P, 1])
        b1t = sbuf("b1", [P, KC])
        xin = [sbuf(f"xin{q}", [P, TILES, D]) for q in range(2)]
        agg = sbuf("agg", [P, TILES, D])
        xh = [sbuf(f"xh{q}", [P, KC, GROUP], F32R) for q in range(2)]
        xl = [sbuf(f"xl{q}", [P, KC, GROUP], F32R) for q in range(2)]
        T = [psum(f"T{q}", [P, KC, GROUP]) for q in range(2)]
        O = [psum(f"O{q}", [P, KC, GROUP]) for q in range(2)]
        ld = (s["ld0"], s["ld1"])
        at = lambda g, w_: slice(g * GROUP, g * GROUP + w_) if isinstance(g, int) else bass.ds(g * GROUP, w_)
        with nc.Block() as block:
            @block.sync
            def _(eng):
                eng.dma_start(e_t[:, :], eps[bass.ds(layer, 1)].partition_broadcast(P)).then_inc(s["eps"], 16)
                eng.dma_start(b1t[:, :], b1[bass.ds(layer, 1), :].rearrange("one (c p) -> (one p) c", p=P),
                              allow_slow_non_contiguous=True).then_inc(s["b1"], 16)

                def load(g, h, q, last):
                    wait_apart(eng, s["T"], g - 1)
                    eng.dma_start(part(xin[q], last), rows(table, g, last)).then_inc(ld[q], 16)
                    wait_apart(eng, s["pre"], g)
                    eng.dma_start(part(agg, last), rows(ed.sums[1], g, last)).then_inc(s["la"], 16)
                pipeline(eng, [(0, load)])

            @block.tensor
            def _(eng):
                def product(g, h, q, last):
                    w_ = width_of(last)
                    eng.wait_ge(s["lo"], g + 1)
                    wait(eng, s["ev"], g - 1)
                    for o in range(KC):
                        for c in range(KC):
                            cs = slice(o * P, (o + 1) * P)
                            m = three(eng, O[q][:, o, 0:w_], wh[:, c, cs], wl[:, c, cs], xh[q][:, c, 0:w_], xl[q][:, c, 0:w_],
                                      c == 0, c == KC - 1)
                    m.then_inc(s["M"], 1)
                pipeline(eng, [(0, lambda g, h, q, last: turn(eng, s, g, h, q, last, None, xin, T, cst.ident)), (1, product)])

            @block.scalar
            def _(eng):
                def evacuate(g, h, q, last):
                    w_ = width_of(last)
                    wait_apart(eng, s["M"], g + 1)
                    for o in range(KC):
                        m = eng.activation(hT[:, o, at(g, w_)], O[q][:, o, 0:w_], ACT.Identity, bias=b1t[:, o:o + 1])
                    m.then_inc(s["ev"], 1)
                eng.wait_ge(s["b1"], 16)
                pipeline(eng, [(0, lambda g, h, q, last: split_hi(eng, s, g, q, last, T, xh)), (1, evacuate)])

            @block.vector
            def _(eng):
                eng.wait_ge(s["eps"], 16)
                eng.tensor_scalar(e_t[:, :], e_t[:, :], 1.0, None, ALU.add).then_inc(s["eps1"], 1)
                eng.wait_ge(s["eps1"], 1)

                def mix(g, h, q, last):
                    eng.wait_ge(ld[q], (h + 1) * 16)
                    eng.wait_ge(s["la"], (g + 1) * 16)
                    eng.scalar_tensor_tensor(part(xin[q], last), part(xin[q], last), e_t[0:REST if last else P, :], part(agg, last),
                                             ALU.mult, ALU.add).then_inc(s["pre"], 1)

                def statistics(g, h, q, last):
                    w_ = width_of(last)
                    wait_apart(eng, s["ev"], g + 1)
                    for o in range(KC):
                        m = eng.bn_stats(stats[:, o, ds1(g), :].rearrange("a one k -> a (one k)"), hT[:, o, at(g, w_)])
                    m.then_inc(s["bn"], 1)
                pipeline(eng, [(0, mix), (1, lambda g, h, q, last: split_lo(eng, s, g, q, last, T, xh, xl)), (2, statistics)])


def output_phase(core, cst, table, gamma, beta, b2, w, layer, hT, stats):
    nc = core.nc
    wh, wl = w
    names = "ld b2 agg var rstd sc mean aff nrm hi lo M add y st0 st1"
    with core.phase("output", names) as (s, sbuf, psum):
        gm = sbuf("gm", [P, KC])
        bt = sbuf("bt", [P, KC])
        b2t = sbuf("b2t", [P, D])
        mv = sbuf("mv", [P, KC, 2])
        rs = sbuf("rs", [P, KC])
        scl = sbuf("scl", [P, KC])
        ms = sbuf("ms", [P, KC])
        shf = sbuf("shf", [P, KC])
        hh = [sbuf(f"hh{q}", [P, KC, GROUP], F32R) for q in range(2)]
        hl = [sbuf(f"hl{q}", [P, KC, GROUP], F32R) for q in range(2)]
        y = [sbuf(f"y{q}", [P, TILES, D]) for q in range(2)]
        O = [psum(f"O{q}", [P, TILES, D]) for q in range(2)]
        st = (s["st0"], s["st1"])
        at = lambda g, w_: slice(g * GROUP, g * GROUP + w_) if isinstance(g, int) else bass.ds(g * GROUP, w_)
        with nc.Block() as block:
            @block.sync
            def _(eng):
                for t, a in ((gm, gamma), (bt, beta)):
                    eng.dma_start(t[:, :], a[bass.ds(layer, 1), :].rearrange("one (c p) -> (one p) c", p=P),
                                  allow_slow_non_contiguous=True).then_inc(s["ld"], 16)
                eng.dma_start(b2t[:, :], b2[bass.ds(layer, 1), :].rearrange("one d -> (one d)").partition_broadcast(P)).then_inc(s["b2"], 16)

                def store(g, h, q, last):
                    wait_apart(eng, s["y"], g + 1)
                    eng.dma_start(rows(table, g, last), part(y[q], last)).then_inc(st[q], 16)
                pipeline(eng, [(0, store)])
                for q in range(2):
                    eng.wait_ge(st[q], 16 * (NG // 2))

            @block.gpsimd
            def _(eng):
                eng.wait_ge(s["var"], 1)
                eng.tensor_tensor(rs[:, :], mv[:, :, 1], cst.half[:, :], ALU.pow).then_inc(s["rstd"], 1)

            @block.vector
            def _(eng):
                for o in range(KC):
                    m = eng.bn_aggr(mv[:, o, :], stats[:, o, :, :].rearrange("a g k -> a (g k)"))
                m.then_inc(s["agg"], 1)
                eng.wait_ge(s["agg"], 1)
                eng.tensor_scalar(mv[:, :, 1], mv[:, :, 1], EPS, None, ALU.add).then_inc(s["var"], 1)
                eng.wait_ge(s["rstd"], 1)
                eng.wait_ge(s["ld"], 32)
                eng.tensor_tensor(scl[:, :], rs[:, :], gm[:, :], ALU.mult).then_inc(s["sc"], 1)
                eng.wait_ge(s["sc"], 1)
                eng.tensor_tensor(ms[:, :], mv[:, :, 0], scl[:, :], ALU.mult).then_inc(s["mean"], 1)
                eng.wait_ge(s["mean"], 1)
                eng.tensor_tensor(shf[:, :], bt[:, :], ms[:, :], ALU.subtract).then_inc(s["aff"], 1)
                eng.wait_ge(s["b2"], 16)

                def low(g, h, q, last):
                    w_ = width_of(last)
                    eng.wait_ge(s["hi"], g + 1)
                    eng.tensor_tensor(hl[q][:, :, 0:w_], hT[:, :, at(g, w_)], hh[q][:, :, 0:w_].bitcast(F32), ALU.subtract).then_inc(s["lo"], 1)

                def add(g, h, q, last):
                    n, k = (REST, 1) if last else (P, TILES)
                    eng.wait_ge(s["M"], g + 1)
                    wait(eng, st[q], h * 16)
                    eng.tensor_tensor(part(y[q], last), part(O[q], last), b2t[0:n, :].unsqueeze(1).to_broadcast([n, k, D]),
                                      ALU.add).then_inc(s["add"], 1)
                pipeline(eng, [(0, low), (1, add)])

            @block.scalar
            def _(eng):
                def normal(g, h, q, last):
                    w_ = width_of(last)
                    for o in range(KC):
                        m = eng.activation(hT[:, o, at(g, w_)], hT[:, o, at(g, w_)], ACT.Relu, bias=shf[:, o:o + 1], scale=scl[:, o:o + 1])
                    m.then_inc(s["nrm"], 1)
                    eng.wait_ge(s["nrm"], g + 1)
                    wait_apart(eng, s["M"], g - 1)
                    eng.activation(hh[q][:, :, 0:w_], hT[:, :, at(g, w_)], ACT.Copy).then_inc(s["hi"], 1)

                def finish(g, h, q, last):
                    eng.wait_ge(s["add"], g + 1)
                    eng.activation(part(y[q], last), part(y[q], last), ACT.Relu).then_inc(s["y"], 1)
                eng.wait_ge(s["aff"], 1)
                pipeline(eng, [(0, normal), (2, finish)])

            @block.tensor
            def _(eng):
                def product(g, h, q, last):
                    eng.wait_ge(s["lo"], g + 1)
                    wait(eng, s["add"], g - 1)
                    for t, n in tiles_of(last):
                        ts = slice(t * P, t * P + n)
                        for c in range(KC):
                            m = three(eng, O[q][0:n, t, :], hh[q][:, c, ts], hl[q][:, c, ts], wh[:, c, :], wl[:, c, :], c == 0, c == KC - 1)
                    m.then_inc(s["M"], 1)
                pipeline(eng, [(0, product)])


def ternary_phase(core, cst, w_up, w_down, up, down, scales):
    nc = core.nc
    names = "ld abs sum mean clip rec sc rnd q cp T"
    with core.phase("ternary", names) as (s, sbuf, psum):
        wu = sbuf("wu", [HID, D])
        wd = sbuf("wd", [P, KC, HID])
        qu = sbuf("qu", [HID, D])
        qd = sbuf("qd", [P, KC, HID])
        bu = sbuf("bu", [HID, D], BF16)
        bd = sbuf("bd", [P, KC, HID], BF16)
        total = sbuf("total", [P, 2])
        ones = sbuf("ones", [P, P])
        inv = sbuf("inv", [P, 2])
        S = psum("S", [P, 2])
        Tu = psum("Tu", [P, KC, HID], BF16)
        Td = psum("Td", [HID, KC, P], BF16)
        with nc.Block() as block:
            @block.sync
            def _(eng):
                eng.dma_start(wu[:, :], w_up).then_inc(s["ld"], 16)
                eng.dma_start(wd[:, :, :], w_down.rearrange("(c p) h -> p c h", p=P)).then_inc(s["ld"], 16)

            @block.vector
            def _(eng):
                eng.memset(total[:, :], 0.0).then_inc(s["abs"], 1)
                eng.memset(ones[:, :], 1.0)
                eng.wait_ge(s["ld"], 32)
                eng.wait_ge(s["abs"], 1)
                eng.tensor_reduce(total[0:HID, 0:1], wu[:, :], AX.X, ALU.add, apply_absolute_value=True)
                eng.tensor_reduce(total[:, 1:2], wd.ap().rearrange("a c h -> a (c h)"), AX.X, ALU.add, apply_absolute_value=True).then_inc(s["sum"], 1)
                eng.wait_ge(s["mean"], 1)
                eng.tensor_scalar(scales[:, :], S[:, :], 1.0 / (HID * D), EPS, ALU.mult, ALU.max).then_inc(s["clip"], 1)
                eng.wait_ge(s["clip"], 1)
                eng.reciprocal(inv[:, :], scales[:, :]).then_inc(s["rec"], 1)
                eng.wait_ge(s["rec"], 1)
                eng.tensor_scalar(qu[:, :], wu[:, :], inv[0:HID, 0:1], MAGIC, ALU.mult, ALU.add)
                eng.tensor_scalar(qd[:, :, :], wd[:, :, :], inv[:, 1:2], MAGIC, ALU.mult, ALU.add).then_inc(s["rnd"], 1)
                eng.wait_ge(s["rnd"], 1)
                eng.tensor_scalar(qu[:, :], qu[:, :], MAGIC, 1.0, ALU.subtract, ALU.min)
                eng.tensor_scalar(qd[:, :, :], qd[:, :, :], MAGIC, 1.0, ALU.subtract, ALU.min).then_inc(s["rnd"], 1)
                eng.wait_ge(s["rnd"], 2)
                eng.tensor_scalar(bu[:, :], qu[:, :], -1.0, None, ALU.max)
                eng.tensor_scalar(bd[:, :, :], qd[:, :, :], -1.0, None, ALU.max).then_inc(s["q"], 1)
                eng.wait_ge(s["T"], 1)
                eng.tensor_copy(up[:, :, :], Tu[:, :, :])
                eng.tensor_copy(down[:, :], Td.ap().rearrange("h c o -> h (c o)"))

            @block.tensor
            def _(eng):
                eng.wait_ge(s["sum"], 1)
                eng.matmul(S[:, :], ones[:, :], total[:, :], start=True, stop=True).then_inc(s["mean"], 1)
                eng.wait_ge(s["q"], 1)
                for c in range(KC):
                    eng.transpose(Tu[:, c, :], bu[:, c * P:(c + 1) * P], cst.ident_b[0:HID, 0:HID])
                for c in range(KC):
                    m = eng.transpose(Td[:, c, :], bd[:, c, :], cst.ident_b[:, :])
                m.then_inc(s["T"], 1)


def quantized_phase(core, cst, x2, gnn, up, down, scales, half, out):
    nc = core.nc
    LVL = 127.0
    W, R = 8, 4
    names = ("ld0 ld1 ld2 ld3 lg0 lg1 lg2 lg3 st0 st1 st2 st3 x3 stats aggr var neg rstd nb nrm amax unit "
             "lvl magic rnd clip q T qT U h0 h1 h2 am2 u2 lv2 s1 s2 q2 T2 q2T O y k")
    with core.phase("quant", names) as (s, sbuf, psum):
        def ring(n, shape, dt=F32):
            return [sbuf(f"{n}{q}", shape, dt) for q in range(R)] * (W // R)

        x3 = [sbuf(f"x3{q}", [P, TILES, D]) for q in range(W)]
        gn, nr, rd, yo = (ring(n, [P, TILES, D]) for n in ("gn", "nr", "rd", "yo"))
        xq, xqT = ring("xq", [P, TILES, D], BF16), ring("xqT", [P, KC, GROUP], BF16)
        bn, mv = ring("bn", [P, TILES, 6]), ring("mv", [P, TILES, 2])
        rs, ng, nb = (ring(n, [P, TILES]) for n in ("rs", "ng", "nb"))
        am, un, lv, k0, am2, un2, lv2, k1 = (ring(n, [P, TILES]) for n in ("am", "un", "lv", "k0", "am2", "un2", "lv2", "k1"))
        hf, hr, hs = (ring(n, [P, TILES, HID]) for n in ("hf", "hr", "hs"))
        magic = sbuf("magic", [P, 1])
        hq, hqT = ring("hq", [P, TILES, HID], BF16), ring("hqT", [HID, GROUP], BF16)
        T = psum("T", [P, KC, GROUP], BF16)
        U = psum("U", [P, TILES, HID])
        T2 = psum("T2", [HID, GROUP], BF16)
        O = psum("O", [P, TILES, D])
        ld, lg, st = ([s[f"{n}{q}"] for q in range(R)] * (W // R) for n in ("ld", "lg", "st"))
        H = lambda h, q: h * (W // R) + q // R
        nk = lambda last: (REST, 1) if last else (P, TILES)

        with nc.Block() as block:
            @block.sync
            def _(eng):
                def load(g, h, q, last):
                    wait_apart(eng, s["y"], g - W + 1)
                    wait_apart(eng, s["x3"], g - R + 1)
                    eng.dma_start(part(x3[q], last), rows(x2, g, last)).then_inc(ld[q], 16)
                    eng.dma_start(part(gn[q], last), rows(gnn, g, last)).then_inc(lg[q], 16)
                pipeline(eng, [(0, load)], ways=W)

            @block.gpsimd
            def _(eng):
                eng.memset(magic[:, :], MAGIC).then_inc(s["magic"], 1)

                def rstd(g, h, q, last):
                    n, k = nk(last)
                    row_rstd(eng, s, g, mv[q], half, rs[q], last)
                    eng.wait_ge(s["rstd"], g + 1)
                    eng.tensor_tensor(nb[q][0:n, 0:k], ng[q][0:n, 0:k], rs[q][0:n, 0:k], ALU.mult).then_inc(s["nb"], 1)

                def add(g, h, q, last):
                    eng.wait_ge(ld[q], (H(h, q) + 1) * 16)
                    eng.wait_ge(lg[q], (H(h, q) + 1) * 16)
                    eng.tensor_tensor(part(x3[q], last), part(x3[q], last), part(gn[q], last), ALU.add).then_inc(s["x3"], 1)
                pipeline(eng, [(2, rstd), (1, add)], ways=W)

            @block.vector
            def _(eng):
                def stats(g, h, q, last):
                    n, k = nk(last)
                    eng.wait_ge(s["x3"], g + 1)
                    wait(eng, s["nb"], g - R + 1)
                    row_stats(eng, s, g, x3[q], bn[q], mv[q], last, negated=ng[q])

                def levels(g, h, q, last):
                    n, k = nk(last)
                    eng.wait_ge(s["nrm"], g + 1)
                    eng.tensor_reduce(am[q][0:n, 0:k], nr[q][0:n, 0:k, :], AX.X, ALU.max, apply_absolute_value=True).then_inc(s["amax"], 1)
                    eng.wait_ge(s["amax"], g + 1)
                    eng.tensor_scalar(un[q][0:n, 0:k], am[q][0:n, 0:k], EPS, 1.0 / LVL, ALU.max, ALU.mult).then_inc(s["unit"], 1)
                    eng.wait_ge(s["unit"], g + 1)
                    eng.reciprocal(lv[q][0:n, 0:k], un[q][0:n, 0:k]).then_inc(s["lvl"], 1)
                    eng.tensor_scalar(k0[q][0:n, 0:k], un[q][0:n, 0:k], scales[0:n, 0:1], None, ALU.mult)

                def clamp(g, h, q, last):
                    n, k = nk(last)
                    eng.wait_ge(s["rnd"], g + 1)
                    eng.tensor_scalar(rd[q][0:n, 0:k, :], rd[q][0:n, 0:k, :], MAGIC + LVL, MAGIC - LVL - 1, ALU.min, ALU.max).then_inc(s["clip"], 1)

                def hidden(g, h, q, last):
                    n, k = nk(last)
                    eng.wait_ge(s["U"], g + 1)
                    for t, r in tiles_of(last):
                        m = eng.tensor_scalar(hf[q][0:r, t, :], U[0:r, t, :], k0[q][0:r, t:t + 1], 0.0, ALU.mult, ALU.max)
                    m.then_inc(s["h0"], 1)
                    eng.wait_ge(s["h0"], g + 1)
                    eng.tensor_scalar(hr[q][0:n, 0:k, :], hf[q][0:n, 0:k, :], MAGIC, MAGIC, ALU.add, ALU.subtract).then_inc(s["h1"], 1)
                    eng.wait_ge(s["h1"], g + 1)
                    eng.tensor_scalar(hf[q][0:n, 0:k, :], hr[q][0:n, 0:k, :], LVL, -LVL - 1, ALU.min, ALU.max).then_inc(s["h2"], 1)
                    eng.wait_ge(s["h2"], g + 1)
                    eng.tensor_reduce(am2[q][0:n, 0:k], hf[q][0:n, 0:k, :], AX.X, ALU.max, apply_absolute_value=True).then_inc(s["am2"], 1)
                    eng.wait_ge(s["am2"], g + 1)
                    eng.tensor_scalar(un2[q][0:n, 0:k], am2[q][0:n, 0:k], EPS, 1.0 / LVL, ALU.max, ALU.mult).then_inc(s["u2"], 1)
                    eng.wait_ge(s["u2"], g + 1)
                    eng.reciprocal(lv2[q][0:n, 0:k], un2[q][0:n, 0:k]).then_inc(s["lv2"], 1)
                    eng.tensor_scalar(k1[q][0:n, 0:k], un2[q][0:n, 0:k], scales[0:n, 1:2], None, ALU.mult).then_inc(s["k"], 1)
                    eng.wait_ge(s["lv2"], g + 1)
                    for t, r in tiles_of(last):
                        m = eng.tensor_scalar(hs[q][0:r, t, :], hf[q][0:r, t, :], lv2[q][0:r, t:t + 1], MAGIC, ALU.mult, ALU.add)
                    m.then_inc(s["s1"], 1)
                    eng.wait_ge(s["s1"], g + 1)
                    eng.tensor_scalar(hr[q][0:n, 0:k, :], hs[q][0:n, 0:k, :], MAGIC + LVL, MAGIC - LVL - 1, ALU.min, ALU.max).then_inc(s["s2"], 1)
                    eng.wait_ge(s["s2"], g + 1)
                    wait(eng, s["T2"], g - R + 1)
                    eng.tensor_scalar(hq[q][0:n, 0:k, :], hr[q][0:n, 0:k, :], MAGIC, None, ALU.subtract).then_inc(s["q2"], 1)

                def final(g, h, q, last):
                    eng.wait_ge(s["O"], g + 1)
                    wait(eng, st[q], H(h, q) * 16)
                    eng.wait_ge(s["k"], g + 1)
                    for t, r in tiles_of(last):
                        m = eng.scalar_tensor_tensor(yo[q][0:r, t, :], O[0:r, t, :], k1[q][0:r, t:t + 1], x3[q][0:r, t, :], ALU.mult, ALU.add)
                    m.then_inc(s["y"], 1)
                pipeline(eng, [(7, final), (6, hidden), (5, clamp), (2, stats), (4, levels)], ways=W)

            @block.scalar
            def _(eng):
                def integers(g, h, q, last):
                    n, k = nk(last)
                    eng.wait_ge(s["clip"], g + 1)
                    wait(eng, s["T"], g - R + 1)
                    eng.activation(xq[q][0:n, 0:k, :], rd[q][0:n, 0:k, :], ACT.Copy, bias=-MAGIC).then_inc(s["q"], 1)

                def norm(g, h, q, last):
                    eng.wait_ge(s["nb"], g + 1)
                    wait(eng, s["rnd"], g - R + 1)
                    for t, r in tiles_of(last):
                        m = eng.activation(nr[q][0:r, t, :], x3[q][0:r, t, :], ACT.Identity, bias=nb[q][0:r, t:t + 1], scale=rs[q][0:r, t:t + 1])
                    m.then_inc(s["nrm"], 1)

                def scale(g, h, q, last):
                    eng.wait_ge(s["lvl"], g + 1)
                    wait(eng, s["q"], g - R + 1)
                    for t, r in tiles_of(last):
                        m = eng.activation(rd[q][0:r, t, :], nr[q][0:r, t, :], ACT.Identity, bias=magic[0:r, :], scale=lv[q][0:r, t:t + 1])
                    m.then_inc(s["rnd"], 1)

                def copy_rows(g, h, q, last):
                    w_ = width_of(last)
                    eng.wait_ge(s["T"], g + 1)
                    wait(eng, s["U"], g - R + 1)
                    eng.activation(xqT[q][:, :, 0:w_], T[:, :, 0:w_], ACT.Copy).then_inc(s["qT"], 1)

                def copy_hidden(g, h, q, last):
                    w_ = width_of(last)
                    eng.wait_ge(s["T2"], g + 1)
                    wait(eng, s["O"], g - R + 1)
                    eng.activation(hqT[q][:, 0:w_], T2[:, 0:w_], ACT.Copy).then_inc(s["q2T"], 1)

                def store(g, h, q, last):
                    eng.wait_ge(s["y"], g + 1)
                    eng.dma_start(rows(out, g, last), part(yo[q], last)).then_inc(st[q], 16)
                eng.wait_ge(s["magic"], 1)
                pipeline(eng, [(3, norm), (7, store), (6, copy_hidden), (5, integers), (5, copy_rows), (4, scale)], ways=W)
                for q in range(R):
                    eng.wait_ge(st[q], 16 * (NG // R))

            @block.tensor
            def _(eng):
                def turn_hidden(g, h, q, last):
                    eng.wait_ge(s["q2"], g + 1)
                    wait_apart(eng, s["q2T"], g)
                    for t, n in tiles_of(last):
                        m = eng.transpose(T2[:, t * P:t * P + n], hq[q][0:n, t, :], cst.ident_b[0:n, 0:n])
                    m.then_inc(s["T2"], 1)

                def down_(g, h, q, last):
                    eng.wait_ge(s["q2T"], g + 1)
                    wait(eng, s["y"], g)
                    for t, n in tiles_of(last):
                        m = eng.matmul(O[0:n, t, :], hqT[q][:, t * P:t * P + n], down[:, :], start=True, stop=True)
                    m.then_inc(s["O"], 1)

                def turn_rows(g, h, q, last):
                    eng.wait_ge(s["q"], g + 1)
                    wait(eng, s["qT"], g)
                    for t, n in tiles_of(last):
                        for c in range(KC):
                            m = eng.transpose(T[:, c, t * P:t * P + n], xq[q][0:n, t, c * P:(c + 1) * P], cst.ident_b[0:n, 0:n])
                    m.then_inc(s["T"], 1)

                def up_(g, h, q, last):
                    eng.wait_ge(s["qT"], g + 1)
                    wait(eng, s["h0"], g)
                    for t, n in tiles_of(last):
                        for c in range(KC):
                            m = eng.matmul(U[0:n, t, :], xqT[q][:, c, t * P:t * P + n], up[:, c, :], start=c == 0, stop=c == KC - 1)
                    m.then_inc(s["U"], 1)
                pipeline(eng, [(6, turn_hidden), (6, down_), (5, turn_rows), (5, up_)], ways=W)


def scratch(nc, name, shape):
    return nc.dram_tensor(name, shape, F32).ap()


def first_gnn(core, cst, ed, a, x, normed, hidden, rows_out, normed_out):
    nc = core.nc
    for n, table in ((1, normed), (2, hidden)):
        with nc.sbuf_tensor(f"w_hi{n}", [P, RELATIONS * KC, D], F32R) as w_hi, \
                nc.sbuf_tensor(f"w_lo{n}", [P, RELATIONS * KC, D], F32R) as w_lo:
            combine_phase(core, cst, a[f"L0_gnn_basis{n}"], a[f"L0_gnn_att{n}"], w_hi, w_lo)
            relation_phase(core, cst, ed, table, a[f"L0_gnn_gate_w{n}"], w_hi, w_lo)
        with nc.sbuf_tensor(f"root_hi{n}", [P, KC, D], F32R) as hi, nc.sbuf_tensor(f"root_lo{n}", [P, KC, D], F32R) as lo:
            split_phase(core, "root_split", [(chunked(a[f"L0_gnn_root{n}"]), hi[:, :, :], lo[:, :, :])])
            if n == 1:
                root_phase(core, cst, ed, normed, (hi, lo), a["L0_gnn_bias1"], cst.half, hidden)
            else:
                root_phase(core, cst, ed, hidden, (hi, lo), a["L0_gnn_bias2"], cst.half, rows_out, x, normed_out)


def first_ffn(core, cst, a, x, normed, probs, chosen, rows_out, normed_out):
    nc = core.nc
    MC = EXPERTS * HID // P
    route_phase(core, cst, normed, a["L0_ffn_gate_w"], probs)
    select_phase(core, cst, probs, chosen)
    with ExitStack() as memory:
        def both(n, shape):
            return [memory.enter_context(nc.sbuf_tensor(f"ffn_{n}_{j}", shape, F32R)) for j in ("hi", "lo")]

        w1, w2 = both("w1", [P, KC, EXPERTS * HID]), both("w2", [P, MC, D])
        s1, s2, b2 = both("s1", [P, KC, HID]), both("s2", [HID, D]), both("b2", [EXPERTS, D])
        b1 = memory.enter_context(nc.sbuf_tensor("ffn_b1", [P, MC], F32))
        sb1 = memory.enter_context(nc.sbuf_tensor("ffn_sb1", [HID, 1], F32))
        w1_in = a["L0_ffn_w1"].rearrange("e (c p) h -> p c e h", p=P)
        split_phase(core, "w1_split", [
            (w1_in[:, c, :, :], w1[0][:, c, :].rearrange("p (e h) -> p e h", e=EXPERTS),
             w1[1][:, c, :].rearrange("p (e h) -> p e h", e=EXPERTS)) for c in range(KC)])
        split_phase(core, "w2_split", [
            (a["L0_ffn_w2"].rearrange("(m a) h d -> (a h) m d", a=2), w2[0][:, :, :], w2[1][:, :, :]),
            (chunked(a["L0_ffn_sw1"]), s1[0][:, :, :], s1[1][:, :, :]),
            (a["L0_ffn_sw2"], s2[0][:, :], s2[1][:, :]), (a["L0_ffn_b2"], b2[0][:, :], b2[1][:, :])])
        with core.phase("ffn_bias", "b1 sb1") as (s, _, _), nc.Block() as block:
            @block.sync
            def _(eng):
                eng.dma_start(b1[:, :], a["L0_ffn_b1"].rearrange("(m a) h -> (a h) m", a=2),
                              allow_slow_non_contiguous=True).then_inc(s["b1"], 16)
                eng.dma_start(sb1[:, :], a["L0_ffn_sb1"].unsqueeze(1)).then_inc(s["sb1"], 16)
                eng.wait_ge(s["b1"], 16)
                eng.wait_ge(s["sb1"], 16)
        experts_phase(core, cst, normed, x, chosen, (w1, w2, s1, s2, b2, b1, sb1, a["L0_ffn_sb2"]), cst.half,
                      rows_out, normed_out)


def second_gnn(core, cst, ed, a, g):
    nc = core.nc
    with nc.Fori(0, LAYERS) as layer:
        def weight(name):
            return a[name][bass.ds(layer, 1)].rearrange("one (c p) n -> (one p) c n", p=P)

        message_phase(core, cst, ed, g, a["L1_gnn_We"], a["L1_gnn_be"], layer)
        with nc.sbuf_tensor("hT", [P, KC, N], F32) as hT, nc.sbuf_tensor("h_stats", [P, KC, NG, 6], F32) as stats:
            with nc.sbuf_tensor("w1_hi", [P, KC, D], F32R) as hi, nc.sbuf_tensor("w1_lo", [P, KC, D], F32R) as lo:
                split_phase(core, "W1_split", [(weight("L1_gnn_W1"), hi[:, :, :], lo[:, :, :])])
                hidden_phase(core, cst, ed, g, a["L1_gnn_eps"], a["L1_gnn_b1"], (hi, lo), layer, hT, stats)
            with nc.sbuf_tensor("w2_hi", [P, KC, D], F32R) as hi, nc.sbuf_tensor("w2_lo", [P, KC, D], F32R) as lo:
                split_phase(core, "W2_split", [(weight("L1_gnn_W2"), hi[:, :, :], lo[:, :, :])])
                output_phase(core, cst, g, a["L1_gnn_gamma"], a["L1_gnn_beta"], a["L1_gnn_b2"], (hi, lo), layer, hT, stats)


def second_ffn(core, cst, a, x, g, out):
    nc = core.nc
    with nc.sbuf_tensor("up", [P, KC, HID], BF16) as up, nc.sbuf_tensor("down", [HID, D], BF16) as down, \
            nc.sbuf_tensor("scales", [P, 2], F32) as scales:
        ternary_phase(core, cst, a["L1_ffn_w_up"], a["L1_ffn_w_down"], up, down, scales)
        quantized_phase(core, cst, x, g, up, down, scales, cst.half, out)


def build(nc, a, out):
    core = Core(nc)
    ed = Edges(nc)
    normed0, hidden, x1, normed1 = (scratch(nc, n, (N, D)) for n in ("normed0", "hidden", "x1", "normed1"))
    x2, g = scratch(nc, "x2", (N, D)), scratch(nc, "g", (N, D))
    probs, chosen = scratch(nc, "probs", (EXPERTS, N)), scratch(nc, "chosen", (EXPERTS, N))
    with ExitStack() as early:
        cst = Constants(core, early)
        order_phase(core, ed, cst, a["src"], a["dst"], a["edge_type_2"], a["edge_weight1"])
        norm_phase(core, a["x"], normed0, cst.half)
        first_gnn(core, cst, ed, a, a["x"], normed0, hidden, x1, normed1)
        first_ffn(core, cst, a, x1, normed1, probs, chosen, x2, g)
    second_gnn(core, cst, ed, a, g)
    second_ffn(core, cst, a, x2, g, out)


_INS = """x src dst edge_type_2 edge_weight1 L0_gnn_basis1 L0_gnn_att1 L0_gnn_gate_w1 L0_gnn_root1 L0_gnn_bias1
    L0_gnn_basis2 L0_gnn_att2 L0_gnn_gate_w2 L0_gnn_root2 L0_gnn_bias2 L0_ffn_gate_w L0_ffn_w1 L0_ffn_b1 L0_ffn_w2
    L0_ffn_b2 L0_ffn_sw1 L0_ffn_sb1 L0_ffn_sw2 L0_ffn_sb2 L1_gnn_eps L1_gnn_We L1_gnn_be L1_gnn_W1 L1_gnn_b1
    L1_gnn_gamma L1_gnn_beta L1_gnn_W2 L1_gnn_b2 L1_ffn_w_up L1_ffn_w_down""".split()


def kernel(**inputs):
    import numpy as np
    import concourse.bacc as bacc
    from concourse.bass_utils import run_bass_kernel_spmd

    nc = bacc.Bacc("TRN2", target_bir_lowering=False, num_devices=1)
    arrays, args = {}, {}
    for name in _INS:
        v = np.ascontiguousarray(inputs[name])
        arrays[f"in_{name}"] = v
        args[name] = nc.dram_tensor(f"in_{name}", v.shape, mybir.dt.from_np(v.dtype), kind="ExternalInput").ap()
    out = nc.dram_tensor("out", (N, D), F32, kind="ExternalOutput").ap()
    build(nc, args, out)
    r = run_bass_kernel_spmd(nc, [arrays], core_ids=[0])
    return r.results[0]["out"]
```

```python
import concourse.bass as bass
from concourse import mybir
from concourse.alu_op_type import AluOpType as ALU
from contextlib import ExitStack, contextmanager

F32, F32R, BF16 = mybir.dt.float32, mybir.dt.float32r, mybir.dt.bfloat16
I32, U32 = mybir.dt.int32, mybir.dt.uint32
ACT = mybir.ActivationFunctionType
AX = mybir.AxisListType

P = 128
N, D, E = 10000, 512, 5000
KC = D // P
RELATIONS, BASES = 2, 30
EXPERTS, HID = 16, 64
CAP = 625
LAYERS = 4
GROUP = 256
TILES = GROUP // P
NG = -(-N // GROUP)
REST = N - (NG - 1) * GROUP
ET = -(-E // P)
EP = ET * P
EPS = 1e-5
MAGIC = 1.5 * 2.0 ** 23
NO_ROW = float(1 << 20)


def wait(eng, sem, value):
    if not isinstance(value, int) or value > 0:
        eng.wait_ge(sem, value)


def pipeline(eng, stages, count=NG, short_last=True, ways=2):
    deepest = max(lag for lag, _ in stages)
    first = deepest + ways
    turns = (count - int(short_last) - first) // ways

    def peeled(r):
        for lag, step in stages:
            g = r - lag
            if 0 <= g < count:
                step(g, g // ways, g % ways, short_last and g == count - 1)

    for r in range(first):
        peeled(r)
    with eng.Fori(0, turns) as i:
        for u in range(ways):
            for lag, step in stages:
                b = first + u - lag
                step(i * ways + b, i + b // ways, b % ways, False)
    for r in range(first + ways * turns, count + deepest):
        peeled(r)


def wait_apart(eng, sem, value):
    wait(eng, sem, value)
    if not isinstance(value, int):
        eng.nop(nofuse=True)


def tiles_of(last):
    return [(0, REST)] if last else [(t, P) for t in range(TILES)]


def width_of(last):
    return REST if last else GROUP


def rows(dram, g, last):
    if last:
        return dram[g * GROUP:g * GROUP + REST, :].rearrange("(t p) d -> p t d", t=1)
    return dram[bass.ds(g * GROUP, GROUP), :].rearrange("(t p) d -> p t d", p=P)


def part(tile, last):
    return tile[0:REST, 0:1, :] if last else tile[:, :, :]


class Core:

    BANK, INDEXED = 48, 10

    def __init__(self, nc):
        self.nc = nc
        self.sems = [nc.alloc_semaphore(name=f"phase_sem{i}") for i in range(self.BANK)]
        self.indexed = [nc.alloc_semaphore(name=f"indexed_sem{i}") for i in range(self.INDEXED)]
        self.phases = 0

    @contextmanager
    def phase(self, name, sem_names):
        names = sem_names.split()
        own = [n for n in names if not n.startswith("sw")]
        indexed = [n for n in names if n.startswith("sw")]
        assert len(own) <= self.BANK and len(indexed) <= self.INDEXED and len(set(names)) == len(names), name
        sems = {**dict(zip(own, self.sems)), **dict(zip(indexed, self.indexed))}
        self.phases += 1
        name = f"{name}{self.phases}"
        with ExitStack() as memory:
            def sbuf(n, shape, dt=F32):
                return memory.enter_context(self.nc.sbuf_tensor(f"{name}_{n}", shape, dt))

            def psum(n, shape, dt=F32):
                return memory.enter_context(self.nc.psum_tensor(f"{name}_{n}", shape, dt))

            yield sems, sbuf, psum
            self.nc.all_engine_barrier()
            if indexed:
                nums = [sems[n].num for n in indexed]
                self.nc.gpsimd.dma_reset(range(min(nums), max(nums) + 1))
            for n in names:
                self.nc.gpsimd.sem_clear(sems[n])
            self.nc.all_engine_barrier()


def norm_phase(core, src, dst, half):
    nc = core.nc
    W = 4
    with core.phase("norm", "ld0 ld1 ld2 ld3 stats aggr var rstd norm st0 st1 st2 st3") as (s, sbuf, psum):
        x = [sbuf(f"x{q}", [P, TILES, D]) for q in range(W)]
        y = [sbuf(f"y{q}", [P, TILES, D]) for q in range(W)]
        bn = [sbuf(f"bn{q}", [P, TILES, 6]) for q in range(W)]
        mv = [sbuf(f"mv{q}", [P, TILES, 2]) for q in range(W)]
        rs = [sbuf(f"rs{q}", [P, TILES]) for q in range(W)]
        ld, st = [s[f"ld{q}"] for q in range(W)], [s[f"st{q}"] for q in range(W)]
        with nc.Block() as block:
            @block.sync
            def _(eng):
                def load(g, h, q, last):
                    wait(eng, s["norm"], g - W + 1)
                    eng.dma_start(part(x[q], last), rows(src, g, last)).then_inc(ld[q], 16)
                pipeline(eng, [(0, load)], ways=W)

            @block.vector
            def _(eng):
                def stats(g, h, q, last):
                    eng.wait_ge(ld[q], (h + 1) * 16)
                    row_stats(eng, s, g, x[q], bn[q], mv[q], last)

                def norm(g, h, q, last):
                    eng.wait_ge(s["rstd"], g + 1)
                    wait(eng, st[q], h * 16)
                    row_norm(eng, x[q], y[q], mv[q], rs[q], last).then_inc(s["norm"], 1)
                pipeline(eng, [(0, stats), (1, norm)], ways=W)

            @block.gpsimd
            def _(eng):
                pipeline(eng, [(0, lambda g, h, q, last: row_rstd(eng, s, g, mv[q], half, rs[q], last))], ways=W)

            @block.scalar
            def _(eng):
                def store(g, h, q, last):
                    eng.wait_ge(s["norm"], g + 1)
                    eng.dma_start(rows(dst, g, last), part(y[q], last)).then_inc(st[q], 16)
                pipeline(eng, [(0, store)], ways=W)
                for q in range(W):
                    eng.wait_ge(st[q], 16 * (NG // W))


def row_norm(eng, x, y, mv, rs, last):
    for t, n in tiles_of(last):
        done = eng.tensor_scalar(y[0:n, t, :], x[0:n, t, :], mv[0:n, t, 0:1], rs[0:n, t:t + 1],
                                 ALU.subtract, ALU.mult)
    return done


def row_stats(eng, s, g, x, bn, mv, last, negated=None):
    for t, n in tiles_of(last):
        done = eng.bn_stats(bn[0:n, t, :], x[0:n, t, :])
    done.then_inc(s["stats"], 1)
    wait_apart(eng, s["stats"], g + 1)
    for t, n in tiles_of(last):
        done = eng.bn_aggr(mv[0:n, t, :], bn[0:n, t, :])
    done.then_inc(s["aggr"], 1)
    eng.wait_ge(s["aggr"], g + 1)
    n = REST if last else P
    k = 1 if last else TILES
    if negated is not None:
        eng.tensor_scalar(negated[0:n, 0:k], mv[0:n, 0:k, 0], -1.0, None, ALU.mult)
    eng.tensor_scalar(mv[0:n, 0:k, 1], mv[0:n, 0:k, 1], EPS, None, ALU.add).then_inc(s["var"], 1)


def row_rstd(eng, s, g, mv, half, rs, last):
    eng.wait_ge(s["var"], g + 1)
    n = REST if last else P
    k = 1 if last else TILES
    eng.tensor_tensor(rs[0:n, 0:k], mv[0:n, 0:k, 1], half[0:n, 0:k], ALU.pow).then_inc(s["rstd"], 1)


HI = 80
KEYS = 2
PAD_NODE = N
ROWS = NG * GROUP


def ds1(i):
    return slice(i, i + 1) if isinstance(i, int) else bass.ds(i, 1)


class Edges:

    def __init__(self, nc):
        def sbuf(n, dt=F32):
            return [nc.alloc_sbuf_tensor(f"edge_{n}{k}", [P, ET], dt) for k in range(KEYS)]

        self.key, self.carried, self.kind, self.weight = sbuf("key"), sbuf("carried"), sbuf("kind"), sbuf("weight")
        self.partner, self.target = sbuf("partner", U32), sbuf("target", U32)
        self.table = [nc.dram_tensor(f"edge_table{k}", (EP, 4), F32).ap() for k in range(KEYS)]
        self.key_row = [nc.dram_tensor(f"edge_key_row{k}", (EP + P,), F32).ap() for k in range(KEYS)]
        self.weight_row = nc.dram_tensor("edge_weight_row", (EP,), F32).ap()
        self.sums = [nc.dram_tensor(f"edge_sums{k}", (ROWS, D), F32).ap() for k in range(KEYS)]
        self.routed = nc.dram_tensor("routed", (ROWS, D), F32).ap()


def order_phase(core, ed, cst, src, dst, kind, weight):
    nc = core.nc
    W = 4
    names = ("ints rows colf hilo shift keyrow hirow hot hist histc scan roll off base put "
             "count look bsb ohT val rank made zero zdone fin1 fin2 fin3 wide "
             "pk0 pk1 pk2 pk3 sw0 sw1 sw2 sw3 sw4 sw5 sw6 sw7")
    with core.phase("order", names) as (s, sbuf, psum):
        load_i = sbuf("load_i", [P, 5, ET], I32)
        col = sbuf("col", [P, 5, ET])
        hl_i = sbuf("hl_i", [P, KEYS, 2, ET], I32)
        hl = sbuf("hl", [P, KEYS, 2, ET])
        wt = sbuf("wt", [P, ET])
        packed = sbuf("packed", [P, KEYS, ET, 4])
        row_i = [sbuf(f"row_i{k}", [P, EP], I32) for k in range(KEYS)]
        key_row = [sbuf(f"key_row{k}", [P, EP]) for k in range(KEYS)]
        hi_row = [sbuf(f"hi_row{k}", [HI, EP]) for k in range(KEYS)]
        hot_hi = [sbuf(f"hot_hi{k}", [P, ET, HI], BF16) for k in range(KEYS)]
        hot_lo = [sbuf(f"hot_lo{k}", [P, ET, P], BF16) for k in range(KEYS)]
        cnt = sbuf("cnt", [HI, KEYS, P])
        incl = sbuf("incl", [HI, KEYS, P])
        ohT = [sbuf(f"ohT{q}", [HI, KEYS, P]) for q in range(2)]
        place = [sbuf(f"place{q}", [HI, KEYS, P]) for q in range(2)]
        junk = [sbuf(f"junk{q}", [P, KEYS, 2, P]) for q in range(2)]
        part_n = [sbuf(f"part_n{q}", [P, KEYS, 2]) for q in range(2)]
        rank = sbuf("rank", [P, KEYS, ET])
        rank_i = sbuf("rank_i", [P, KEYS, ET], I32)
        rr_i = sbuf("rr_i", [P, 2, KEYS, ET], I32)
        rr = sbuf("rr", [P, 2, KEYS, ET])
        slot = sbuf("slot", [P, KEYS, ET], U32)
        pk = [sbuf(f"pk{q}", [P, KEYS, 4]) for q in range(W)]
        ix = [sbuf(f"ix{q}", [P, KEYS], U32) for q in range(W)]
        zeros = sbuf("zeros", [P, 2, D])
        tab = sbuf("tab", [P, KEYS, ET, 4])
        lineT = sbuf("lineT", [ET, KEYS + 1, P])
        nextT = sbuf("nextT", [ET, KEYS, P])
        same = sbuf("same", [P, KEYS, ET])
        minus = sbuf("minus", [1, P])
        h_ps = psum("h_ps", [HI, KEYS, P])
        o_ps = psum("o_ps", [HI, KEYS])
        c_ps = [psum(f"c_ps{q}", [HI, KEYS, P]) for q in range(2)]
        l_ps = [psum(f"l_ps{q}", [P, KEYS, P]) for q in range(2)]
        t_ps = psum("t_ps", [P, 3, P])
        key_in = (src, dst)
        pk_s, sc_s = [s[f"pk{q}"] for q in range(W)], [[s[f"sw{q * KEYS + k}"] for k in range(KEYS)] for q in range(W)]
        USED = E // ET
        assert USED * ET == E

        with nc.Block() as block:
            @block.gpsimd
            def _(eng):
                eng.memset(load_i[:, 0:2, :], PAD_NODE)
                eng.memset(load_i[:, 2, :], RELATIONS)
                eng.memset(load_i[:, 3:5, :], 0)
                eng.memset(wt[:, :], 0.0)
                for k in range(KEYS):
                    eng.memset(row_i[k][:, E:EP], PAD_NODE)
                eng.memset(minus[:, :], -1.0)
                eng.memset(zeros[:, :, :], 0.0).then_inc(s["made"], 1)

                def scatter(t, h, q, last):
                    wait_apart(eng, pk_s[q], h + 1)
                    for k in range(KEYS):
                        eng.indirect_dma_start(ed.table[k], bass.IndirectOffsetOnAxis(ap=ix[q][:, k:k + 1], axis=0),
                                               pk[q][:, k, :], None).then_inc(sc_s[q][k], 16)
                pipeline(eng, [(0, scatter)], count=ET, short_last=False, ways=W)

            @block.sync
            def _(eng):
                eng.wait_ge(s["made"], 1)
                for j, a in enumerate((src, dst, kind, src, dst)):
                    eng.dma_start(load_i[0:USED, j, :], a.rearrange("(p t) -> p t", t=ET)).then_inc(s["ints"], 16)
                eng.dma_start(wt[0:USED, :], weight.rearrange("(p t) one -> p (t one)", t=ET)).then_inc(s["ints"], 16)
                for k in range(KEYS):
                    eng.dma_start(row_i[k][:, 0:E], key_in[k].partition_broadcast(P)).then_inc(s["rows"], 16)
                for k in range(KEYS):
                    eng.dma_start(ed.key_row[k].rearrange("(a n) -> a n", a=1)[:, EP:EP + P], minus[:, :]).then_inc(s["fin1"], 16)

                def clear(g, h, q, last):
                    for sums in (*ed.sums, ed.routed):
                        eng.dma_start(sums[bass.ds(g * GROUP, GROUP), :].rearrange("(t p) d -> p t d", p=P),
                                      zeros[:, :, :]).then_inc(s["zdone"], 16)
                with eng.Fori(0, NG) as g:
                    clear(g, 0, 0, False)
                for q in range(W):
                    for k in range(KEYS):
                        eng.wait_ge(sc_s[q][k], 16 * (ET // W))
                for k in range(KEYS):
                    eng.dma_start(tab[:, k, :, :], ed.table[k].rearrange("(p t) c -> p t c", t=ET)).then_inc(s["fin2"], 16)
                eng.wait_ge(s["wide"], 1)
                for k in range(KEYS):
                    eng.dma_start(ed.key_row[k].rearrange("(t p) -> t p", p=P)[0:ET, :], lineT[:, k, :]).then_inc(s["fin1"], 16)
                eng.dma_start(ed.weight_row.rearrange("(t p) -> t p", p=P), lineT[:, KEYS, :]).then_inc(s["fin1"], 16)
                eng.wait_ge(s["fin1"], 16 * (2 * KEYS + 1))
                for k in range(KEYS):
                    eng.dma_start(nextT[:, k, :], ed.key_row[k][1:EP + 1].rearrange("(t p) -> t p", p=P)).then_inc(s["fin3"], 16)
                eng.wait_ge(s["zdone"], 16 * (KEYS + 1) * NG)

            @block.vector
            def _(eng):
                eng.wait_ge(s["ints"], 96)
                eng.tensor_copy(col[:, :, :], load_i[:, :, :]).then_inc(s["colf"], 1)
                for k in range(KEYS):
                    eng.tensor_scalar(hl_i[:, k, 0, :], load_i[:, k, :], 7, None, ALU.logical_shift_right)
                    m = eng.tensor_scalar(hl_i[:, k, 1, :], load_i[:, k, :], P - 1, None, ALU.bitwise_and)
                m.then_inc(s["hilo"], 1)
                eng.wait_ge(s["hilo"], 1)
                eng.tensor_copy(hl[:, :, :, :], hl_i[:, :, :, :]).then_inc(s["hilo"], 1)
                eng.wait_ge(s["hilo"], 2)
                for k in range(KEYS):
                    for t0 in range(0, ET, ET // 2):
                        ts = slice(t0, t0 + ET // 2)
                        for hot, part_, w in ((hot_hi, 0, HI), (hot_lo, 1, P)):
                            m = eng.tensor_tensor(hot[k][:, ts, :], cst.iota[:, 0:w].unsqueeze(1).to_broadcast([P, ET // 2, w]),
                                                  hl[:, k, part_, ts].unsqueeze(2).to_broadcast([P, ET // 2, w]), ALU.is_equal)
                m.then_inc(s["hot"], 1)
                for k in range(KEYS):
                    for c, j in ((0, k), (1, 4 - k), (2, 2)):
                        eng.tensor_copy(packed[:, k, :, c], col[:, j, :])
                    eng.tensor_copy(packed[:, k, :, 3], wt[:, :])
                eng.wait_ge(s["rows"], 32)
                for k in range(KEYS):
                    eng.tensor_copy(key_row[k][:, :], row_i[k][:, :]).then_inc(s["keyrow"], 1)
                eng.wait_ge(s["keyrow"], 2)
                for k in range(KEYS):
                    eng.tensor_scalar(row_i[k][0:HI, :], row_i[k][0:HI, :], 7, None, ALU.logical_shift_right).then_inc(s["shift"], 1)
                    eng.wait_ge(s["shift"], k + 1)
                    eng.tensor_copy(hi_row[k][:, :], row_i[k][0:HI, :]).then_inc(s["hirow"], 1)
                eng.wait_ge(s["hist"], 1)
                eng.tensor_copy(cnt[:, :, :], h_ps[:, :, :]).then_inc(s["histc"], 1)
                eng.wait_ge(s["histc"], 1)
                for k in range(KEYS):
                    m = eng.tensor_tensor_scan(incl[:, k, :], cnt[:, k, :], cnt[:, k, :], 0.0, ALU.add, ALU.bypass)
                m.then_inc(s["scan"], 1)
                eng.wait_ge(s["scan"], 1)
                eng.wait_ge(s["off"], 1)
                eng.tensor_tensor(incl[:, :, :], incl[:, :, :], cnt[:, :, :], ALU.subtract).then_inc(s["base"], 1)
                eng.wait_ge(s["base"], 1)
                eng.tensor_tensor(place[0][:, :, :], incl[:, :, :], o_ps[:, :].unsqueeze(2).to_broadcast([HI, KEYS, P]),
                                  ALU.add).then_inc(s["put"], 1)
                eng.wait_ge(s["hirow"], 2)

                def columns(t, k):
                    return key_row[k].ap().rearrange("a (p t) -> a t p", t=ET)[:, ds1(t), :].rearrange("a one p -> a (one p)")

                def spread(t, h, q, last):
                    wait(eng, s["look"], t - 1)
                    for k in range(KEYS):
                        v = hi_row[k].ap().rearrange("a (p t) -> a t p", t=ET)[:, ds1(t), :].rearrange("a one p -> a (one p)")
                        m = eng.tensor_scalar(ohT[q][:, k, :], v, cst.index[0:HI, :], None, ALU.is_equal)
                    m.then_inc(s["ohT"], 1)

                def ranks(t, h, q, last):
                    eng.wait_ge(s["look"], t + 1)
                    for k in range(KEYS):
                        eng.scalar_tensor_tensor(junk[q][:, k, 0, :], l_ps[q][:, k, :], 1.0,
                                                 hot_lo[k].ap()[:, ds1(t), :].rearrange("a one p -> a (one p)"),
                                                 ALU.mult, ALU.mult, accum_out=part_n[q][:, k, 0:1])
                        m = eng.scalar_tensor_tensor(junk[q][:, k, 1, :], columns(t, k), col[:, k, ds1(t)], cst.before[:, :],
                                                     ALU.is_equal, ALU.mult, accum_out=part_n[q][:, k, 1:2])
                    m.then_inc(s["val"], 1)
                    eng.wait_ge(s["put"], t + 1)
                    eng.tensor_tensor(place[1 - q][:, :, :], place[q][:, :, :], c_ps[q][:, :, :], ALU.add).then_inc(s["put"], 1)
                    eng.wait_ge(s["val"], t + 1)
                    eng.tensor_tensor(rank[:, :, ds1(t)], part_n[q][:, :, 0:1], part_n[q][:, :, 1:2], ALU.add).then_inc(s["rank"], 1)
                pipeline(eng, [(0, spread), (1, ranks)], count=ET, short_last=False)
                eng.wait_ge(s["rank"], ET)
                eng.tensor_copy(rank_i[:, :, :], rank[:, :, :]).then_inc(s["rank"], 1)
                eng.wait_ge(s["rank"], ET + 1)
                eng.tensor_scalar(rr_i[:, 0, :, :], rank_i[:, :, :], 7, None, ALU.logical_shift_right)
                eng.tensor_scalar(rr_i[:, 1, :, :], rank_i[:, :, :], P - 1, None, ALU.bitwise_and).then_inc(s["rank"], 1)
                eng.wait_ge(s["rank"], ET + 2)
                eng.tensor_copy(rr[:, :, :, :], rr_i[:, :, :, :]).then_inc(s["rank"], 1)
                eng.wait_ge(s["rank"], ET + 3)
                eng.scalar_tensor_tensor(slot[:, :, :], rr[:, 1, :, :], float(ET), rr[:, 0, :, :], ALU.mult, ALU.add).then_inc(s["rank"], 1)
                eng.wait_ge(s["rank"], ET + 4)

                def pack(t, h, q, last):
                    for k in range(KEYS):
                        wait(eng, sc_s[q][k], h * 16)
                    eng.tensor_copy(pk[q][:, :, :], packed[:, :, ds1(t), :].rearrange("a k one c -> a (k one) c"))
                    eng.tensor_copy(ix[q][:, :], slot[:, :, ds1(t)].rearrange("a k one -> a (k one)")).then_inc(pk_s[q], 1)
                pipeline(eng, [(0, pack)], count=ET, short_last=False, ways=W)
                eng.wait_ge(s["fin2"], 32)
                for k in range(KEYS):
                    for c, dst_ in enumerate((ed.key[k], ed.partner[k], ed.kind[k], ed.weight[k])):
                        m = eng.tensor_copy(dst_[:, :], tab[:, k, :, c])
                m.then_inc(s["count"], 1)
                eng.wait_ge(s["count"], 2)
                eng.tensor_copy(lineT[:, :, :], t_ps[0:ET, :, :]).then_inc(s["wide"], 1)
                for k in range(KEYS):
                    eng.memset(ed.carried[k][:, 0:1], 0.0)
                    m = eng.tensor_scalar(ed.carried[k][:, 1:ET], ed.key[k][:, 0:ET - 1], 1.0, cst.last_row[:, :], ALU.add, ALU.mult)
                m.then_inc(s["roll"], 1)
                eng.wait_ge(s["roll"], 1)
                for k in range(KEYS):
                    eng.tensor_scalar(ed.carried[k][:, :], ed.carried[k][:, :], -1.0, None, ALU.add)
                eng.wait_ge(s["count"], 3)
                for k in range(KEYS):
                    m = eng.tensor_tensor(same[:, k, :], ed.key[k][:, :], t_ps[:, k, 0:ET], ALU.is_equal)
                m.then_inc(s["roll"], 1)
                eng.wait_ge(s["roll"], 2)
                for k in range(KEYS):
                    eng.scalar_tensor_tensor(ed.target[k][:, :], same[:, k, :], NO_ROW, ed.key[k][:, :], ALU.mult, ALU.add)

            @block.tensor
            def _(eng):
                eng.wait_ge(s["hot"], 1)
                for k in range(KEYS):
                    def hist(t, start, stop):
                        return eng.matmul(h_ps[:, k, :], hot_hi[k].ap()[:, ds1(t), :].rearrange("a one p -> a (one p)"),
                                          hot_lo[k].ap()[:, ds1(t), :].rearrange("a one p -> a (one p)"), start=start, stop=stop)
                    hist(0, True, False)
                    with eng.Fori(1, ET - 1) as t:
                        hist(t, False, False)
                    m = hist(ET - 1, False, True)
                m.then_inc(s["hist"], 1)
                eng.wait_ge(s["scan"], 1)
                for k in range(KEYS):
                    m = eng.matmul(o_ps[:, k:k + 1], cst.after[0:HI, 0:HI], incl[:, k, P - 1:P], start=True, stop=True)
                m.then_inc(s["off"], 1)

                def look(t, h, q, last):
                    wait(eng, s["put"], t)
                    wait(eng, s["val"], t - 1)
                    for k in range(KEYS):
                        eng.matmul(c_ps[q][:, k, :], hot_hi[k].ap()[:, ds1(t), :].rearrange("a one p -> a (one p)"),
                                   hot_lo[k].ap()[:, ds1(t), :].rearrange("a one p -> a (one p)"), start=True, stop=True)
                    eng.wait_ge(s["ohT"], t + 1)
                    eng.wait_ge(s["put"], t + 1)
                    for k in range(KEYS):
                        m = eng.matmul(l_ps[q][:, k, :], ohT[q][:, k, :], place[q][:, k, :], start=True, stop=True)
                    m.then_inc(s["look"], 1)
                pipeline(eng, [(0, look)], count=ET, short_last=False)
                eng.wait_ge(s["count"], 1)
                for k in range(KEYS):
                    eng.transpose(t_ps[0:ET, k, :], ed.key[k][:, :], cst.ident[:, :])
                eng.transpose(t_ps[0:ET, KEYS, :], ed.weight[1][:, :], cst.ident[:, :]).then_inc(s["count"], 1)
                eng.wait_ge(s["fin3"], 32)
                eng.wait_ge(s["wide"], 1)
                for k in range(KEYS):
                    m = eng.transpose(t_ps[:, k, 0:ET], nextT[:, k, :], cst.ident[0:ET, 0:ET])
                m.then_inc(s["count"], 1)


class Constants:

    def __init__(self, core, early):
        nc = core.nc

        def early_sbuf(n, shape, dt=F32):
            return early.enter_context(nc.sbuf_tensor(f"cst_{n}", shape, dt))

        def sbuf(n, shape, dt=F32):
            return nc.alloc_sbuf_tensor(f"cst_{n}", shape, dt)

        self.half = sbuf("half", [P, KC])
        self.ident = sbuf("ident", [P, P])
        self.ident_b = sbuf("ident_b", [P, P], BF16)
        self.last_row = sbuf("last_row", [P, 1])
        self.iota = early_sbuf("iota", [P, P])
        self.index = early_sbuf("index", [P, 1])
        self.before = early_sbuf("before", [P, P])
        self.after = early_sbuf("after", [P, P])
        with core.phase("const", "a b") as (s, _, _), nc.Block() as block:
            @block.gpsimd
            def _(eng):
                eng.memset(self.half[:, :], -0.5)
                eng.iota(self.iota[:, :], [[1, P]], base=0, channel_multiplier=0, allow_small_or_imprecise_dtypes=True)
                eng.iota(self.index[:, :], [[1, 1]], base=0, channel_multiplier=1, allow_small_or_imprecise_dtypes=True).then_inc(s["a"], 1)

            @block.vector
            def _(eng):
                eng.wait_ge(s["a"], 1)
                for m, op in ((self.before, ALU.is_lt), (self.after, ALU.is_gt), (self.ident, ALU.is_equal),
                              (self.ident_b, ALU.is_equal)):
                    eng.tensor_scalar(m[:, :], self.iota[:, :], self.index[:, :], None, op)
                eng.tensor_scalar(self.last_row[:, :], self.index[:, :], float(P - 1), None, ALU.is_equal)


def split_phase(core, name, items):
    nc = core.nc
    with core.phase(name, "load hi lo") as (s, sbuf, _):
        stage = [sbuf(f"stage{j}", list(hi.shape)) for j, (_, hi, _) in enumerate(items)]
        with nc.Block() as block:
            @block.sync
            def _(eng):
                for st, (value, _, _) in zip(stage, items):
                    eng.dma_start(st.ap(), value).then_inc(s["load"], 16)

            @block.scalar
            def _(eng):
                eng.wait_ge(s["load"], 16 * len(items))
                for st, (_, hi, _) in zip(stage, items):
                    eng.activation(hi, st.ap(), ACT.Copy).then_inc(s["hi"], 1)

            @block.vector
            def _(eng):
                for j, (st, (_, hi, lo)) in enumerate(zip(stage, items)):
                    eng.wait_ge(s["hi"], j + 1)
                    eng.tensor_tensor(lo, st.ap(), hi.bitcast(F32), ALU.subtract)


def chunked(w):
    return w.rearrange("(c p) n -> p c n", p=P)


def combine_phase(core, cst, basis, att, w_hi, w_lo):
    nc = core.nc
    W = 4
    TE = KC - 1
    with core.phase("combine", "att ld0 ld1 ld2 ld3 diag te ve hi lo") as (s, sbuf, psum):
        b_t = [sbuf(f"basis{q}", [P, KC, D]) for q in range(W)]
        att_t = sbuf("att", [P, RELATIONS * BASES])
        diag = [sbuf(f"diag{q}", [P, P]) for q in range(W)]
        acc = sbuf("acc", [P, KC + 1, D])
        rest = psum("rest", [P, TE, D])
        ld = [s[f"ld{q}"] for q in range(W)]
        with nc.Block() as block:
            @block.sync
            def _(eng):
                eng.dma_start(att_t[:, :], att.rearrange("r b -> (r b)").partition_broadcast(P)).then_inc(s["att"], 16)

                def load(b, h, q, last):
                    wait(eng, s["te"], b - W + 1)
                    wait(eng, s["ve"], b - W + 1)
                    eng.dma_start(b_t[q][:, :, :], chunked(basis[ds1(b), :, :].rearrange("one i o -> (one i) o"))).then_inc(ld[q], 16)
                pipeline(eng, [(0, load)], count=BASES, short_last=False, ways=W)

            @block.scalar
            def _(eng):
                eng.wait_ge(s["att"], 16)

                def diagonal(b, h, q, last):
                    wait(eng, s["te"], b - W + 1)
                    a = BASES + b
                    eng.activation(diag[q][:, :], cst.ident[:, :], ACT.Copy, scale=att_t[:, ds1(a)]).then_inc(s["diag"], 1)
                pipeline(eng, [(0, diagonal)], count=BASES, short_last=False, ways=W)
                eng.wait_ge(s["ve"], BASES)
                eng.activation(w_hi[:, 0:KC, :], acc[:, 0:KC, :], ACT.Copy)
                eng.activation(w_hi[:, 2 * KC - 1, :], acc[:, KC, :], ACT.Copy)
                eng.wait_ge(s["te"], BASES)
                eng.activation(w_hi[:, KC:KC + TE, :], rest[:, :, :], ACT.Copy).then_inc(s["hi"], 1)

            @block.vector
            def _(eng):
                eng.memset(acc[:, :, :], 0.0).then_inc(s["lo"], 1)
                eng.wait_ge(s["lo"], 1)
                eng.wait_ge(s["att"], 16)

                def add(b, h, q, last):
                    eng.wait_ge(ld[q], (h + 1) * 16)
                    wait(eng, s["ve"], b)
                    eng.scalar_tensor_tensor(acc[:, 0:KC, :], b_t[q][:, :, :], att_t[:, ds1(b)], acc[:, 0:KC, :], ALU.mult, ALU.add)
                    a = BASES + b
                    eng.scalar_tensor_tensor(acc[:, KC, :], b_t[q][:, TE, :], att_t[:, ds1(a)], acc[:, KC, :],
                                             ALU.mult, ALU.add).then_inc(s["ve"], 1)
                pipeline(eng, [(0, add)], count=BASES, short_last=False, ways=W)
                eng.wait_ge(s["hi"], 1)
                eng.tensor_tensor(w_lo[:, 0:KC, :], acc[:, 0:KC, :], w_hi[:, 0:KC, :].bitcast(F32), ALU.subtract)
                eng.tensor_tensor(w_lo[:, 2 * KC - 1, :], acc[:, KC, :], w_hi[:, 2 * KC - 1, :].bitcast(F32), ALU.subtract)
                eng.tensor_tensor(w_lo[:, KC:KC + TE, :], rest[:, :, :], w_hi[:, KC:KC + TE, :].bitcast(F32), ALU.subtract)

            @block.tensor
            def _(eng):
                def term(b, h, q, last):
                    eng.wait_ge(ld[q], (h + 1) * 16)
                    eng.wait_ge(s["diag"], b + 1)
                    for c in range(TE):
                        m = eng.matmul(rest[:, c, :], diag[q][:, :], b_t[q][:, c, :],
                                       start=isinstance(b, int) and b == 0, stop=isinstance(b, int) and b == BASES - 1)
                    m.then_inc(s["te"], 1)
                pipeline(eng, [(0, term)], count=BASES, short_last=False, ways=W)


def three(eng, out, a_hi, a_lo, b_hi, b_lo, start, stop):
    eng.matmul(out, a_hi, b_hi, start=start, stop=False)
    eng.matmul(out, a_lo, b_hi, start=False, stop=False)
    return eng.matmul(out, a_hi, b_lo, start=False, stop=stop)


def relation_phase(core, cst, ed, table, gate_w, w_hi, w_lo):
    nc = core.nc
    W = 4
    names = ("gw krow mask hk hix ends ix swg0 swg1 swg2 swg3 z sig copy lo coef ch sel A pth ptl B res tix hd H hres "
             "sws0 sws1 sws2 sws3")
    with core.phase("relation", names) as (s, sbuf, psum):
        gw = sbuf("gw", [P, RELATIONS, D])
        krow = sbuf("krow", [P, EP])
        mask = sbuf("mask", [P, RELATIONS, ET])
        ix = [sbuf(f"ix{q}", [P, 1], U32) for q in range(W)]
        tix = [sbuf(f"tix{q}", [P, 1], U32) for q in range(W)]
        x = [sbuf(f"x{q}", [P, D]) for q in range(W)]
        xh = [sbuf(f"xh{q}", [P, D], F32R) for q in range(W)]
        xl = [sbuf(f"xl{q}", [P, D], F32R) for q in range(W)]
        junk = [sbuf(f"junk{q}", [P, RELATIONS, D]) for q in range(W)]
        z = [sbuf(f"z{q}", [P, RELATIONS]) for q in range(W)]
        sig = [sbuf(f"sig{q}", [P, RELATIONS]) for q in range(W)]
        cf = [sbuf(f"cf{q}", [P, RELATIONS]) for q in range(W)]
        ch = [sbuf(f"ch{q}", [P, RELATIONS], F32R) for q in range(W)]
        cl = [sbuf(f"cl{q}", [P, RELATIONS]) for q in range(W)]
        sh = [sbuf(f"sh{q}", [P, RELATIONS, P], F32R) for q in range(W)]
        sl = [sbuf(f"sl{q}", [P, RELATIONS, P], F32R) for q in range(W)]
        hd = [sbuf(f"hd{q}", [P, ET]) for q in range(W)]
        ends = sbuf("ends", [P, ET])
        hkey = sbuf("hkey", [ET, 2])
        hsame = sbuf("hsame", [ET, 1])
        hix = sbuf("hix", [ET, 1], U32)
        hres = sbuf("hres", [ET, D])
        pth = [sbuf(f"pth{q}", [P, KC, RELATIONS, P], F32R) for q in range(2)]
        ptl = [sbuf(f"ptl{q}", [P, KC, RELATIONS, P], F32R) for q in range(2)]
        res = [sbuf(f"res{q}", [P, D]) for q in range(W)]
        A = [psum(f"A{q}", [P, KC, RELATIONS, P]) for q in range(2)]
        B = [psum(f"B{q}", [P, D]) for q in range(2)]
        H = psum("H", [ET, D])
        heads = krow.ap().rearrange("a (t p) -> a p t", p=P)[:, 0, :]
        ga, sc = [s[f"swg{q}"] for q in range(W)], [s[f"sws{q}"] for q in range(W)]

        def run(eng, *stages):
            pipeline(eng, stages, count=ET, short_last=False, ways=W)

        with nc.Block() as block:
            @block.sync
            def _(eng):
                eng.dma_start(krow[:, :], ed.key_row[0][0:EP].partition_broadcast(P)).then_inc(s["krow"], 16)
                eng.dma_start(gw[:, :, :], gate_w.rearrange("r i one -> (r i one)").partition_broadcast(P)
                              .rearrange("a (r i) -> a r i", r=RELATIONS)).then_inc(s["gw"], 16)
                for j in range(2):
                    eng.dma_start(hkey[:, j:j + 1], ed.key_row[0][j * P:j * P + EP].rearrange("(t p) -> t p", p=P)[:, 0:1],
                                  allow_slow_non_contiguous=True).then_inc(s["hk"], 16)

            @block.gpsimd
            def _(eng):
                def gather(t, h, q, last):
                    wait(eng, s["lo"], t - W + 1)
                    wait(eng, s["z"], t - W + 1)
                    wait_apart(eng, s["ix"], t + 1)
                    eng.indirect_dma_start(x[q][:, :], None, table, bass.IndirectOffsetOnAxis(ap=ix[q][:, :], axis=0)).then_inc(ga[q], 16)

                def scatter(t, h, q, last):
                    eng.wait_ge(s["tix"], t + 1)
                    wait_apart(eng, s["res"], t + 1)
                    eng.indirect_dma_start(ed.sums[0], bass.IndirectOffsetOnAxis(ap=tix[q][:, :], axis=0), res[q][:, :], None,
                                           bounds_check=ROWS - 1, oob_is_err=False).then_inc(sc[q], 16)
                run(eng, (0, gather), (4, scatter))
                for q in range(W):
                    eng.wait_ge(sc[q], 16 * (ET // W))
                eng.wait_ge(s["hres"], 1)
                eng.indirect_dma_start(ed.sums[0], bass.IndirectOffsetOnAxis(ap=hix[:, :], axis=0), hres[:, :], None,
                                       bounds_check=ROWS - 1, oob_is_err=False).then_inc(sc[0], 16)
                eng.wait_ge(sc[0], 16 * (ET // W) + 16)

            @block.vector
            def _(eng):
                for r in range(RELATIONS):
                    if r == 0:
                        m = eng.tensor_scalar(mask[:, 0, :], ed.kind[0][:, :], 0.0, None, ALU.is_equal)
                    else:
                        m = eng.tensor_scalar(mask[:, 1, :], ed.kind[0][:, :], 0.0, None, ALU.not_equal)
                m.then_inc(s["mask"], 1)
                eng.wait_ge(s["hk"], 32)
                eng.tensor_tensor(hsame[:, :], hkey[:, 0:1], hkey[:, 1:2], ALU.is_equal).then_inc(s["hix"], 1)
                eng.wait_ge(s["hix"], 1)
                eng.scalar_tensor_tensor(hix[:, :], hsame[:, :], NO_ROW, hkey[:, 0:1], ALU.mult, ALU.add).then_inc(s["hix"], 1)
                eng.tensor_scalar(ends[:, :], ed.target[0][:, :], NO_ROW, cst.last_row[:, :], ALU.is_lt, ALU.max).then_inc(s["ends"], 1)

                def index(t, h, q, last):
                    wait(eng, ga[q], h * 16)
                    eng.tensor_copy(ix[q][:, :], ed.partner[0][:, ds1(t)]).then_inc(s["ix"], 1)

                def gates(t, h, q, last):
                    eng.wait_ge(ga[q], (h + 1) * 16)
                    wait(eng, s["sig"], t - W + 1)
                    for r in range(RELATIONS):
                        m = eng.scalar_tensor_tensor(junk[q][:, r, :], x[q][:, :], 1.0, gw[:, r, :], ALU.mult, ALU.mult,
                                                     accum_out=z[q][:, r:r + 1])
                    m.then_inc(s["z"], 1)
                    eng.wait_ge(s["copy"], t + 1)
                    wait(eng, s["A"], t - W + 1)
                    eng.tensor_tensor(xl[q][:, :], x[q][:, :], xh[q][:, :].bitcast(F32), ALU.subtract).then_inc(s["lo"], 1)

                def select(t, h, q, last):
                    eng.wait_ge(s["sig"], t + 1)
                    eng.tensor_tensor(cf[q][:, :], sig[q][:, :], mask[:, :, ds1(t)].rearrange("a r one -> a (r one)"),
                                      ALU.mult).then_inc(s["coef"], 1)
                    wait(eng, s["H"], t - W + 1)
                    eng.tensor_scalar(hd[q][:, :], heads, ed.key[0][:, ds1(t)], ends[:, ds1(t)], ALU.is_equal, ALU.mult).then_inc(s["hd"], 1)
                    wait(eng, sc[q], h * 16)
                    eng.tensor_copy(tix[q][:, :], ed.target[0][:, ds1(t)]).then_inc(s["tix"], 1)
                    eng.wait_ge(s["coef"], t + 1)
                    eng.tensor_copy(ch[q][:, :], cf[q][:, :]).then_inc(s["ch"], 1)
                    eng.wait_ge(s["ch"], t * 2 + 1)
                    eng.tensor_tensor(cl[q][:, :], cf[q][:, :], ch[q][:, :].bitcast(F32), ALU.subtract).then_inc(s["ch"], 1)
                    eng.wait_ge(s["ch"], t * 2 + 2)
                    for r in range(RELATIONS):
                        eng.tensor_scalar(sh[q][:, r, :], krow[:, bass.ts(t, P)], ed.key[0][:, ds1(t)],
                                          ch[q][:, r:r + 1].bitcast(F32), ALU.is_equal, ALU.mult)
                        m = eng.tensor_scalar(sl[q][:, r, :], krow[:, bass.ts(t, P)], ed.key[0][:, ds1(t)],
                                              cl[q][:, r:r + 1], ALU.is_equal, ALU.mult)
                    m.then_inc(s["sel"], 1)

                def low(t, h, q, last):
                    eng.wait_ge(s["pth"], t + 1)
                    eng.tensor_tensor(ptl[q % 2][:, :, :, :], A[q % 2][:, :, :, :], pth[q % 2][:, :, :, :].bitcast(F32),
                                      ALU.subtract).then_inc(s["ptl"], 1)
                eng.wait_ge(s["krow"], 16)
                eng.wait_ge(s["gw"], 16)
                eng.wait_ge(s["mask"], 1)
                eng.wait_ge(s["ends"], 1)
                run(eng, (0, index), (1, gates), (2, select), (3, low))
                eng.wait_ge(s["H"], ET)
                eng.wait_ge(s["hix"], 2)
                eng.tensor_copy(hres[:, :], H[:, :]).then_inc(s["hres"], 1)

            @block.scalar
            def _(eng):
                def copy(t, h, q, last):
                    eng.wait_ge(ga[q], (h + 1) * 16)
                    wait(eng, s["A"], t - W + 1)
                    eng.activation(xh[q][:, :], x[q][:, :], ACT.Copy).then_inc(s["copy"], 1)
                    eng.wait_ge(s["z"], t + 1)
                    wait(eng, s["coef"], t - W + 1)
                    eng.activation(sig[q][:, :], z[q][:, :], ACT.Sigmoid).then_inc(s["sig"], 1)

                def high(t, h, q, last):
                    eng.wait_ge(s["A"], t + 1)
                    wait(eng, s["B"], t - 1)
                    eng.activation(pth[q % 2][:, :, :, :], A[q % 2][:, :, :, :], ACT.Copy).then_inc(s["pth"], 1)

                def result(t, h, q, last):
                    eng.wait_ge(s["B"], t + 1)
                    wait(eng, sc[q], h * 16)
                    wait(eng, s["H"], t - W + 1)
                    eng.activation(res[q][:, :], B[q % 2][:, :], ACT.Copy).then_inc(s["res"], 1)
                run(eng, (1, copy), (3, high), (4, result))

            @block.tensor
            def _(eng):
                def sums(t, h, q, last):
                    eng.wait_ge(s["lo"], t + 1)
                    eng.wait_ge(s["sel"], t + 1)
                    wait(eng, s["ptl"], t - 1)
                    for c in range(KC):
                        cs = slice(c * P, (c + 1) * P)
                        m = three(eng, A[q % 2][:, c, :, :], xh[q][:, cs], xl[q][:, cs], sh[q][:, :, :], sl[q][:, :, :], True, True)
                    m.then_inc(s["A"], 1)

                def product(t, h, q, last):
                    eng.wait_ge(s["ptl"], t + 1)
                    wait(eng, s["res"], t - 1)
                    for r in range(RELATIONS):
                        for c in range(KC):
                            m = three(eng, B[q % 2][:, :], pth[q % 2][:, c, r, :], ptl[q % 2][:, c, r, :], w_hi[:, r * KC + c, :],
                                      w_lo[:, r * KC + c, :], r == 0 and c == 0, r == RELATIONS - 1 and c == KC - 1)
                    m.then_inc(s["B"], 1)

                def head(t, h, q, last):
                    eng.wait_ge(s["res"], t + 1)
                    eng.wait_ge(s["hd"], t + 1)
                    eng.matmul(H[:, :], hd[q][:, :], res[q][:, :], start=isinstance(t, int) and t == 0,
                               stop=isinstance(t, int) and t == ET - 1).then_inc(s["H"], 1)
                run(eng, (2, sums), (3, product), (4, head))


def root_phase(core, cst, ed, rows_in, root, bias, half, rows_out, skip=None, normed=None):
    nc = core.nc
    fin = skip is not None
    root_hi, root_lo = root
    names = ("bias ld0 ld1 la0 la1 lx0 lx1 T hi lo M pa pb pc y r st0 st1 sn0 sn1 stats aggr var rstd norm")
    with core.phase("root", names) as (s, sbuf, psum):
        bt = sbuf("bias", [P, D])
        xin = [sbuf(f"xin{q}", [P, TILES, D]) for q in range(2)]
        agg = [sbuf(f"agg{q}", [P, TILES, D]) for q in range(2)]
        skp = [sbuf(f"skp{q}", [P, TILES, D]) for q in range(2)] if fin else None
        xh = [sbuf(f"xh{q}", [P, KC, GROUP], F32R) for q in range(2)]
        xl = [sbuf(f"xl{q}", [P, KC, GROUP], F32R) for q in range(2)]
        y = [sbuf(f"y{q}", [P, TILES, D]) for q in range(2)]
        nrm = [sbuf(f"nrm{q}", [P, TILES, D]) for q in range(2)] if fin else None
        bn = [sbuf(f"bn{q}", [P, TILES, 6]) for q in range(2)]
        mv = [sbuf(f"mv{q}", [P, TILES, 2]) for q in range(2)]
        rs = [sbuf(f"rs{q}", [P, TILES]) for q in range(2)]
        T = [psum(f"T{q}", [P, KC, GROUP]) for q in range(2)]
        O = [psum(f"O{q}", [P, TILES, D]) for q in range(2)]
        ld, la, lx = (s["ld0"], s["ld1"]), (s["la0"], s["la1"]), (s["lx0"], s["lx1"])
        st, sn = (s["st0"], s["st1"]), (s["sn0"], s["sn1"])
        with nc.Block() as block:
            @block.sync
            def _(eng):
                eng.dma_start(bt[:, :], bias.partition_broadcast(P)).then_inc(s["bias"], 16)

                def load(g, h, q, last):
                    wait(eng, s["T"], g - 1)
                    eng.dma_start(part(xin[q], last), rows(rows_in, g, last)).then_inc(ld[q], 16)
                    wait(eng, s["y"], g - 1)
                    eng.dma_start(part(agg[q], last), rows(ed.sums[0], g, last)).then_inc(la[q], 16)
                    if fin:
                        eng.dma_start(part(skp[q], last), rows(skip, g, last)).then_inc(lx[q], 16)
                pipeline(eng, [(0, load)])

            @block.tensor
            def _(eng):
                root_T = lambda g, h, q, last: turn(eng, s, g, h, q, last, ld, xin, T, cst.ident)

                def product(g, h, q, last):
                    eng.wait_ge(s["lo"], g + 1)
                    wait(eng, s["y"], g - 1)
                    for t, n in tiles_of(last):
                        ts = slice(t * P, t * P + n)
                        for c in range(KC):
                            m = three(eng, O[q][0:n, t, :], xh[q][:, c, ts], xl[q][:, c, ts], root_hi[:, c, :], root_lo[:, c, :],
                                      c == 0, c == KC - 1)
                    m.then_inc(s["M"], 1)
                pipeline(eng, [(0, root_T), (1, product)])

            @block.gpsimd
            def _(eng):
                def add_bias(g, h, q, last):
                    n = REST if last else P
                    eng.wait_ge(la[q], (h + 1) * 16)
                    k = 1 if last else TILES
                    eng.tensor_tensor(agg[q][0:n, 0:k, :], agg[q][0:n, 0:k, :], bt[0:n, :].unsqueeze(1).to_broadcast([n, k, D]),
                                      ALU.add).then_inc(s["pa"], 1)
                    if fin:
                        eng.wait_ge(lx[q], (h + 1) * 16)
                        eng.wait_ge(s["pa"], g + 1)
                        eng.tensor_tensor(agg[q][0:n, 0:k, :], agg[q][0:n, 0:k, :], skp[q][0:n, 0:k, :], ALU.add).then_inc(s["pb"], 1)
                eng.wait_ge(s["bias"], 16)
                stages = [(0, add_bias)]
                if fin:
                    stages.append((2, lambda g, h, q, last: row_rstd(eng, s, g, mv[q], half, rs[q], last)))
                pipeline(eng, stages)

            @block.scalar
            def _(eng):
                def high(g, h, q, last):
                    split_hi(eng, s, g, q, last, T, xh)

                def finish(g, h, q, last):
                    eng.wait_ge(s["y"], g + 1)
                    if not fin:
                        eng.activation(part(y[q], last), part(y[q], last), ACT.Relu).then_inc(s["r"], 1)
                        eng.wait_ge(s["r"], g + 1)
                    eng.dma_start(rows(rows_out, g, last), part(y[q], last)).then_inc(st[q], 16)
                    if fin:
                        eng.wait_ge(s["norm"], g + 1)
                        eng.dma_start(rows(normed, g, last), part(nrm[q], last)).then_inc(sn[q], 16)
                pipeline(eng, [(0, high), (2, finish)])
                for q in range(2):
                    eng.wait_ge(st[q], 16 * (NG // 2))
                    if fin:
                        eng.wait_ge(sn[q], 16 * (NG // 2))

            @block.vector
            def _(eng):
                def low(g, h, q, last):
                    split_lo(eng, s, g, q, last, T, xh, xl)

                def total(g, h, q, last):
                    eng.wait_ge(s["M"], g + 1)
                    eng.wait_ge(s["pb" if fin else "pa"], g + 1)
                    wait(eng, st[q], h * 16)
                    if fin:
                        wait(eng, s["norm"], g - 1)
                    eng.tensor_tensor(part(y[q], last), part(O[q], last), part(agg[q], last), ALU.add).then_inc(s["y"], 1)
                    if fin:
                        eng.wait_ge(s["y"], g + 1)
                        row_stats(eng, s, g, y[q], bn[q], mv[q], last)

                def norm(g, h, q, last):
                    eng.wait_ge(s["rstd"], g + 1)
                    wait(eng, sn[q], h * 16)
                    row_norm(eng, y[q], nrm[q], mv[q], rs[q], last).then_inc(s["norm"], 1)
                pipeline(eng, [(0, low), (1, total)] + ([(2, norm)] if fin else []))


def turn(eng, s, g, h, q, last, ready, x, T, ident, value=None):
    if ready is None:
        eng.wait_ge(s["pre"], g + 1)
    else:
        eng.wait_ge(ready[q], (h + 1) * 16)
    wait(eng, s["lo"], g - 1)
    for t, n in tiles_of(last):
        for c in range(KC):
            m = eng.transpose(T[q][:, c, t * P:t * P + n], x[q][0:n, t, c * P:(c + 1) * P], ident[0:n, 0:n])
    m.then_inc(s["T"], 1)


def split_hi(eng, s, g, q, last, T, xh):
    w = width_of(last)
    eng.wait_ge(s["T"], g + 1)
    wait(eng, s["M"], g - 1)
    eng.activation(xh[q][:, :, 0:w], T[q][:, :, 0:w], ACT.Copy).then_inc(s["hi"], 1)


def split_lo(eng, s, g, q, last, T, xh, xl):
    w = width_of(last)
    eng.wait_ge(s["hi"], g + 1)
    eng.tensor_tensor(xl[q][:, :, 0:w], T[q][:, :, 0:w], xh[q][:, :, 0:w].bitcast(F32), ALU.subtract).then_inc(s["lo"], 1)


SUB = P // EXPERTS
LINE = N // SUB
TPE = 5
SL = CAP // TPE
ST = EXPERTS * TPE
BLOCK = 125
NB = N // BLOCK
BITS = 30


def route_phase(core, cst, rows_in, gate_w, probs):
    nc = core.nc
    names = "gw gwh gwl ld0 ld1 T hi lo M mx sub exp sum rec pr pt ptc st"
    with core.phase("route", names) as (s, sbuf, psum):
        gw = sbuf("gw", [P, KC, EXPERTS])
        gh = sbuf("gh", [P, KC, EXPERTS], F32R)
        gl = sbuf("gl", [P, KC, EXPERTS], F32R)
        xin = [sbuf(f"xin{q}", [P, TILES, D]) for q in range(2)]
        xh = [sbuf(f"xh{q}", [P, KC, GROUP], F32R) for q in range(2)]
        xl = [sbuf(f"xl{q}", [P, KC, GROUP], F32R) for q in range(2)]
        mx = [sbuf(f"mx{q}", [P, TILES]) for q in range(2)]
        sm = [sbuf(f"sm{q}", [P, TILES]) for q in range(2)]
        rc = [sbuf(f"rc{q}", [P, TILES]) for q in range(2)]
        lg = [sbuf(f"lg{q}", [P, TILES, EXPERTS]) for q in range(2)]
        ex = [sbuf(f"ex{q}", [P, TILES, EXPERTS]) for q in range(2)]
        pr = [sbuf(f"pr{q}", [P, TILES, EXPERTS]) for q in range(2)]
        pT = sbuf("pT", [EXPERTS, NG * GROUP])
        T = [psum(f"T{q}", [P, KC, GROUP]) for q in range(2)]
        L = [psum(f"L{q}", [P, TILES, EXPERTS]) for q in range(2)]
        Q = [psum(f"Q{q}", [EXPERTS, GROUP]) for q in range(2)]
        ld = (s["ld0"], s["ld1"])
        with nc.Block() as block:
            @block.sync
            def _(eng):
                eng.dma_start(gw[:, :, :], chunked(gate_w)).then_inc(s["gw"], 16)

                def load(g, h, q, last):
                    wait(eng, s["T"], g - 1)
                    eng.dma_start(part(xin[q], last), rows(rows_in, g, last)).then_inc(ld[q], 16)
                pipeline(eng, [(0, load)])
                eng.wait_ge(s["ptc"], NG)
                eng.dma_start(probs, pT[:, 0:N]).then_inc(s["st"], 16)
                eng.wait_ge(s["st"], 16)

            @block.tensor
            def _(eng):
                def product(g, h, q, last):
                    eng.wait_ge(s["lo"], g + 1)
                    wait(eng, s["sub"], g - 1)
                    for t, n in tiles_of(last):
                        ts = slice(t * P, t * P + n)
                        for c in range(KC):
                            m = three(eng, L[q][0:n, t, :], xh[q][:, c, ts], xl[q][:, c, ts], gh[:, c, :], gl[:, c, :],
                                      c == 0, c == KC - 1)
                    m.then_inc(s["M"], 1)

                def turn_probs(g, h, q, last):
                    eng.wait_ge(s["pr"], g + 1)
                    wait(eng, s["ptc"], g - 1)
                    for t, n in tiles_of(last):
                        m = eng.transpose(Q[q][:, t * P:t * P + n], pr[q][0:n, t, :], cst.ident[0:n, 0:n])
                    m.then_inc(s["pt"], 1)
                eng.wait_ge(s["gwl"], 1)
                pipeline(eng, [(0, lambda g, h, q, last: turn(eng, s, g, h, q, last, ld, xin, T, cst.ident)),
                               (1, product), (3, turn_probs)])

            @block.scalar
            def _(eng):
                eng.wait_ge(s["gw"], 16)
                eng.activation(gh[:, :, :], gw[:, :, :], ACT.Copy).then_inc(s["gwh"], 1)

                def exps(g, h, q, last):
                    n, k = (REST, 1) if last else (P, TILES)
                    eng.wait_ge(s["sub"], g + 1)
                    wait(eng, s["pr"], g - 1)
                    eng.activation(ex[q][0:n, 0:k, :], lg[q][0:n, 0:k, :], ACT.Exp).then_inc(s["exp"], 1)

                def out(g, h, q, last):
                    wait_apart(eng, s["pt"], g + 1)
                    w = width_of(last)
                    at = slice(g * GROUP, g * GROUP + w) if isinstance(g, int) else bass.ds(g * GROUP, w)
                    eng.activation(pT[:, at], Q[q][:, 0:w], ACT.Copy).then_inc(s["ptc"], 1)
                pipeline(eng, [(0, lambda g, h, q, last: split_hi(eng, s, g, q, last, T, xh)), (1, exps), (3, out)])

            @block.vector
            def _(eng):
                eng.wait_ge(s["gwh"], 1)
                eng.tensor_tensor(gl[:, :, :], gw[:, :, :], gh[:, :, :].bitcast(F32), ALU.subtract).then_inc(s["gwl"], 1)

                def shift(g, h, q, last):
                    n, k = (REST, 1) if last else (P, TILES)
                    eng.wait_ge(s["M"], g + 1)
                    eng.tensor_reduce(mx[q][0:n, 0:k], L[q][0:n, 0:k, :], AX.X, ALU.max).then_inc(s["mx"], 1)
                    eng.wait_ge(s["mx"], g + 1)
                    wait(eng, s["exp"], g - 1)
                    eng.tensor_tensor(lg[q][0:n, 0:k, :], L[q][0:n, 0:k, :], mx[q][0:n, 0:k].unsqueeze(2).to_broadcast([n, k, EXPERTS]),
                                      ALU.subtract).then_inc(s["sub"], 1)

                def divide(g, h, q, last):
                    n, k = (REST, 1) if last else (P, TILES)
                    eng.wait_ge(s["exp"], g + 1)
                    eng.tensor_reduce(sm[q][0:n, 0:k], ex[q][0:n, 0:k, :], AX.X, ALU.add).then_inc(s["sum"], 1)
                    eng.wait_ge(s["sum"], g + 1)
                    eng.reciprocal(rc[q][0:n, 0:k], sm[q][0:n, 0:k]).then_inc(s["rec"], 1)
                    eng.wait_ge(s["rec"], g + 1)
                    wait(eng, s["pt"], g - 1)
                    eng.tensor_tensor(pr[q][0:n, 0:k, :], ex[q][0:n, 0:k, :], rc[q][0:n, 0:k].unsqueeze(2).to_broadcast([n, k, EXPERTS]),
                                      ALU.mult).then_inc(s["pr"], 1)
                pipeline(eng, [(0, lambda g, h, q, last: split_lo(eng, s, g, q, last, T, xh, xl)), (1, shift), (2, divide)])


def select_phase(core, cst, probs, table, ends):
    nc = core.nc
    names = "ld blk ibit cand cnt tot keep th gt eq sc tg off need okr pick count val rank st one"
    with core.phase("select", names) as (s, sbuf, psum):
        p = sbuf("p", [P, LINE])
        same = sbuf("same", [P, P])
        prior = sbuf("prior", [P, P])
        grp = sbuf("grp", [P, P])
        grp_i = sbuf("grp_i", [P, P], I32)
        own_i = sbuf("own_i", [P, 1], I32)
        own = sbuf("own", [P, 1])
        thr = [sbuf(f"thr{q}", [P, 1], I32) for q in range(2)]
        cand = [sbuf(f"cand{q}", [P, 1], I32) for q in range(2)]
        cnt = [sbuf(f"cnt{q}", [P, 1]) for q in range(2)]
        junk = [sbuf(f"junk{q}", [P, LINE]) for q in range(2)]
        gt = sbuf("gt", [P, LINE])
        eq = sbuf("eq", [P, LINE])
        scan = sbuf("scan", [P, LINE])
        need = sbuf("need", [P, 2])
        before = sbuf("before", [P, 1])
        last = sbuf("last", [P, LINE // BLOCK])
        two = sbuf("two", [P, 2])
        tot = [psum(f"tot{q}", [P, 1]) for q in range(2)]
        off = psum("off", [P, 2])
        sums = psum("sums", [P, 1])
        with nc.Block() as block:
            @block.sync
            def _(eng):
                eng.dma_start(p[:, :], probs.rearrange("e (k n) -> (e k) n", k=SUB)).then_inc(s["ld"], 16)
                lines = table.rearrange("(a b) w -> a b w", a=P)
                eng.wait_ge(s["val"], 1)
                eng.dma_start(lines[:, :, BLOCK:2 * BLOCK], eq.ap().rearrange("a (b n) -> a b n", n=BLOCK)).then_inc(s["st"], 16)
                eng.wait_ge(s["rank"], 1)
                eng.dma_start(lines[:, :, 0:BLOCK], scan.ap().rearrange("a (b n) -> a b n", n=BLOCK)).then_inc(s["st"], 16)
                eng.dma_start(ends.rearrange("(a b) -> a b", a=P), last[:, :]).then_inc(s["st"], 16)
                eng.wait_ge(s["st"], 48)

            @block.gpsimd
            def _(eng):
                eng.iota(grp_i[:, :], [[1, P]], base=0, channel_multiplier=0)
                eng.iota(own_i[:, :], [[1, 1]], base=0, channel_multiplier=1).then_inc(s["ibit"], 1)

            @block.tensor
            def _(eng):
                eng.wait_ge(s["blk"], 1)
                for b in range(BITS):
                    q = b % 2
                    eng.wait_ge(s["cnt"], b + 1)
                    eng.matmul(tot[q][:, :], same[:, :], cnt[q][:, :], start=True, stop=True).then_inc(s["tot"], 1)
                eng.wait_ge(s["tg"], 1)
                eng.matmul(sums[:, :], same[:, :], two[:, 0:1], start=True, stop=True)
                eng.matmul(off[:, 0:1], prior[:, :], two[:, 1:2], start=True, stop=True).then_inc(s["off"], 1)
                eng.wait_ge(s["tg"], 2)
                eng.matmul(off[:, 1:2], prior[:, :], two[:, 1:2], start=True, stop=True).then_inc(s["off"], 1)

            @block.vector
            def _(eng):
                eng.wait_ge(s["ibit"], 1)
                eng.tensor_scalar(grp_i[:, :], grp_i[:, :], 3, None, ALU.logical_shift_right)
                eng.tensor_scalar(own_i[:, :], own_i[:, :], 3, None, ALU.logical_shift_right)
                eng.memset(thr[0][:, :], 0).then_inc(s["one"], 1)
                eng.wait_ge(s["one"], 1)
                eng.tensor_copy(grp[:, :], grp_i[:, :])
                eng.tensor_copy(own[:, :], own_i[:, :]).then_inc(s["one"], 1)
                eng.wait_ge(s["one"], 2)
                eng.tensor_scalar(same[:, :], grp[:, :], own[:, :], None, ALU.is_equal).then_inc(s["one"], 1)
                eng.wait_ge(s["one"], 3)
                eng.tensor_tensor(prior[:, :], same[:, :], cst.after[:, :], ALU.mult).then_inc(s["blk"], 1)
                eng.wait_ge(s["ld"], 16)
                assert 1 << SUB.bit_length() - 1 == SUB == 8
                for b in range(BITS):
                    q = b % 2
                    wait(eng, s["th"], b)
                    eng.tensor_scalar(cand[q][:, :], thr[q][:, :], 1 << (BITS - 1 - b), None, ALU.bitwise_or).then_inc(s["cand"], 1)
                    eng.wait_ge(s["cand"], b + 1)
                    eng.tensor_scalar(junk[q][:, :], p[:, :], cand[q][:, :].bitcast(F32), 0.0, ALU.is_ge, ALU.add,
                                      accum_out=cnt[q][:, :]).then_inc(s["cnt"], 1)
                    eng.wait_ge(s["tot"], b + 1)
                    eng.scalar_tensor_tensor(two[:, 0:1], tot[q][:, :], float(CAP), cand[q][:, :].bitcast(F32),
                                             ALU.is_ge, ALU.mult).then_inc(s["keep"], 1)
                    eng.wait_ge(s["keep"], b + 1)
                    eng.tensor_tensor(thr[1 - q][:, :].bitcast(F32), two[:, 0:1], thr[q][:, :].bitcast(F32), ALU.max).then_inc(s["th"], 1)
                border = thr[BITS % 2][:, :].bitcast(F32)
                eng.wait_ge(s["th"], BITS)
                eng.tensor_scalar(gt[:, :], p[:, :], border, 0.0, ALU.is_gt, ALU.add, accum_out=two[:, 0:1])
                eng.tensor_scalar(eq[:, :], p[:, :], border, None, ALU.is_equal).then_inc(s["gt"], 1)
                eng.wait_ge(s["gt"], 1)
                eng.tensor_tensor_scan(scan[:, :], eq[:, :], eq[:, :], 0.0, ALU.add, ALU.bypass).then_inc(s["sc"], 1)
                eng.wait_ge(s["sc"], 1)
                eng.tensor_copy(two[:, 1:2], scan[:, LINE - 1:LINE]).then_inc(s["tg"], 1)
                eng.wait_ge(s["off"], 1)
                eng.tensor_scalar(need[:, 0:1], sums[:, :], -1.0, float(CAP), ALU.mult, ALU.add).then_inc(s["need"], 1)
                eng.wait_ge(s["need"], 1)
                eng.tensor_tensor(need[:, 1:2], need[:, 0:1], off[:, 0:1], ALU.subtract).then_inc(s["need"], 1)
                eng.wait_ge(s["need"], 2)
                eng.scalar_tensor_tensor(eq[:, :], scan[:, :], need[:, 1:2], eq[:, :], ALU.is_le, ALU.mult).then_inc(s["okr"], 1)
                eng.wait_ge(s["okr"], 1)
                eng.tensor_tensor(gt[:, :], gt[:, :], eq[:, :], ALU.add).then_inc(s["pick"], 1)
                eng.wait_ge(s["pick"], 1)
                eng.tensor_tensor_scan(scan[:, :], gt[:, :], gt[:, :], 0.0, ALU.add, ALU.bypass).then_inc(s["count"], 1)
                eng.tensor_tensor(eq[:, :], gt[:, :], p[:, :], ALU.mult).then_inc(s["val"], 1)
                eng.wait_ge(s["count"], 1)
                eng.tensor_copy(two[:, 1:2], scan[:, LINE - 1:LINE]).then_inc(s["tg"], 1)
                eng.wait_ge(s["off"], 2)
                eng.tensor_copy(before[:, :], off[:, 1:2]).then_inc(s["count"], 1)
                eng.wait_ge(s["count"], 2)
                eng.tensor_scalar(last[:, :], scan.ap().rearrange("a (b n) -> a n b", n=BLOCK)[:, BLOCK - 1, :], before[:, :], None, ALU.add).then_inc(s["count"], 1)
                eng.wait_ge(s["count"], 3)
                eng.tensor_scalar(scan[:, :], scan[:, :], before[:, :], None, ALU.add).then_inc(s["rank"], 1)


def slots_phase(core, table, ends, token, score):
    nc = core.nc
    W = 4
    names = "io r ends cmp blk row ix swr0 swr1 swr2 swr3 cnt put tok"
    with core.phase("slots", names) as (s, sbuf, psum):
        r_i = sbuf("r_i", [SL, ST], I32)
        r0 = sbuf("r0", [SL, ST])
        r1 = sbuf("r1", [SL, ST])
        row0_i = sbuf("row0_i", [SL, ST], I32)
        row0 = sbuf("row0", [SL, ST])
        end = sbuf("end", [SL, EXPERTS, NB])
        cmp = [sbuf(f"cmp{i}", [SL, EXPERTS, NB]) for i in range(TPE)]
        blk = sbuf("blk", [SL, EXPERTS, TPE])
        row = sbuf("row", [SL, ST], U32)
        ix = [sbuf(f"ix{q}", [SL, 1], U32) for q in range(W)]
        line = [sbuf(f"line{q}", [SL, 2 * BLOCK]) for q in range(W)]
        junk = [sbuf(f"junk{q}", [SL, 2, BLOCK]) for q in range(W)]
        found = [sbuf(f"found{q}", [SL, 2]) for q in range(W)]
        both = sbuf("both", [SL, 2, ST])
        ga = [s[f"swr{q}"] for q in range(W)]
        blk_flat = blk.ap().rearrange("a e i -> a (e i)")

        def run(eng, *stages):
            pipeline(eng, stages, count=ST, short_last=False, ways=W)

        with nc.Block() as block:
            @block.sync
            def _(eng):
                eng.dma_start(end[:, :, :], ends.partition_broadcast(SL).rearrange("a (e b) -> a e b", e=EXPERTS)).then_inc(s["ends"], 16)

            @block.gpsimd
            def _(eng):
                eng.iota(r_i[:, :], [[0, EXPERTS], [SL, TPE]], base=0, channel_multiplier=1)
                eng.iota(row0_i[:, :], [[NB, EXPERTS], [0, TPE]], base=0, channel_multiplier=0).then_inc(s["io"], 1)

                def gather(t, h, q, last):
                    wait(eng, s["cnt"], t - W + 1)
                    wait_apart(eng, s["ix"], t + 1)
                    eng.indirect_dma_start(line[q][:, :], None, table, bass.IndirectOffsetOnAxis(ap=ix[q][:, :], axis=0)).then_inc(ga[q], 16)
                run(eng, (0, gather))

            @block.vector
            def _(eng):
                eng.wait_ge(s["io"], 1)
                eng.tensor_copy(r0[:, :], r_i[:, :])
                eng.tensor_copy(row0[:, :], row0_i[:, :]).then_inc(s["r"], 1)
                eng.wait_ge(s["r"], 1)
                eng.tensor_scalar(r1[:, :], r0[:, :], 1.0, None, ALU.add).then_inc(s["r"], 1)
                eng.wait_ge(s["ends"], 16)
                for i in range(TPE):
                    eng.tensor_scalar(cmp[i][:, :, :], end[:, :, :], r0[:, i:i + 1], None, ALU.is_le).then_inc(s["cmp"], 1)
                for i in range(TPE):
                    eng.wait_ge(s["cmp"], i + 1)
                    m = eng.tensor_reduce(blk[:, :, i], cmp[i][:, :, :], AX.X, ALU.add)
                m.then_inc(s["blk"], 1)
                eng.wait_ge(s["blk"], 1)
                eng.tensor_tensor(row[:, :], blk_flat, row0[:, :], ALU.add).then_inc(s["row"], 1)
                eng.wait_ge(s["row"], 1)
                eng.wait_ge(s["r"], 2)

                def index(t, h, q, last):
                    wait(eng, ga[q], h * 16)
                    eng.tensor_copy(ix[q][:, :], row[:, ds1(t)]).then_inc(s["ix"], 1)

                def find(t, h, q, last):
                    eng.wait_ge(ga[q], (h + 1) * 16)
                    wait(eng, s["put"], t - W + 1)
                    eng.tensor_scalar(junk[q][:, 0, :], line[q][:, 0:BLOCK], r0[:, ds1(t)], 0.0, ALU.is_le, ALU.add,
                                      accum_out=found[q][:, 0:1])
                    eng.scalar_tensor_tensor(junk[q][:, 1, :], line[q][:, 0:BLOCK], r1[:, ds1(t)], line[q][:, BLOCK:2 * BLOCK],
                                             ALU.is_equal, ALU.mult, accum_out=found[q][:, 1:2]).then_inc(s["cnt"], 1)

                def put(t, h, q, last):
                    eng.wait_ge(s["cnt"], t + 1)
                    eng.tensor_copy(both[:, :, ds1(t)].rearrange("a c one -> a (c one)"), found[q][:, :]).then_inc(s["put"], 1)
                run(eng, (0, index), (3, find), (4, put))
                eng.wait_ge(s["put"], ST)
                eng.tensor_copy(score[:, :], both[:, 1, :])
                eng.scalar_tensor_tensor(token[:, :], blk_flat, float(BLOCK), both[:, 0, :], ALU.mult, ALU.add)


def routed_phase(core, cst, rows_in, w1, b1, w2, b2, token, score, routed):
    nc = core.nc
    R = 2
    K = HID + 1
    HALF = SL * TPE // 2 + 2 - SL * TPE // 2 % 2
    names = ("w whi wlo ix T hi lo hm act gh gl one O ev "
             + " ".join(f"swg{i}" for i in range(TPE)) + " " + " ".join(f"sws{i}" for i in range(TPE)))
    with core.phase("routed", names) as (s, sbuf, psum):
        def ring(n, shape, dt=F32):
            return [sbuf(f"{n}{q}", shape, dt) for q in range(R)] * 2

        w1r, w1h, w1l = ring("w1r", [P, KC, HID]), ring("w1h", [P, KC, HID], F32R), ring("w1l", [P, KC, HID], F32R)
        w2r, w2h, w2l = ring("w2r", [K, D]), ring("w2h", [K, D], F32R), ring("w2l", [K, D], F32R)
        b1r = ring("b1r", [HID, 1])
        ix = [sbuf(f"ix{q}", [SL, TPE], U32) for q in range(4)]
        sc = [sbuf(f"sc{q}", [SL, TPE]) for q in range(4)]
        x = ring("x", [SL, TPE, D])
        xh, xl = ring("xh", [P, KC, 2 * HALF], F32R), ring("xl", [P, KC, 2 * HALF], F32R)
        act = sbuf("act", [K, 2, HALF])
        gh, gl = sbuf("gh", [K, 2, HALF], F32R), sbuf("gl", [K, 2, HALF], F32R)
        zero = sbuf("zero", [P, KC, 2 * HALF - SL * TPE])
        res = [sbuf(f"res{i}", [SL, D]) for i in range(TPE)]
        T = [psum(f"T{j}", [P, KC, P]) for j in range(2)]
        Hp = psum("Hp", [HID, 2, 512])
        O = [psum(f"O{j}", [SL, D]) for j in range(2)]
        ga, sc_ = [s[f"swg{i}"] for i in range(TPE)], [s[f"sws{i}"] for i in range(TPE)]
        gh_f, gl_f = (v.ap().rearrange("a b n -> a (b n)") for v in (gh, gl))

        def run(eng, *stages):
            pipeline(eng, stages, count=EXPERTS, short_last=False, ways=4)

        with nc.Block() as block:
            @block.sync
            def _(eng):
                def load(e, h, q, last):
                    wait_apart(eng, s["wlo"], (e - R + 1) * 2)
                    wait_apart(eng, s["act"], e - R + 1)
                    wait_apart(eng, s["whi"], e * 2)
                    eng.dma_start(w1r[q][:, :, :], chunked(w1[ds1(e)].rearrange("one i o -> (one i) o"))).then_inc(s["w"], 16)
                    eng.dma_start(w2r[q][0:HID, :], w2[ds1(e)].rearrange("one i o -> (one i) o")).then_inc(s["w"], 16)
                    eng.dma_start(w2r[q][HID:K, :], b2[ds1(e), :]).then_inc(s["w"], 16)
                    eng.dma_start(b1r[q][:, :], b1[ds1(e), :].rearrange("one h -> h one"), allow_slow_non_contiguous=True).then_inc(s["w"], 16)
                run(eng, (0, load))

            @block.gpsimd
            def _(eng):
                def gather(e, h, q, last):
                    for i in range(TPE):
                        wait(eng, s["T"], (e - 1) * TPE + i + 1)
                        wait_apart(eng, s["ix"], e + 1)
                        eng.indirect_dma_start(x[q][:, i, :], None, rows_in,
                                               bass.IndirectOffsetOnAxis(ap=ix[q][:, i:i + 1], axis=0)).then_inc(ga[i], 16)

                def scatter(e, h, q, last):
                    for i in range(TPE):
                        wait(eng, sc_[i], e * 16)
                    for i in range(TPE):
                        wait_apart(eng, s["ev"], e * TPE + i + 1)
                        eng.indirect_dma_start(routed, bass.IndirectOffsetOnAxis(ap=ix[q][:, i:i + 1], axis=0), res[i][:, :], None,
                                               compute_op=ALU.add).then_inc(sc_[i], 16)
                run(eng, (3, scatter), (0, gather))
                for i in range(TPE):
                    eng.wait_ge(sc_[i], EXPERTS * 16)

            @block.tensor
            def _(eng):
                def turn_slots(e, h, q, last):
                    for i in range(TPE):
                        n = e * TPE + i
                        eng.wait_ge(ga[i], (e + 1) * 16)
                        wait(eng, s["lo"], n if i == 0 else n - 1)
                        for c in range(KC):
                            m = eng.transpose(T[i % 2][:, c, 0:SL], x[q][:, i, c * P:(c + 1) * P], cst.ident[0:SL, 0:SL])
                        m.then_inc(s["T"], 1)

                def up(e, h, q, last):
                    eng.wait_ge(s["lo"], (e + 1) * TPE)
                    eng.wait_ge(s["wlo"], (e + 1) * 2)
                    wait(eng, s["act"], e)
                    for b in range(2):
                        cols = slice(b * HALF, (b + 1) * HALF)
                        for c in range(KC):
                            m = three(eng, Hp[:, b, 0:HALF], w1h[q][:, c, :], w1l[q][:, c, :], xh[q][:, c, cols], xl[q][:, c, cols],
                                      c == 0, c == KC - 1)
                    m.then_inc(s["hm"], 1)

                def down(e, h, q, last):
                    eng.wait_ge(s["gl"], e + 1)
                    for i in range(TPE):
                        n = e * TPE + i
                        wait(eng, s["ev"], n if i == 0 else n - 1)
                        cols = slice(i * SL, (i + 1) * SL)
                        three(eng, O[i % 2][:, :], gh_f[:, cols], gl_f[:, cols], w2h[q][:, :], w2l[q][:, :], True, True).then_inc(s["O"], 1)
                eng.wait_ge(s["one"], 2)
                run(eng, (1, turn_slots), (2, down), (1, up))

            @block.scalar
            def _(eng):
                def weights(e, h, q, last):
                    eng.wait_ge(s["w"], (e + 1) * 64)
                    wait(eng, s["O"], (e - R + 1) * TPE)
                    eng.activation(w1h[q][:, :, :], w1r[q][:, :, :], ACT.Copy).then_inc(s["whi"], 1)
                    eng.activation(w2h[q][:, :], w2r[q][:, :], ACT.Copy).then_inc(s["whi"], 1)

                def high(e, h, q, last):
                    wait(eng, s["hm"], e - R + 1)
                    for i in range(TPE):
                        eng.wait_ge(s["T"], e * TPE + i + 1)
                        eng.activation(xh[q][:, :, i * SL:(i + 1) * SL], T[i % 2][:, :, 0:SL], ACT.Copy).then_inc(s["hi"], 1)

                def acts(e, h, q, last):
                    eng.wait_ge(s["hm"], e + 1)
                    wait(eng, s["gl"], e)
                    eng.activation(act[0:HID, :, :], Hp[:, :, 0:HALF], ACT.Gelu_apprx_tanh, bias=b1r[q][:, :]).then_inc(s["act"], 1)
                    eng.wait_ge(s["act"], e + 1)
                    wait(eng, s["O"], e * TPE)
                    eng.activation(gh[:, :, :], act[:, :, :], ACT.Copy).then_inc(s["gh"], 1)
                eng.wait_ge(s["one"], 1)
                for q in range(R):
                    eng.activation(xh[q][:, :, SL * TPE:2 * HALF], zero[:, :, :], ACT.Copy)
                    m = eng.activation(xl[q][:, :, SL * TPE:2 * HALF], zero[:, :, :], ACT.Copy)
                m.then_inc(s["one"], 1)
                run(eng, (1, high), (1, acts), (0, weights))

            @block.vector
            def _(eng):
                def index(e, h, q, last):
                    for i in range(TPE):
                        wait(eng, sc_[i], h * 16)
                    at = slice(e * TPE, e * TPE + TPE) if isinstance(e, int) else bass.ds(e * TPE, TPE)
                    eng.tensor_copy(sc[q][:, :], score[:, at])
                    eng.tensor_copy(ix[q][:, :], token[:, at]).then_inc(s["ix"], 1)

                def weights(e, h, q, last):
                    eng.wait_ge(s["whi"], e * 2 + 1)
                    eng.tensor_tensor(w1l[q][:, :, :], w1r[q][:, :, :], w1h[q][:, :, :].bitcast(F32), ALU.subtract).then_inc(s["wlo"], 1)
                    eng.wait_ge(s["whi"], e * 2 + 2)
                    eng.tensor_tensor(w2l[q][:, :], w2r[q][:, :], w2h[q][:, :].bitcast(F32), ALU.subtract).then_inc(s["wlo"], 1)

                def low(e, h, q, last):
                    for i in range(TPE):
                        cols = slice(i * SL, (i + 1) * SL)
                        eng.wait_ge(s["hi"], e * TPE + i + 1)
                        eng.tensor_tensor(xl[q][:, :, cols], T[i % 2][:, :, 0:SL], xh[q][:, :, cols].bitcast(F32), ALU.subtract).then_inc(s["lo"], 1)

                def weigh(e, h, q, last):
                    eng.wait_ge(s["ix"], e + 1)
                    for i in range(TPE):
                        wait(eng, sc_[i], e * 16)
                        eng.wait_ge(s["O"], e * TPE + i + 1)
                        eng.tensor_scalar(res[i][:, :], O[i % 2][:, :], sc[q][:, i:i + 1], None, ALU.mult).then_inc(s["ev"], 1)

                def low_units(e, h, q, last):
                    eng.wait_ge(s["gh"], e + 1)
                    eng.tensor_tensor(gl[:, :, :], act[:, :, :], gh[:, :, :].bitcast(F32), ALU.subtract).then_inc(s["gl"], 1)
                eng.memset(zero[:, :, :], 0.0)
                eng.memset(act[HID:K, :, :], 1.0).then_inc(s["one"], 1)
                run(eng, (0, index), (1, low), (2, weigh), (1, low_units), (0, weights))


def shared_phase(core, cst, rows_in, residual, routed, w1, b1, w2, b2, half, rows_out, normed):
    nc = core.nc
    K = HID + 1
    W = 4
    names = ("w whi wlo ld0 ld1 ld2 ld3 lr0 lr1 lr2 lr3 lo0 lo1 lo2 lo3 T hi lo hm act gh gl M pa y stats aggr var rstd "
             "norm st0 st1 st2 st3 sn0 sn1 sn2 sn3 one")
    with core.phase("shared", names) as (s, sbuf, psum):
        xin = [sbuf(f"xin{q}", [P, TILES, D]) for q in range(W)]
        rsd = [sbuf(f"rsd{q}", [P, TILES, D]) for q in range(W)]
        y = [sbuf(f"y{q}", [P, TILES, D]) for q in range(W)]
        nrm = [sbuf(f"nrm{q}", [P, TILES, D]) for q in range(W)]
        bn = [sbuf(f"bn{q}", [P, TILES, 6]) for q in range(W)]
        mv = [sbuf(f"mv{q}", [P, TILES, 2]) for q in range(W)]
        rs = [sbuf(f"rs{q}", [P, TILES]) for q in range(W)]
        xh = [sbuf(f"xh{q}", [P, KC, GROUP], F32R) for q in range(2)] * 2
        xl = [sbuf(f"xl{q}", [P, KC, GROUP], F32R) for q in range(2)] * 2
        rtd = [sbuf(f"rtd{q}", [P, TILES, D]) for q in range(W)]
        w1r, w1h, w1l = (sbuf(n, [P, KC, HID], dt) for n, dt in (("w1r", F32), ("w1h", F32R), ("w1l", F32R)))
        w2r, w2h, w2l = (sbuf(n, [K, D], dt) for n, dt in (("w2r", F32), ("w2h", F32R), ("w2l", F32R)))
        b1r = sbuf("b1r", [HID, 1])
        act = [sbuf(f"act{q}", [K, GROUP]) for q in range(2)] * 2
        gh = [sbuf(f"gh{q}", [K, GROUP], F32R) for q in range(2)] * 2
        gl = [sbuf(f"gl{q}", [K, GROUP], F32R) for q in range(2)] * 2
        T = psum("T", [P, KC, GROUP])
        Hp = [psum(f"Hp{q}", [HID, 512]) for q in range(2)] * 2
        O = [psum(f"O{q}", [P, TILES, D]) for q in range(2)] * 2
        ld, lr, lo, st, sn = ([s[f"{n}{q}"] for q in range(W)] for n in ("ld", "lr", "lo", "st", "sn"))
        with nc.Block() as block:
            @block.sync
            def _(eng):
                eng.dma_start(w1r[:, :, :], chunked(w1)).then_inc(s["w"], 16)
                eng.dma_start(w2r[0:HID, :], w2).then_inc(s["w"], 16)
                eng.dma_start(w2r[HID:K, :], b2.unsqueeze(0)).then_inc(s["w"], 16)
                eng.dma_start(b1r[:, :], b1.unsqueeze(1)).then_inc(s["w"], 16)

                def load(g, h, q, last):
                    wait_apart(eng, s["T"], g - W + 1)
                    eng.dma_start(part(xin[q], last), rows(rows_in, g, last)).then_inc(ld[q], 16)

                def load_addends(g, h, q, last):
                    wait_apart(eng, s["y"], g - W + 1)
                    eng.dma_start(part(rsd[q], last), rows(residual, g, last)).then_inc(lr[q], 16)
                    eng.dma_start(part(rtd[q], last), rows(routed, g, last)).then_inc(lo[q], 16)
                pipeline(eng, [(0, load), (1, load_addends)], ways=W)

            @block.gpsimd
            def _(eng):
                def add(g, h, q, last):
                    eng.wait_ge(lr[q], (h + 1) * 16)
                    eng.wait_ge(lo[q], (h + 1) * 16)
                    eng.tensor_tensor(part(rsd[q], last), part(rsd[q], last), part(rtd[q], last), ALU.add).then_inc(s["pa"], 1)
                pipeline(eng, [(1, add), (3, lambda g, h, q, last: row_rstd(eng, s, g, mv[q], half, rs[q], last))], ways=W)

            @block.tensor
            def _(eng):
                def turn_rows(g, h, q, last):
                    eng.wait_ge(ld[q], (h + 1) * 16)
                    wait(eng, s["lo"], g)
                    for t, n in tiles_of(last):
                        for c in range(KC):
                            m = eng.transpose(T[:, c, t * P:t * P + n], xin[q][0:n, t, c * P:(c + 1) * P], cst.ident[0:n, 0:n])
                    m.then_inc(s["T"], 1)

                def up(g, h, q, last):
                    w_ = width_of(last)
                    eng.wait_ge(s["lo"], g + 1)
                    wait(eng, s["act"], g - 1)
                    for c in range(KC):
                        m = three(eng, Hp[q][:, 0:w_], w1h[:, c, :], w1l[:, c, :], xh[q][:, c, 0:w_], xl[q][:, c, 0:w_], c == 0, c == KC - 1)
                    m.then_inc(s["hm"], 1)

                def down(g, h, q, last):
                    eng.wait_ge(s["gl"], g + 1)
                    wait(eng, s["y"], g - 1)
                    for t, n in tiles_of(last):
                        ts = slice(t * P, t * P + n)
                        m = three(eng, O[q][0:n, t, :], gh[q][:, ts], gl[q][:, ts], w2h[:, :], w2l[:, :], True, True)
                    m.then_inc(s["M"], 1)
                eng.wait_ge(s["wlo"], 1)
                pipeline(eng, [(0, turn_rows), (2, down), (1, up)], ways=W)

            @block.scalar
            def _(eng):
                def high(g, h, q, last):
                    w_ = width_of(last)
                    eng.wait_ge(s["T"], g + 1)
                    wait(eng, s["hm"], g - 1)
                    eng.activation(xh[q][:, :, 0:w_], T[:, :, 0:w_], ACT.Copy).then_inc(s["hi"], 1)

                def acts(g, h, q, last):
                    w_ = width_of(last)
                    eng.wait_ge(s["hm"], g + 1)
                    wait(eng, s["gl"], g - 1)
                    eng.activation(act[q][0:HID, 0:w_], Hp[q][:, 0:w_], ACT.Gelu_apprx_tanh, bias=b1r[:, :]).then_inc(s["act"], 1)
                    eng.wait_ge(s["act"], g + 1)
                    wait(eng, s["M"], g - 1)
                    eng.activation(gh[q][:, 0:w_], act[q][:, 0:w_], ACT.Copy).then_inc(s["gh"], 1)

                def store(g, h, q, last):
                    eng.wait_ge(s["y"], g + 1)
                    eng.dma_start(rows(rows_out, g, last), part(y[q], last)).then_inc(st[q], 16)
                    eng.wait_ge(s["norm"], g + 1)
                    eng.dma_start(rows(normed, g, last), part(nrm[q], last)).then_inc(sn[q], 16)
                eng.wait_ge(s["w"], 64)
                eng.activation(w1h[:, :, :], w1r[:, :, :], ACT.Copy)
                eng.activation(w2h[:, :], w2r[:, :], ACT.Copy).then_inc(s["whi"], 1)
                eng.wait_ge(s["one"], 1)
                pipeline(eng, [(0, high), (1, acts), (4, store)], ways=W)
                for q in range(W):
                    eng.wait_ge(st[q], 16 * (NG // W))
                    eng.wait_ge(sn[q], 16 * (NG // W))

            @block.vector
            def _(eng):
                def low(g, h, q, last):
                    w_ = width_of(last)
                    eng.wait_ge(s["hi"], g + 1)
                    eng.tensor_tensor(xl[q][:, :, 0:w_], T[:, :, 0:w_], xh[q][:, :, 0:w_].bitcast(F32), ALU.subtract).then_inc(s["lo"], 1)

                def low_units(g, h, q, last):
                    w_ = width_of(last)
                    eng.wait_ge(s["gh"], g + 1)
                    eng.tensor_tensor(gl[q][:, 0:w_], act[q][:, 0:w_], gh[q][:, 0:w_].bitcast(F32), ALU.subtract).then_inc(s["gl"], 1)

                def total(g, h, q, last):
                    eng.wait_ge(s["M"], g + 1)
                    eng.wait_ge(s["pa"], g + 1)
                    wait(eng, st[q], h * 16)
                    wait(eng, s["norm"], g - W + 1)
                    eng.tensor_tensor(part(y[q], last), part(O[q], last), part(rsd[q], last), ALU.add).then_inc(s["y"], 1)
                    eng.wait_ge(s["y"], g + 1)
                    row_stats(eng, s, g, y[q], bn[q], mv[q], last)

                def norm(g, h, q, last):
                    eng.wait_ge(s["rstd"], g + 1)
                    wait(eng, sn[q], h * 16)
                    row_norm(eng, y[q], nrm[q], mv[q], rs[q], last).then_inc(s["norm"], 1)
                for q in range(2):
                    m = eng.memset(act[q][HID:K, :], 1.0)
                m.then_inc(s["one"], 1)
                eng.wait_ge(s["whi"], 1)
                eng.tensor_tensor(w1l[:, :, :], w1r[:, :, :], w1h[:, :, :].bitcast(F32), ALU.subtract)
                eng.tensor_tensor(w2l[:, :], w2r[:, :], w2h[:, :].bitcast(F32), ALU.subtract).then_inc(s["wlo"], 1)
                pipeline(eng, [(0, low), (3, total), (1, low_units), (4, norm)], ways=W)


def layer_of(a, layer):
    v = a[bass.ds(layer, 1)]
    names = " ".join("abc"[:len(a.shape) - 1])
    return v.rearrange(f"one {names} -> (one {names.split()[0]}) {' '.join(names.split()[1:])}")


def message_phase(core, cst, ed, table, We, be, layer):
    nc = core.nc
    W = 4
    names = ("krow we hk hix ix swg0 swg1 swg2 swg3 mix sum mh ml sel tix B res hres head sws0 sws1 sws2 sws3")
    with core.phase("message", names) as (s, sbuf, psum):
        krow = sbuf("krow", [P, EP])
        We_b = sbuf("We", [P, D])
        be_b = sbuf("be", [P, D])
        ix = [sbuf(f"ix{q}", [P, 1], U32) for q in range(W)]
        tix = [sbuf(f"tix{q}", [P, 1], U32) for q in range(W)]
        x = [sbuf(f"x{q}", [P, D]) for q in range(W)]
        y = [sbuf(f"y{q}", [P, D]) for q in range(W)]
        z = [sbuf(f"z{q}", [P, D]) for q in range(W)]
        mh = [sbuf(f"mh{q}", [P, D], F32R) for q in range(W)]
        ml = [sbuf(f"ml{q}", [P, D], F32R) for q in range(W)]
        sel = [sbuf(f"sel{q}", [P, P], F32R) for q in range(W)]
        hd = [sbuf(f"hd{q}", [P, ET], F32R) for q in range(W)]
        hkey = sbuf("hkey", [ET, 2])
        hsame = sbuf("hsame", [ET, 1])
        hix = sbuf("hix", [ET, 1], U32)
        hres = sbuf("hres", [ET, D])
        res = [sbuf(f"res{q}", [P, D]) for q in range(W)]
        B = [psum(f"B{q}", [P, D]) for q in range(2)]
        H = psum("H", [ET, D])
        ga, sc = [s[f"swg{q}"] for q in range(W)], [s[f"sws{q}"] for q in range(W)]

        heads = krow.ap().rearrange("a (t p) -> a p t", p=P)[:, 0, :]

        def run(eng, *stages):
            pipeline(eng, stages, count=ET, short_last=False, ways=W)

        with nc.Block() as block:
            @block.sync
            def _(eng):
                eng.dma_start(krow[:, :], ed.key_row[1][0:EP].partition_broadcast(P)).then_inc(s["krow"], 16)
                eng.dma_start(We_b[:, :], layer_of(We, layer).rearrange("one d -> (one d)").partition_broadcast(P)).then_inc(s["we"], 16)
                eng.dma_start(be_b[:, :], be[bass.ds(layer, 1), :].rearrange("one d -> (one d)").partition_broadcast(P)).then_inc(s["we"], 16)
                for j in range(2):
                    eng.dma_start(hkey[:, j:j + 1], ed.key_row[1][j * P:j * P + EP].rearrange("(t p) -> t p", p=P)[:, 0:1],
                                  allow_slow_non_contiguous=True).then_inc(s["hk"], 16)

            @block.gpsimd
            def _(eng):
                def gather(t, h, q, last):
                    wait(eng, s["mix"], t - W + 1)
                    wait_apart(eng, s["ix"], t + 1)
                    eng.indirect_dma_start(x[q][:, :], None, table, bass.IndirectOffsetOnAxis(ap=ix[q][:, :], axis=0)).then_inc(ga[q], 16)

                def scatter(t, h, q, last):
                    eng.wait_ge(s["tix"], t + 1)
                    wait_apart(eng, s["res"], t + 1)
                    eng.indirect_dma_start(ed.sums[1], bass.IndirectOffsetOnAxis(ap=tix[q][:, :], axis=0), res[q][:, :], None,
                                           bounds_check=ROWS - 1, oob_is_err=False).then_inc(sc[q], 16)
                run(eng, (0, gather), (5, scatter))
                for q in range(W):
                    eng.wait_ge(sc[q], 16 * (ET // W))
                eng.wait_ge(s["hres"], 1)
                eng.indirect_dma_start(ed.sums[1], bass.IndirectOffsetOnAxis(ap=hix[:, :], axis=0), hres[:, :], None,
                                       bounds_check=ROWS - 1, oob_is_err=False).then_inc(sc[0], 16)
                eng.wait_ge(sc[0], 16 * (ET // W) + 16)

            @block.vector
            def _(eng):
                eng.wait_ge(s["krow"], 16)
                eng.wait_ge(s["we"], 32)
                eng.wait_ge(s["hk"], 32)
                eng.tensor_tensor(hsame[:, :], hkey[:, 0:1], hkey[:, 1:2], ALU.is_equal).then_inc(s["hix"], 1)
                eng.wait_ge(s["hix"], 1)
                eng.scalar_tensor_tensor(hix[:, :], hsame[:, :], NO_ROW, hkey[:, 0:1], ALU.mult, ALU.add).then_inc(s["hix"], 1)

                def index(t, h, q, last):
                    wait(eng, ga[q], h * 16)
                    eng.tensor_copy(ix[q][:, :], ed.partner[1][:, ds1(t)]).then_inc(s["ix"], 1)

                def select(t, h, q, last):
                    wait(eng, s["B"], t - W + 1)
                    eng.tensor_scalar(hd[q][:, :], heads, ed.key[1][:, ds1(t)], None, ALU.is_equal).then_inc(s["head"], 1)
                    eng.tensor_scalar(sel[q][:, :], krow[:, bass.ts(t, P)], ed.key[1][:, ds1(t)], None, ALU.is_equal).then_inc(s["sel"], 1)

                def target(t, h, q, last):
                    wait(eng, sc[q], h * 16)
                    eng.tensor_copy(tix[q][:, :], ed.target[1][:, ds1(t)]).then_inc(s["tix"], 1)

                def add(t, h, q, last):
                    eng.wait_ge(ga[q], (h + 1) * 16)
                    eng.scalar_tensor_tensor(y[q][:, :], We_b[:, :], ed.weight[1][:, ds1(t)], x[q][:, :], ALU.mult, ALU.add).then_inc(s["mix"], 1)
                    eng.wait_ge(s["mix"], t + 1)
                    wait(eng, s["ml"], t - W + 1)
                    eng.tensor_tensor(z[q][:, :], y[q][:, :], be_b[:, :], ALU.add).then_inc(s["sum"], 1)

                def low(t, h, q, last):
                    eng.wait_ge(s["mh"], t + 1)
                    wait(eng, s["B"], t - W + 1)
                    eng.scalar_tensor_tensor(ml[q][:, :], z[q][:, :], 0.0, mh[q][:, :].bitcast(F32), ALU.max, ALU.subtract).then_inc(s["ml"], 1)
                run(eng, (0, index), (3, add), (4, low), (3, select), (4, target))
                eng.wait_ge(s["B"], ET)
                eng.wait_ge(s["hix"], 2)
                eng.tensor_copy(hres[:, :], H[:, :]).then_inc(s["hres"], 1)

            @block.scalar
            def _(eng):
                def high(t, h, q, last):
                    eng.wait_ge(s["sum"], t + 1)
                    wait(eng, s["B"], t - W + 1)
                    eng.activation(mh[q][:, :], z[q][:, :], ACT.Relu).then_inc(s["mh"], 1)

                def result(t, h, q, last):
                    eng.wait_ge(s["B"], t + 1)
                    wait(eng, sc[q], h * 16)
                    eng.activation(res[q][:, :], B[q % 2][:, :], ACT.Copy).then_inc(s["res"], 1)
                run(eng, (3, high), (5, result))

            @block.tensor
            def _(eng):
                def sums(t, h, q, last):
                    eng.wait_ge(s["ml"], t + 1)
                    eng.wait_ge(s["sel"], t + 1)
                    wait(eng, s["res"], t - 1)
                    eng.matmul(B[q % 2][:, :], sel[q][:, :], mh[q][:, :], start=True, stop=False)
                    eng.matmul(B[q % 2][:, :], sel[q][:, :], ml[q][:, :], start=False, stop=True)
                    eng.wait_ge(s["head"], t + 1)
                    first, end = (isinstance(t, int) and t == 0), (isinstance(t, int) and t == ET - 1)
                    eng.matmul(H[:, :], hd[q][:, :], mh[q][:, :], start=first, stop=False)
                    eng.matmul(H[:, :], hd[q][:, :], ml[q][:, :], start=False, stop=end).then_inc(s["B"], 1)
                run(eng, (4, sums))


def hidden_phase(core, cst, ed, table, eps, b1, w, layer, hT, stats):
    nc = core.nc
    wh, wl = w
    names = "eps eps1 b1 ld0 ld1 la pre T hi lo M ev bn"
    with core.phase("hidden", names) as (s, sbuf, psum):
        e_t = sbuf("eps", [P, 1])
        b1t = sbuf("b1", [P, KC])
        xin = [sbuf(f"xin{q}", [P, TILES, D]) for q in range(2)]
        agg = sbuf("agg", [P, TILES, D])
        xh = [sbuf(f"xh{q}", [P, KC, GROUP], F32R) for q in range(2)]
        xl = [sbuf(f"xl{q}", [P, KC, GROUP], F32R) for q in range(2)]
        T = [psum(f"T{q}", [P, KC, GROUP]) for q in range(2)]
        O = [psum(f"O{q}", [P, KC, GROUP]) for q in range(2)]
        ld = (s["ld0"], s["ld1"])
        at = lambda g, w_: slice(g * GROUP, g * GROUP + w_) if isinstance(g, int) else bass.ds(g * GROUP, w_)
        with nc.Block() as block:
            @block.sync
            def _(eng):
                eng.dma_start(e_t[:, :], eps[bass.ds(layer, 1)].partition_broadcast(P)).then_inc(s["eps"], 16)
                eng.dma_start(b1t[:, :], b1[bass.ds(layer, 1), :].rearrange("one (c p) -> (one p) c", p=P),
                              allow_slow_non_contiguous=True).then_inc(s["b1"], 16)

                def load(g, h, q, last):
                    wait_apart(eng, s["T"], g - 1)
                    eng.dma_start(part(xin[q], last), rows(table, g, last)).then_inc(ld[q], 16)
                    wait_apart(eng, s["pre"], g)
                    eng.dma_start(part(agg, last), rows(ed.sums[1], g, last)).then_inc(s["la"], 16)
                pipeline(eng, [(0, load)])

            @block.tensor
            def _(eng):
                def product(g, h, q, last):
                    w_ = width_of(last)
                    eng.wait_ge(s["lo"], g + 1)
                    wait(eng, s["ev"], g - 1)
                    for o in range(KC):
                        for c in range(KC):
                            cs = slice(o * P, (o + 1) * P)
                            m = three(eng, O[q][:, o, 0:w_], wh[:, c, cs], wl[:, c, cs], xh[q][:, c, 0:w_], xl[q][:, c, 0:w_],
                                      c == 0, c == KC - 1)
                    m.then_inc(s["M"], 1)
                pipeline(eng, [(0, lambda g, h, q, last: turn(eng, s, g, h, q, last, None, xin, T, cst.ident)), (1, product)])

            @block.scalar
            def _(eng):
                def evacuate(g, h, q, last):
                    w_ = width_of(last)
                    wait_apart(eng, s["M"], g + 1)
                    for o in range(KC):
                        m = eng.activation(hT[:, o, at(g, w_)], O[q][:, o, 0:w_], ACT.Identity, bias=b1t[:, o:o + 1])
                    m.then_inc(s["ev"], 1)
                eng.wait_ge(s["b1"], 16)
                pipeline(eng, [(0, lambda g, h, q, last: split_hi(eng, s, g, q, last, T, xh)), (1, evacuate)])

            @block.vector
            def _(eng):
                eng.wait_ge(s["eps"], 16)
                eng.tensor_scalar(e_t[:, :], e_t[:, :], 1.0, None, ALU.add).then_inc(s["eps1"], 1)
                eng.wait_ge(s["eps1"], 1)

                def mix(g, h, q, last):
                    eng.wait_ge(ld[q], (h + 1) * 16)
                    eng.wait_ge(s["la"], (g + 1) * 16)
                    eng.scalar_tensor_tensor(part(xin[q], last), part(xin[q], last), e_t[0:REST if last else P, :], part(agg, last),
                                             ALU.mult, ALU.add).then_inc(s["pre"], 1)

                def statistics(g, h, q, last):
                    w_ = width_of(last)
                    wait_apart(eng, s["ev"], g + 1)
                    for o in range(KC):
                        m = eng.bn_stats(stats[:, o, ds1(g), :].rearrange("a one k -> a (one k)"), hT[:, o, at(g, w_)])
                    m.then_inc(s["bn"], 1)
                pipeline(eng, [(0, mix), (1, lambda g, h, q, last: split_lo(eng, s, g, q, last, T, xh, xl)), (2, statistics)])


def output_phase(core, cst, table, gamma, beta, b2, w, layer, hT, stats):
    nc = core.nc
    wh, wl = w
    names = "ld b2 agg var rstd sc mean aff nrm hi lo M add y st0 st1"
    with core.phase("output", names) as (s, sbuf, psum):
        gm = sbuf("gm", [P, KC])
        bt = sbuf("bt", [P, KC])
        b2t = sbuf("b2t", [P, D])
        mv = sbuf("mv", [P, KC, 2])
        rs = sbuf("rs", [P, KC])
        scl = sbuf("scl", [P, KC])
        ms = sbuf("ms", [P, KC])
        shf = sbuf("shf", [P, KC])
        hh = [sbuf(f"hh{q}", [P, KC, GROUP], F32R) for q in range(2)]
        hl = [sbuf(f"hl{q}", [P, KC, GROUP], F32R) for q in range(2)]
        y = [sbuf(f"y{q}", [P, TILES, D]) for q in range(2)]
        O = [psum(f"O{q}", [P, TILES, D]) for q in range(2)]
        st = (s["st0"], s["st1"])
        at = lambda g, w_: slice(g * GROUP, g * GROUP + w_) if isinstance(g, int) else bass.ds(g * GROUP, w_)
        with nc.Block() as block:
            @block.sync
            def _(eng):
                for t, a in ((gm, gamma), (bt, beta)):
                    eng.dma_start(t[:, :], a[bass.ds(layer, 1), :].rearrange("one (c p) -> (one p) c", p=P),
                                  allow_slow_non_contiguous=True).then_inc(s["ld"], 16)
                eng.dma_start(b2t[:, :], b2[bass.ds(layer, 1), :].rearrange("one d -> (one d)").partition_broadcast(P)).then_inc(s["b2"], 16)

                def store(g, h, q, last):
                    wait_apart(eng, s["y"], g + 1)
                    eng.dma_start(rows(table, g, last), part(y[q], last)).then_inc(st[q], 16)
                pipeline(eng, [(0, store)])
                for q in range(2):
                    eng.wait_ge(st[q], 16 * (NG // 2))

            @block.gpsimd
            def _(eng):
                eng.wait_ge(s["var"], 1)
                eng.tensor_tensor(rs[:, :], mv[:, :, 1], cst.half[:, :], ALU.pow).then_inc(s["rstd"], 1)

            @block.vector
            def _(eng):
                for o in range(KC):
                    m = eng.bn_aggr(mv[:, o, :], stats[:, o, :, :].rearrange("a g k -> a (g k)"))
                m.then_inc(s["agg"], 1)
                eng.wait_ge(s["agg"], 1)
                eng.tensor_scalar(mv[:, :, 1], mv[:, :, 1], EPS, None, ALU.add).then_inc(s["var"], 1)
                eng.wait_ge(s["rstd"], 1)
                eng.wait_ge(s["ld"], 32)
                eng.tensor_tensor(scl[:, :], rs[:, :], gm[:, :], ALU.mult).then_inc(s["sc"], 1)
                eng.wait_ge(s["sc"], 1)
                eng.tensor_tensor(ms[:, :], mv[:, :, 0], scl[:, :], ALU.mult).then_inc(s["mean"], 1)
                eng.wait_ge(s["mean"], 1)
                eng.tensor_tensor(shf[:, :], bt[:, :], ms[:, :], ALU.subtract).then_inc(s["aff"], 1)
                eng.wait_ge(s["b2"], 16)

                def low(g, h, q, last):
                    w_ = width_of(last)
                    eng.wait_ge(s["hi"], g + 1)
                    eng.tensor_tensor(hl[q][:, :, 0:w_], hT[:, :, at(g, w_)], hh[q][:, :, 0:w_].bitcast(F32), ALU.subtract).then_inc(s["lo"], 1)

                def add(g, h, q, last):
                    n, k = (REST, 1) if last else (P, TILES)
                    eng.wait_ge(s["M"], g + 1)
                    wait(eng, st[q], h * 16)
                    eng.tensor_tensor(part(y[q], last), part(O[q], last), b2t[0:n, :].unsqueeze(1).to_broadcast([n, k, D]),
                                      ALU.add).then_inc(s["add"], 1)
                pipeline(eng, [(0, low), (1, add)])

            @block.scalar
            def _(eng):
                def normal(g, h, q, last):
                    w_ = width_of(last)
                    for o in range(KC):
                        m = eng.activation(hT[:, o, at(g, w_)], hT[:, o, at(g, w_)], ACT.Relu, bias=shf[:, o:o + 1], scale=scl[:, o:o + 1])
                    m.then_inc(s["nrm"], 1)
                    eng.wait_ge(s["nrm"], g + 1)
                    wait_apart(eng, s["M"], g - 1)
                    eng.activation(hh[q][:, :, 0:w_], hT[:, :, at(g, w_)], ACT.Copy).then_inc(s["hi"], 1)

                def finish(g, h, q, last):
                    eng.wait_ge(s["add"], g + 1)
                    eng.activation(part(y[q], last), part(y[q], last), ACT.Relu).then_inc(s["y"], 1)
                eng.wait_ge(s["aff"], 1)
                pipeline(eng, [(0, normal), (2, finish)])

            @block.tensor
            def _(eng):
                def product(g, h, q, last):
                    eng.wait_ge(s["lo"], g + 1)
                    wait(eng, s["add"], g - 1)
                    for t, n in tiles_of(last):
                        ts = slice(t * P, t * P + n)
                        for c in range(KC):
                            m = three(eng, O[q][0:n, t, :], hh[q][:, c, ts], hl[q][:, c, ts], wh[:, c, :], wl[:, c, :], c == 0, c == KC - 1)
                    m.then_inc(s["M"], 1)
                pipeline(eng, [(0, product)])


def ternary_phase(core, cst, w_up, w_down, up, down, scales):
    nc = core.nc
    names = "ld abs sum mean clip rec sc rnd q cp T"
    with core.phase("ternary", names) as (s, sbuf, psum):
        wu = sbuf("wu", [HID, D])
        wd = sbuf("wd", [P, KC, HID])
        qu = sbuf("qu", [HID, D])
        qd = sbuf("qd", [P, KC, HID])
        bu = sbuf("bu", [HID, D], BF16)
        bd = sbuf("bd", [P, KC, HID], BF16)
        total = sbuf("total", [P, 2])
        ones = sbuf("ones", [P, P])
        inv = sbuf("inv", [P, 2])
        S = psum("S", [P, 2])
        Tu = psum("Tu", [P, KC, HID], BF16)
        Td = psum("Td", [HID, KC, P], BF16)
        with nc.Block() as block:
            @block.sync
            def _(eng):
                eng.dma_start(wu[:, :], w_up).then_inc(s["ld"], 16)
                eng.dma_start(wd[:, :, :], w_down.rearrange("(c p) h -> p c h", p=P)).then_inc(s["ld"], 16)

            @block.vector
            def _(eng):
                eng.memset(total[:, :], 0.0).then_inc(s["abs"], 1)
                eng.memset(ones[:, :], 1.0)
                eng.wait_ge(s["ld"], 32)
                eng.wait_ge(s["abs"], 1)
                eng.tensor_reduce(total[0:HID, 0:1], wu[:, :], AX.X, ALU.add, apply_absolute_value=True)
                eng.tensor_reduce(total[:, 1:2], wd.ap().rearrange("a c h -> a (c h)"), AX.X, ALU.add, apply_absolute_value=True).then_inc(s["sum"], 1)
                eng.wait_ge(s["mean"], 1)
                eng.tensor_scalar(scales[:, :], S[:, :], 1.0 / (HID * D), EPS, ALU.mult, ALU.max).then_inc(s["clip"], 1)
                eng.wait_ge(s["clip"], 1)
                eng.reciprocal(inv[:, :], scales[:, :]).then_inc(s["rec"], 1)
                eng.wait_ge(s["rec"], 1)
                eng.tensor_scalar(qu[:, :], wu[:, :], inv[0:HID, 0:1], MAGIC, ALU.mult, ALU.add)
                eng.tensor_scalar(qd[:, :, :], wd[:, :, :], inv[:, 1:2], MAGIC, ALU.mult, ALU.add).then_inc(s["rnd"], 1)
                eng.wait_ge(s["rnd"], 1)
                eng.tensor_scalar(qu[:, :], qu[:, :], MAGIC, 1.0, ALU.subtract, ALU.min)
                eng.tensor_scalar(qd[:, :, :], qd[:, :, :], MAGIC, 1.0, ALU.subtract, ALU.min).then_inc(s["rnd"], 1)
                eng.wait_ge(s["rnd"], 2)
                eng.tensor_scalar(bu[:, :], qu[:, :], -1.0, None, ALU.max)
                eng.tensor_scalar(bd[:, :, :], qd[:, :, :], -1.0, None, ALU.max).then_inc(s["q"], 1)
                eng.wait_ge(s["T"], 1)
                eng.tensor_copy(up[:, :, :], Tu[:, :, :])
                eng.tensor_copy(down[:, :], Td.ap().rearrange("h c o -> h (c o)"))

            @block.tensor
            def _(eng):
                eng.wait_ge(s["sum"], 1)
                eng.matmul(S[:, :], ones[:, :], total[:, :], start=True, stop=True).then_inc(s["mean"], 1)
                eng.wait_ge(s["q"], 1)
                for c in range(KC):
                    eng.transpose(Tu[:, c, :], bu[:, c * P:(c + 1) * P], cst.ident_b[0:HID, 0:HID])
                for c in range(KC):
                    m = eng.transpose(Td[:, c, :], bd[:, c, :], cst.ident_b[:, :])
                m.then_inc(s["T"], 1)


def quantized_phase(core, cst, x2, gnn, up, down, scales, half, out):
    nc = core.nc
    LVL = 127.0
    W, R = 8, 4
    names = ("ld0 ld1 ld2 ld3 lg0 lg1 lg2 lg3 st0 st1 st2 st3 x3 stats aggr var neg rstd nb nrm amax unit "
             "lvl magic rnd clip q T qT U h0 h1 h2 am2 u2 lv2 s1 s2 q2 T2 q2T O y k")
    with core.phase("quant", names) as (s, sbuf, psum):
        def ring(n, shape, dt=F32):
            return [sbuf(f"{n}{q}", shape, dt) for q in range(R)] * (W // R)

        x3 = [sbuf(f"x3{q}", [P, TILES, D]) for q in range(W)]
        gn, nr, rd, yo = (ring(n, [P, TILES, D]) for n in ("gn", "nr", "rd", "yo"))
        xq, xqT = ring("xq", [P, TILES, D], BF16), ring("xqT", [P, KC, GROUP], BF16)
        bn, mv = ring("bn", [P, TILES, 6]), ring("mv", [P, TILES, 2])
        rs, ng, nb = (ring(n, [P, TILES]) for n in ("rs", "ng", "nb"))
        am, un, lv, k0, am2, un2, lv2, k1 = (ring(n, [P, TILES]) for n in ("am", "un", "lv", "k0", "am2", "un2", "lv2", "k1"))
        hf, hr, hs = (ring(n, [P, TILES, HID]) for n in ("hf", "hr", "hs"))
        magic = sbuf("magic", [P, 1])
        hq, hqT = ring("hq", [P, TILES, HID], BF16), ring("hqT", [HID, GROUP], BF16)
        T = psum("T", [P, KC, GROUP], BF16)
        U = psum("U", [P, TILES, HID])
        T2 = psum("T2", [HID, GROUP], BF16)
        O = psum("O", [P, TILES, D])
        ld, lg, st = ([s[f"{n}{q}"] for q in range(R)] * (W // R) for n in ("ld", "lg", "st"))
        H = lambda h, q: h * (W // R) + q // R
        nk = lambda last: (REST, 1) if last else (P, TILES)

        with nc.Block() as block:
            @block.sync
            def _(eng):
                def load(g, h, q, last):
                    wait_apart(eng, s["y"], g - W + 1)
                    wait_apart(eng, s["x3"], g - R + 1)
                    eng.dma_start(part(x3[q], last), rows(x2, g, last)).then_inc(ld[q], 16)
                    eng.dma_start(part(gn[q], last), rows(gnn, g, last)).then_inc(lg[q], 16)
                pipeline(eng, [(0, load)], ways=W)

            @block.gpsimd
            def _(eng):
                eng.memset(magic[:, :], MAGIC).then_inc(s["magic"], 1)

                def rstd(g, h, q, last):
                    n, k = nk(last)
                    row_rstd(eng, s, g, mv[q], half, rs[q], last)
                    eng.wait_ge(s["rstd"], g + 1)
                    eng.tensor_tensor(nb[q][0:n, 0:k], ng[q][0:n, 0:k], rs[q][0:n, 0:k], ALU.mult).then_inc(s["nb"], 1)

                def add(g, h, q, last):
                    eng.wait_ge(ld[q], (H(h, q) + 1) * 16)
                    eng.wait_ge(lg[q], (H(h, q) + 1) * 16)
                    eng.tensor_tensor(part(x3[q], last), part(x3[q], last), part(gn[q], last), ALU.add).then_inc(s["x3"], 1)
                pipeline(eng, [(2, rstd), (1, add)], ways=W)

            @block.vector
            def _(eng):
                def stats(g, h, q, last):
                    n, k = nk(last)
                    eng.wait_ge(s["x3"], g + 1)
                    wait(eng, s["nb"], g - R + 1)
                    row_stats(eng, s, g, x3[q], bn[q], mv[q], last, negated=ng[q])

                def levels(g, h, q, last):
                    n, k = nk(last)
                    eng.wait_ge(s["nrm"], g + 1)
                    eng.tensor_reduce(am[q][0:n, 0:k], nr[q][0:n, 0:k, :], AX.X, ALU.max, apply_absolute_value=True).then_inc(s["amax"], 1)
                    eng.wait_ge(s["amax"], g + 1)
                    eng.tensor_scalar(un[q][0:n, 0:k], am[q][0:n, 0:k], EPS, 1.0 / LVL, ALU.max, ALU.mult).then_inc(s["unit"], 1)
                    eng.wait_ge(s["unit"], g + 1)
                    eng.reciprocal(lv[q][0:n, 0:k], un[q][0:n, 0:k]).then_inc(s["lvl"], 1)
                    eng.tensor_scalar(k0[q][0:n, 0:k], un[q][0:n, 0:k], scales[0:n, 0:1], None, ALU.mult)

                def clamp(g, h, q, last):
                    n, k = nk(last)
                    eng.wait_ge(s["rnd"], g + 1)
                    eng.tensor_scalar(rd[q][0:n, 0:k, :], rd[q][0:n, 0:k, :], MAGIC + LVL, MAGIC - LVL - 1, ALU.min, ALU.max).then_inc(s["clip"], 1)

                def hidden(g, h, q, last):
                    n, k = nk(last)
                    eng.wait_ge(s["U"], g + 1)
                    for t, r in tiles_of(last):
                        m = eng.tensor_scalar(hf[q][0:r, t, :], U[0:r, t, :], k0[q][0:r, t:t + 1], 0.0, ALU.mult, ALU.max)
                    m.then_inc(s["h0"], 1)
                    eng.wait_ge(s["h0"], g + 1)
                    eng.tensor_scalar(hr[q][0:n, 0:k, :], hf[q][0:n, 0:k, :], MAGIC, MAGIC, ALU.add, ALU.subtract).then_inc(s["h1"], 1)
                    eng.wait_ge(s["h1"], g + 1)
                    eng.tensor_scalar(hf[q][0:n, 0:k, :], hr[q][0:n, 0:k, :], LVL, -LVL - 1, ALU.min, ALU.max).then_inc(s["h2"], 1)
                    eng.wait_ge(s["h2"], g + 1)
                    eng.tensor_reduce(am2[q][0:n, 0:k], hf[q][0:n, 0:k, :], AX.X, ALU.max, apply_absolute_value=True).then_inc(s["am2"], 1)
                    eng.wait_ge(s["am2"], g + 1)
                    eng.tensor_scalar(un2[q][0:n, 0:k], am2[q][0:n, 0:k], EPS, 1.0 / LVL, ALU.max, ALU.mult).then_inc(s["u2"], 1)
                    eng.wait_ge(s["u2"], g + 1)
                    eng.reciprocal(lv2[q][0:n, 0:k], un2[q][0:n, 0:k]).then_inc(s["lv2"], 1)
                    eng.tensor_scalar(k1[q][0:n, 0:k], un2[q][0:n, 0:k], scales[0:n, 1:2], None, ALU.mult).then_inc(s["k"], 1)
                    eng.wait_ge(s["lv2"], g + 1)
                    for t, r in tiles_of(last):
                        m = eng.tensor_scalar(hs[q][0:r, t, :], hf[q][0:r, t, :], lv2[q][0:r, t:t + 1], MAGIC, ALU.mult, ALU.add)
                    m.then_inc(s["s1"], 1)
                    eng.wait_ge(s["s1"], g + 1)
                    eng.tensor_scalar(hr[q][0:n, 0:k, :], hs[q][0:n, 0:k, :], MAGIC + LVL, MAGIC - LVL - 1, ALU.min, ALU.max).then_inc(s["s2"], 1)
                    eng.wait_ge(s["s2"], g + 1)
                    wait(eng, s["T2"], g - R + 1)
                    eng.tensor_scalar(hq[q][0:n, 0:k, :], hr[q][0:n, 0:k, :], MAGIC, None, ALU.subtract).then_inc(s["q2"], 1)

                def final(g, h, q, last):
                    eng.wait_ge(s["O"], g + 1)
                    wait(eng, st[q], H(h, q) * 16)
                    eng.wait_ge(s["k"], g + 1)
                    for t, r in tiles_of(last):
                        m = eng.scalar_tensor_tensor(yo[q][0:r, t, :], O[0:r, t, :], k1[q][0:r, t:t + 1], x3[q][0:r, t, :], ALU.mult, ALU.add)
                    m.then_inc(s["y"], 1)
                pipeline(eng, [(7, final), (6, hidden), (5, clamp), (2, stats), (4, levels)], ways=W)

            @block.scalar
            def _(eng):
                def integers(g, h, q, last):
                    n, k = nk(last)
                    eng.wait_ge(s["clip"], g + 1)
                    wait(eng, s["T"], g - R + 1)
                    eng.activation(xq[q][0:n, 0:k, :], rd[q][0:n, 0:k, :], ACT.Copy, bias=-MAGIC).then_inc(s["q"], 1)

                def norm(g, h, q, last):
                    eng.wait_ge(s["nb"], g + 1)
                    wait(eng, s["rnd"], g - R + 1)
                    for t, r in tiles_of(last):
                        m = eng.activation(nr[q][0:r, t, :], x3[q][0:r, t, :], ACT.Identity, bias=nb[q][0:r, t:t + 1], scale=rs[q][0:r, t:t + 1])
                    m.then_inc(s["nrm"], 1)

                def scale(g, h, q, last):
                    eng.wait_ge(s["lvl"], g + 1)
                    wait(eng, s["q"], g - R + 1)
                    for t, r in tiles_of(last):
                        m = eng.activation(rd[q][0:r, t, :], nr[q][0:r, t, :], ACT.Identity, bias=magic[0:r, :], scale=lv[q][0:r, t:t + 1])
                    m.then_inc(s["rnd"], 1)

                def copy_rows(g, h, q, last):
                    w_ = width_of(last)
                    eng.wait_ge(s["T"], g + 1)
                    wait(eng, s["U"], g - R + 1)
                    eng.activation(xqT[q][:, :, 0:w_], T[:, :, 0:w_], ACT.Copy).then_inc(s["qT"], 1)

                def copy_hidden(g, h, q, last):
                    w_ = width_of(last)
                    eng.wait_ge(s["T2"], g + 1)
                    wait(eng, s["O"], g - R + 1)
                    eng.activation(hqT[q][:, 0:w_], T2[:, 0:w_], ACT.Copy).then_inc(s["q2T"], 1)

                def store(g, h, q, last):
                    eng.wait_ge(s["y"], g + 1)
                    eng.dma_start(rows(out, g, last), part(yo[q], last)).then_inc(st[q], 16)
                eng.wait_ge(s["magic"], 1)
                pipeline(eng, [(3, norm), (7, store), (6, copy_hidden), (5, integers), (5, copy_rows), (4, scale)], ways=W)
                for q in range(R):
                    eng.wait_ge(st[q], 16 * (NG // R))

            @block.tensor
            def _(eng):
                def turn_hidden(g, h, q, last):
                    eng.wait_ge(s["q2"], g + 1)
                    wait_apart(eng, s["q2T"], g)
                    for t, n in tiles_of(last):
                        m = eng.transpose(T2[:, t * P:t * P + n], hq[q][0:n, t, :], cst.ident_b[0:n, 0:n])
                    m.then_inc(s["T2"], 1)

                def down_(g, h, q, last):
                    eng.wait_ge(s["q2T"], g + 1)
                    wait(eng, s["y"], g)
                    for t, n in tiles_of(last):
                        m = eng.matmul(O[0:n, t, :], hqT[q][:, t * P:t * P + n], down[:, :], start=True, stop=True)
                    m.then_inc(s["O"], 1)

                def turn_rows(g, h, q, last):
                    eng.wait_ge(s["q"], g + 1)
                    wait(eng, s["qT"], g)
                    for t, n in tiles_of(last):
                        for c in range(KC):
                            m = eng.transpose(T[:, c, t * P:t * P + n], xq[q][0:n, t, c * P:(c + 1) * P], cst.ident_b[0:n, 0:n])
                    m.then_inc(s["T"], 1)

                def up_(g, h, q, last):
                    eng.wait_ge(s["qT"], g + 1)
                    wait(eng, s["h0"], g)
                    for t, n in tiles_of(last):
                        for c in range(KC):
                            m = eng.matmul(U[0:n, t, :], xqT[q][:, c, t * P:t * P + n], up[:, c, :], start=c == 0, stop=c == KC - 1)
                    m.then_inc(s["U"], 1)
                pipeline(eng, [(6, turn_hidden), (6, down_), (5, turn_rows), (5, up_)], ways=W)


def scratch(nc, name, shape):
    return nc.dram_tensor(name, shape, F32).ap()


def first_gnn(core, cst, ed, a, x, normed, hidden, rows_out, normed_out):
    nc = core.nc
    for n, table in ((1, normed), (2, hidden)):
        with nc.sbuf_tensor(f"w_hi{n}", [P, RELATIONS * KC, D], F32R) as w_hi, \
                nc.sbuf_tensor(f"w_lo{n}", [P, RELATIONS * KC, D], F32R) as w_lo:
            combine_phase(core, cst, a[f"L0_gnn_basis{n}"], a[f"L0_gnn_att{n}"], w_hi, w_lo)
            relation_phase(core, cst, ed, table, a[f"L0_gnn_gate_w{n}"], w_hi, w_lo)
        with nc.sbuf_tensor(f"root_hi{n}", [P, KC, D], F32R) as hi, nc.sbuf_tensor(f"root_lo{n}", [P, KC, D], F32R) as lo:
            split_phase(core, "root_split", [(chunked(a[f"L0_gnn_root{n}"]), hi[:, :, :], lo[:, :, :])])
            if n == 1:
                root_phase(core, cst, ed, normed, (hi, lo), a["L0_gnn_bias1"], cst.half, hidden)
            else:
                root_phase(core, cst, ed, hidden, (hi, lo), a["L0_gnn_bias2"], cst.half, rows_out, x, normed_out)


def first_ffn(core, cst, ed, a, x, normed, probs, rows_out, normed_out):
    nc = core.nc
    table, ends = scratch(nc, "slot_table", (EXPERTS * NB, 2 * BLOCK)), scratch(nc, "slot_ends", (EXPERTS * NB,))
    route_phase(core, cst, normed, a["L0_ffn_gate_w"], probs)
    select_phase(core, cst, probs, table, ends)
    with nc.sbuf_tensor("slot_token", [SL, ST], U32) as token, nc.sbuf_tensor("slot_score", [SL, ST], F32) as score:
        slots_phase(core, table, ends, token, score)
        routed_phase(core, cst, normed, a["L0_ffn_w1"], a["L0_ffn_b1"], a["L0_ffn_w2"], a["L0_ffn_b2"], token, score, ed.routed)
    shared_phase(core, cst, normed, x, ed.routed, a["L0_ffn_sw1"], a["L0_ffn_sb1"], a["L0_ffn_sw2"], a["L0_ffn_sb2"],
                 cst.half, rows_out, normed_out)


def second_gnn(core, cst, ed, a, g):
    nc = core.nc
    with nc.Fori(0, LAYERS) as layer:
        def weight(name):
            return a[name][bass.ds(layer, 1)].rearrange("one (c p) n -> (one p) c n", p=P)

        message_phase(core, cst, ed, g, a["L1_gnn_We"], a["L1_gnn_be"], layer)
        with nc.sbuf_tensor("hT", [P, KC, N], F32) as hT, nc.sbuf_tensor("h_stats", [P, KC, NG, 6], F32) as stats:
            with nc.sbuf_tensor("w1_hi", [P, KC, D], F32R) as hi, nc.sbuf_tensor("w1_lo", [P, KC, D], F32R) as lo:
                split_phase(core, "W1_split", [(weight("L1_gnn_W1"), hi[:, :, :], lo[:, :, :])])
                hidden_phase(core, cst, ed, g, a["L1_gnn_eps"], a["L1_gnn_b1"], (hi, lo), layer, hT, stats)
            with nc.sbuf_tensor("w2_hi", [P, KC, D], F32R) as hi, nc.sbuf_tensor("w2_lo", [P, KC, D], F32R) as lo:
                split_phase(core, "W2_split", [(weight("L1_gnn_W2"), hi[:, :, :], lo[:, :, :])])
                output_phase(core, cst, g, a["L1_gnn_gamma"], a["L1_gnn_beta"], a["L1_gnn_b2"], (hi, lo), layer, hT, stats)


def second_ffn(core, cst, a, x, g, out):
    nc = core.nc
    with nc.sbuf_tensor("up", [P, KC, HID], BF16) as up, nc.sbuf_tensor("down", [HID, D], BF16) as down, \
            nc.sbuf_tensor("scales", [P, 2], F32) as scales:
        ternary_phase(core, cst, a["L1_ffn_w_up"], a["L1_ffn_w_down"], up, down, scales)
        quantized_phase(core, cst, x, g, up, down, scales, cst.half, out)


def build(nc, a, out):
    core = Core(nc)
    ed = Edges(nc)
    normed0, hidden, x1, normed1 = (scratch(nc, n, (N, D)) for n in ("normed0", "hidden", "x1", "normed1"))
    x2, g = scratch(nc, "x2", (N, D)), scratch(nc, "g", (N, D))
    probs = scratch(nc, "probs", (EXPERTS, N))
    with ExitStack() as early:
        cst = Constants(core, early)
        order_phase(core, ed, cst, a["src"], a["dst"], a["edge_type_2"], a["edge_weight1"])
        norm_phase(core, a["x"], normed0, cst.half)
        first_gnn(core, cst, ed, a, a["x"], normed0, hidden, x1, normed1)
        first_ffn(core, cst, ed, a, x1, normed1, probs, x2, g)
    second_gnn(core, cst, ed, a, g)
    second_ffn(core, cst, a, x2, g, out)


_INS = """x src dst edge_type_2 edge_weight1 L0_gnn_basis1 L0_gnn_att1 L0_gnn_gate_w1 L0_gnn_root1 L0_gnn_bias1
    L0_gnn_basis2 L0_gnn_att2 L0_gnn_gate_w2 L0_gnn_root2 L0_gnn_bias2 L0_ffn_gate_w L0_ffn_w1 L0_ffn_b1 L0_ffn_w2
    L0_ffn_b2 L0_ffn_sw1 L0_ffn_sb1 L0_ffn_sw2 L0_ffn_sb2 L1_gnn_eps L1_gnn_We L1_gnn_be L1_gnn_W1 L1_gnn_b1
    L1_gnn_gamma L1_gnn_beta L1_gnn_W2 L1_gnn_b2 L1_ffn_w_up L1_ffn_w_down""".split()


def kernel(**inputs):
    import numpy as np
    import concourse.bacc as bacc
    from concourse.bass_utils import run_bass_kernel_spmd

    nc = bacc.Bacc("TRN2", target_bir_lowering=False, num_devices=1)
    arrays, args = {}, {}
    for name in _INS:
        v = np.ascontiguousarray(inputs[name])
        arrays[f"in_{name}"] = v
        args[name] = nc.dram_tensor(f"in_{name}", v.shape, mybir.dt.from_np(v.dtype), kind="ExternalInput").ap()
    out = nc.dram_tensor("out", (N, D), F32, kind="ExternalOutput").ap()
    build(nc, args, out)
    r = run_bass_kernel_spmd(nc, [arrays], core_ids=[0])
    return r.results[0]["out"]
```

```python
import concourse.bass as bass
from concourse import mybir
from concourse.alu_op_type import AluOpType as ALU
from contextlib import ExitStack, contextmanager

F32, F32R, BF16 = mybir.dt.float32, mybir.dt.float32r, mybir.dt.bfloat16
I32, U32 = mybir.dt.int32, mybir.dt.uint32
ACT = mybir.ActivationFunctionType
AX = mybir.AxisListType

P = 128
N, D, E = 10000, 512, 5000
KC = D // P
RELATIONS, BASES = 2, 30
EXPERTS, HID = 16, 64
CAP = 625
LAYERS = 4
GROUP = 256
TILES = GROUP // P
NG = -(-N // GROUP)
REST = N - (NG - 1) * GROUP
ET = -(-E // P)
EP = ET * P
EPS = 1e-5
MAGIC = 1.5 * 2.0 ** 23
NO_ROW = float(1 << 20)


def wait(eng, sem, value):
    if not isinstance(value, int) or value > 0:
        eng.wait_ge(sem, value)


def pipeline(eng, stages, count=NG, short_last=True, ways=2):
    deepest = max(lag for lag, _ in stages)
    first = deepest + ways
    turns = (count - int(short_last) - first) // ways

    def peeled(r):
        for lag, step in stages:
            g = r - lag
            if 0 <= g < count:
                step(g, g // ways, g % ways, short_last and g == count - 1)

    for r in range(first):
        peeled(r)
    with eng.Fori(0, turns) as i:
        for u in range(ways):
            for lag, step in stages:
                b = first + u - lag
                step(i * ways + b, i + b // ways, b % ways, False)
    for r in range(first + ways * turns, count + deepest):
        peeled(r)


def wait_apart(eng, sem, value):
    wait(eng, sem, value)
    if not isinstance(value, int):
        eng.nop(nofuse=True)


def tiles_of(last):
    return [(0, REST)] if last else [(t, P) for t in range(TILES)]


def width_of(last):
    return REST if last else GROUP


def rows(dram, g, last):
    if last:
        return dram[g * GROUP:g * GROUP + REST, :].rearrange("(t p) d -> p t d", t=1)
    return dram[bass.ds(g * GROUP, GROUP), :].rearrange("(t p) d -> p t d", p=P)


def part(tile, last):
    return tile[0:REST, 0:1, :] if last else tile[:, :, :]


class Core:

    BANK, INDEXED = 56, 10

    def __init__(self, nc):
        self.nc = nc
        self.sems = [nc.alloc_semaphore(name=f"phase_sem{i}") for i in range(self.BANK)]
        self.indexed = [nc.alloc_semaphore(name=f"indexed_sem{i}") for i in range(self.INDEXED)]
        self.phases = 0

    @staticmethod
    def span(names, sems):
        first = sems[names[0]].num
        assert [sems[n].num for n in names] == list(range(first, first + len(names)))
        return range(first, first + len(names))

    @contextmanager
    def phase(self, name, sem_names):
        names = sem_names.split()
        own = [n for n in names if not n.startswith("sw")]
        indexed = [n for n in names if n.startswith("sw")]
        assert len(own) <= self.BANK and len(indexed) <= self.INDEXED and len(set(names)) == len(names), name
        sems = {**dict(zip(own, self.sems)), **dict(zip(indexed, self.indexed))}
        self.phases += 1
        name = f"{name}{self.phases}"
        with ExitStack() as memory:
            def sbuf(n, shape, dt=F32):
                return memory.enter_context(self.nc.sbuf_tensor(f"{name}_{n}", shape, dt))

            def psum(n, shape, dt=F32):
                return memory.enter_context(self.nc.psum_tensor(f"{name}_{n}", shape, dt))

            yield sems, sbuf, psum
            self.nc.all_engine_barrier()
            if indexed:
                self.nc.gpsimd.dma_reset(self.span(indexed, sems))
                self.nc.gpsimd.sem_clear(self.span(indexed, sems))
            self.nc.gpsimd.sem_clear(self.span(own, sems))
            self.nc.all_engine_barrier()


def row_norm(eng, x, y, mv, rs, last):
    for t, n in tiles_of(last):
        done = eng.tensor_scalar(y[0:n, t, :], x[0:n, t, :], mv[0:n, t, 0:1], rs[0:n, t:t + 1],
                                 ALU.subtract, ALU.mult)
    return done


def row_stats(eng, s, g, x, bn, mv, last, negated=None):
    for t, n in tiles_of(last):
        done = eng.bn_stats(bn[0:n, t, :], x[0:n, t, :])
    done.then_inc(s["stats"], 1)
    wait_apart(eng, s["stats"], g + 1)
    for t, n in tiles_of(last):
        done = eng.bn_aggr(mv[0:n, t, :], bn[0:n, t, :])
    done.then_inc(s["aggr"], 1)
    eng.wait_ge(s["aggr"], g + 1)
    n = REST if last else P
    k = 1 if last else TILES
    if negated is not None:
        eng.tensor_scalar(negated[0:n, 0:k], mv[0:n, 0:k, 0], -1.0, None, ALU.mult)
    eng.tensor_scalar(mv[0:n, 0:k, 1], mv[0:n, 0:k, 1], EPS, None, ALU.add).then_inc(s["var"], 1)


def row_rstd(eng, s, g, mv, half, rs, last):
    eng.wait_ge(s["var"], g + 1)
    n = REST if last else P
    k = 1 if last else TILES
    eng.tensor_tensor(rs[0:n, 0:k], mv[0:n, 0:k, 1], half[0:n, 0:k], ALU.pow).then_inc(s["rstd"], 1)


HI = 80
KEYS = 2
PAD_NODE = N
ROWS = NG * GROUP


def ds1(i):
    return slice(i, i + 1) if isinstance(i, int) else bass.ds(i, 1)


class Edges:

    def __init__(self, nc):
        def sbuf(n, dt=F32):
            return [nc.alloc_sbuf_tensor(f"edge_{n}{k}", [P, ET], dt) for k in range(KEYS)]

        self.key, self.kind, self.weight = sbuf("key"), sbuf("kind"), sbuf("weight")
        self.partner, self.target = sbuf("partner", U32), sbuf("target", U32)
        self.table = [nc.dram_tensor(f"edge_table{k}", (EP, 4), F32).ap() for k in range(KEYS)]
        self.key_row = [nc.dram_tensor(f"edge_key_row{k}", (EP + P,), F32).ap() for k in range(KEYS)]
        self.sums = [nc.dram_tensor(f"edge_sums{k}", (ROWS, D), F32).ap() for k in range(KEYS)]


def order_phase(core, ed, cst, src, dst, kind, weight, rows_in, normed):
    nc = core.nc
    W = 4
    assert ET == NG
    names = ("ld0 ld1 ld2 ld3 st0 st1 st2 st3 stats aggr var rstd norm "
             "ints rows hilo shift keyrow hirow hot hist histc scan roll off base put "
             "count tile look ohT val rank made zero zdone fin1 fin2 fin3 wide "
             "pk0 pk1 pk2 pk3 sw0 sw1 sw2 sw3 sw4 sw5 sw6 sw7")
    with core.phase("order", names) as (s, sbuf, psum):
        load_i = sbuf("load_i", [P, 5, ET], I32)
        col = sbuf("col", [P, 5, ET])
        hl_i = sbuf("hl_i", [P, KEYS, 2, ET], I32)
        hl = sbuf("hl", [P, KEYS, 2, ET])
        wt = sbuf("wt", [P, ET])
        packed = sbuf("packed", [P, KEYS, ET, 4])
        row_i = [sbuf(f"row_i{k}", [P, EP], I32) for k in range(KEYS)]
        key_row = [sbuf(f"key_row{k}", [P, EP]) for k in range(KEYS)]
        hi_row = [sbuf(f"hi_row{k}", [HI, EP]) for k in range(KEYS)]
        hot_hi = [sbuf(f"hot_hi{k}", [P, ET, HI], BF16) for k in range(KEYS)]
        hot_lo = [sbuf(f"hot_lo{k}", [P, ET, P], BF16) for k in range(KEYS)]
        cnt = sbuf("cnt", [HI, KEYS, P])
        incl = sbuf("incl", [HI, KEYS, P])
        ohT = [sbuf(f"ohT{q}", [HI, KEYS, P]) for q in range(2)] * 2
        place = [sbuf(f"place{q}", [HI, KEYS, P]) for q in range(W)]
        junk = [sbuf(f"junk{q}", [P, KEYS, 2, P]) for q in range(2)] * 2
        part_n = [sbuf(f"part_n{q}", [P, KEYS, 2]) for q in range(2)] * 2
        rank = sbuf("rank", [P, KEYS, ET])
        rank_i = sbuf("rank_i", [P, KEYS, ET], I32)
        rr_i = sbuf("rr_i", [P, 2, KEYS, ET], I32)
        rr = sbuf("rr", [P, 2, KEYS, ET])
        slot = sbuf("slot", [P, KEYS, ET], U32)
        pk = [sbuf(f"pk{q}", [P, KEYS, 4]) for q in range(W)]
        ix = [sbuf(f"ix{q}", [P, KEYS], U32) for q in range(W)]
        zeros = sbuf("zeros", [P, 2, D])
        tab = sbuf("tab", [P, KEYS, ET, 4])
        lineT = sbuf("lineT", [ET, KEYS, P])
        nextT = sbuf("nextT", [ET, KEYS, P])
        same = sbuf("same", [P, KEYS, ET])
        minus = sbuf("minus", [1, P])
        x = [sbuf(f"x{q}", [P, TILES, D]) for q in range(W)]
        bn = [sbuf(f"bn{q}", [P, TILES, 6]) for q in range(W)]
        mv = [sbuf(f"mv{q}", [P, TILES, 2]) for q in range(W)]
        rs = [sbuf(f"rs{q}", [P, TILES]) for q in range(W)]
        ld, st = ([s[f"{n}{q}"] for q in range(W)] for n in ("ld", "st"))
        h_ps = psum("h_ps", [HI, KEYS, P])
        o_ps = psum("o_ps", [HI, KEYS])
        c_ps = [psum(f"c_ps{q}", [HI, KEYS, P]) for q in range(2)] * 2
        l_ps = [psum(f"l_ps{q}", [P, KEYS, P]) for q in range(2)] * 2
        t_ps = psum("t_ps", [P, KEYS, P])
        key_in = (src, dst)
        pk_s, sc_s = [s[f"pk{q}"] for q in range(W)], [[s[f"sw{q * KEYS + k}"] for k in range(KEYS)] for q in range(W)]
        USED = E // ET
        assert USED * ET == E

        with nc.Block() as block:
            @block.gpsimd
            def _(eng):
                eng.memset(load_i[:, 0:2, :], PAD_NODE)
                eng.memset(load_i[:, 2, :], RELATIONS)
                eng.memset(load_i[:, 3:5, :], 0)
                eng.memset(wt[:, :], 0.0)
                for k in range(KEYS):
                    eng.memset(row_i[k][:, E:EP], PAD_NODE)
                eng.memset(minus[:, :], -1.0)
                eng.memset(zeros[:, :, :], 0.0).then_inc(s["made"], 1)

                def scatter(t, h, q, last):
                    wait_apart(eng, pk_s[q], h + 1)
                    for k in range(KEYS):
                        eng.indirect_dma_start(ed.table[k], bass.IndirectOffsetOnAxis(ap=ix[q][:, k:k + 1], axis=0),
                                               pk[q][:, k, :], None).then_inc(sc_s[q][k], 16)
                pipeline(eng, [(0, lambda g, h, q, last: row_rstd(eng, s, g, mv[q], cst.half, rs[q], last)), (0, scatter)], ways=W)

            @block.sync
            def _(eng):
                eng.wait_ge(s["made"], 1)
                for j, a in enumerate((src, dst, kind, src, dst)):
                    eng.dma_start(load_i[0:USED, j, :], a.rearrange("(p t) -> p t", t=ET)).then_inc(s["ints"], 16)
                eng.dma_start(wt[0:USED, :], weight.rearrange("(p t) one -> p (t one)", t=ET)).then_inc(s["ints"], 16)
                for k in range(KEYS):
                    eng.dma_start(row_i[k][:, 0:E], key_in[k].partition_broadcast(P)).then_inc(s["rows"], 16)
                for k in range(KEYS):
                    eng.dma_start(ed.key_row[k].rearrange("(a n) -> a n", a=1)[:, EP:EP + P], minus[:, :]).then_inc(s["fin1"], 16)

                def clear(g, h, q, last):
                    eng.dma_start(ed.sums[0][bass.ds(g * GROUP, GROUP), :].rearrange("(t p) d -> p t d", p=P),
                                  zeros[:, :, :]).then_inc(s["zdone"], 16)
                with eng.Fori(0, NG) as g:
                    clear(g, 0, 0, False)

                def load(g, h, q, last):
                    wait_apart(eng, st[q], h * 16)
                    eng.dma_start(part(x[q], last), rows(rows_in, g, last)).then_inc(ld[q], 16)
                pipeline(eng, [(0, load)], ways=W)
                for q in range(W):
                    for k in range(KEYS):
                        eng.wait_ge(sc_s[q][k], 16 * (ET // W))
                for k in range(KEYS):
                    eng.dma_start(tab[:, k, :, :], ed.table[k].rearrange("(p t) c -> p t c", t=ET)).then_inc(s["fin2"], 16)
                eng.wait_ge(s["wide"], 1)
                for k in range(KEYS):
                    eng.dma_start(ed.key_row[k].rearrange("(t p) -> t p", p=P)[0:ET, :], lineT[:, k, :]).then_inc(s["fin1"], 16)
                eng.wait_ge(s["fin1"], 16 * 2 * KEYS)
                for k in range(KEYS):
                    eng.dma_start(nextT[:, k, :], ed.key_row[k][1:EP + 1].rearrange("(t p) -> t p", p=P)).then_inc(s["fin3"], 16)
                eng.wait_ge(s["zdone"], 16 * NG)

            @block.scalar
            def _(eng):
                def store(g, h, q, last):
                    eng.wait_ge(s["norm"], g + 1)
                    eng.dma_start(rows(normed, g, last), part(x[q], last)).then_inc(st[q], 16)
                pipeline(eng, [(0, store)], ways=W)
                for q in range(W):
                    eng.wait_ge(st[q], 16 * (NG // W))

            @block.vector
            def _(eng):
                eng.wait_ge(s["ints"], 96)
                eng.tensor_copy(col[:, :, :], load_i[:, :, :])
                for k in range(KEYS):
                    eng.tensor_scalar(hl_i[:, k, 0, :], load_i[:, k, :], 7, None, ALU.logical_shift_right)
                    m = eng.tensor_scalar(hl_i[:, k, 1, :], load_i[:, k, :], P - 1, None, ALU.bitwise_and)
                m.then_inc(s["hilo"], 1)
                eng.wait_ge(s["hilo"], 1)
                eng.tensor_copy(hl[:, :, :, :], hl_i[:, :, :, :]).then_inc(s["hilo"], 1)
                eng.wait_ge(s["hilo"], 2)
                for k in range(KEYS):
                    for t0 in range(0, ET, ET // 2):
                        ts = slice(t0, t0 + ET // 2)
                        for hot, part_, w in ((hot_hi, 0, HI), (hot_lo, 1, P)):
                            m = eng.tensor_tensor(hot[k][:, ts, :], cst.iota[:, 0:w].unsqueeze(1).to_broadcast([P, ET // 2, w]),
                                                  hl[:, k, part_, ts].unsqueeze(2).to_broadcast([P, ET // 2, w]), ALU.is_equal)
                m.then_inc(s["hot"], 1)
                for k in range(KEYS):
                    for c, j in ((0, k), (1, 4 - k), (2, 2)):
                        eng.tensor_copy(packed[:, k, :, c], col[:, j, :])
                    eng.tensor_copy(packed[:, k, :, 3], wt[:, :])
                eng.wait_ge(s["rows"], 32)
                for k in range(KEYS):
                    eng.tensor_copy(key_row[k][:, :], row_i[k][:, :]).then_inc(s["keyrow"], 1)
                eng.wait_ge(s["keyrow"], 2)
                for k in range(KEYS):
                    eng.tensor_scalar(row_i[k][0:HI, :], row_i[k][0:HI, :], 7, None, ALU.logical_shift_right).then_inc(s["shift"], 1)
                    eng.wait_ge(s["shift"], k + 1)
                    eng.tensor_copy(hi_row[k][:, :], row_i[k][0:HI, :]).then_inc(s["hirow"], 1)
                eng.wait_ge(s["hist"], 1)
                eng.tensor_copy(cnt[:, :, :], h_ps[:, :, :]).then_inc(s["histc"], 1)
                eng.wait_ge(s["histc"], 1)
                for k in range(KEYS):
                    m = eng.tensor_tensor_scan(incl[:, k, :], cnt[:, k, :], cnt[:, k, :], 0.0, ALU.add, ALU.bypass)
                m.then_inc(s["scan"], 1)
                eng.wait_ge(s["scan"], 1)
                eng.wait_ge(s["off"], 1)
                eng.tensor_tensor(incl[:, :, :], incl[:, :, :], cnt[:, :, :], ALU.subtract).then_inc(s["base"], 1)
                eng.wait_ge(s["base"], 1)
                eng.tensor_tensor(place[0][:, :, :], incl[:, :, :], o_ps[:, :].unsqueeze(2).to_broadcast([HI, KEYS, P]),
                                  ALU.add).then_inc(s["put"], 1)
                eng.wait_ge(s["hirow"], 2)

                def columns(t, k):
                    return key_row[k].ap().rearrange("a (p t) -> a t p", t=ET)[:, ds1(t), :].rearrange("a one p -> a (one p)")

                def spread(t, h, q, last):
                    wait(eng, s["look"], t - 1)
                    for k in range(KEYS):
                        v = hi_row[k].ap().rearrange("a (p t) -> a t p", t=ET)[:, ds1(t), :].rearrange("a one p -> a (one p)")
                        m = eng.tensor_scalar(ohT[q][:, k, :], v, cst.index[0:HI, :], None, ALU.is_equal)
                    m.then_inc(s["ohT"], 1)

                def ranks(t, h, q, last):
                    eng.wait_ge(s["look"], t + 1)
                    for k in range(KEYS):
                        eng.scalar_tensor_tensor(junk[q][:, k, 0, :], l_ps[q][:, k, :], 1.0,
                                                 hot_lo[k].ap()[:, ds1(t), :].rearrange("a one p -> a (one p)"),
                                                 ALU.mult, ALU.mult, accum_out=part_n[q][:, k, 0:1])
                        m = eng.scalar_tensor_tensor(junk[q][:, k, 1, :], columns(t, k), col[:, k, ds1(t)], cst.before[:, :],
                                                     ALU.is_equal, ALU.mult, accum_out=part_n[q][:, k, 1:2])
                    m.then_inc(s["val"], 1)
                    eng.wait_ge(s["val"], t + 1)
                    eng.tensor_tensor(rank[:, :, ds1(t)], part_n[q][:, :, 0:1], part_n[q][:, :, 1:2], ALU.add).then_inc(s["rank"], 1)

                def advance(t, h, q, last):
                    eng.wait_ge(s["tile"], t + 1)
                    eng.wait_ge(s["put"], t + 1)
                    wait(eng, s["look"], t - W + 2)
                    eng.tensor_tensor(place[(q + 1) % W][:, :, :], place[q][:, :, :], c_ps[q][:, :, :], ALU.add).then_inc(s["put"], 1)
                pipeline(eng, [(0, spread), (2, ranks), (0, advance)], count=ET, short_last=False, ways=W)
                eng.wait_ge(s["rank"], ET)
                eng.tensor_copy(rank_i[:, :, :], rank[:, :, :]).then_inc(s["rank"], 1)
                eng.wait_ge(s["rank"], ET + 1)
                eng.tensor_scalar(rr_i[:, 0, :, :], rank_i[:, :, :], 7, None, ALU.logical_shift_right)
                eng.tensor_scalar(rr_i[:, 1, :, :], rank_i[:, :, :], P - 1, None, ALU.bitwise_and).then_inc(s["rank"], 1)
                eng.wait_ge(s["rank"], ET + 2)
                eng.tensor_copy(rr[:, :, :, :], rr_i[:, :, :, :]).then_inc(s["rank"], 1)
                eng.wait_ge(s["rank"], ET + 3)
                eng.scalar_tensor_tensor(slot[:, :, :], rr[:, 1, :, :], float(ET), rr[:, 0, :, :], ALU.mult, ALU.add).then_inc(s["rank"], 1)
                eng.wait_ge(s["rank"], ET + 4)

                def pack(t, h, q, last):
                    for k in range(KEYS):
                        wait(eng, sc_s[q][k], h * 16)
                    eng.tensor_copy(pk[q][:, :, :], packed[:, :, ds1(t), :].rearrange("a k one c -> a (k one) c"))
                    eng.tensor_copy(ix[q][:, :], slot[:, :, ds1(t)].rearrange("a k one -> a (k one)")).then_inc(pk_s[q], 1)

                def stats(g, h, q, last):
                    eng.wait_ge(ld[q], (h + 1) * 16)
                    row_stats(eng, s, g, x[q], bn[q], mv[q], last)

                def norm(g, h, q, last):
                    eng.wait_ge(s["rstd"], g + 1)
                    row_norm(eng, x[q], x[q], mv[q], rs[q], last).then_inc(s["norm"], 1)
                pipeline(eng, [(0, pack), (0, stats), (1, norm)], ways=W)
                eng.wait_ge(s["fin2"], 32)
                for k in range(KEYS):
                    for c, dst_ in enumerate((ed.key[k], ed.partner[k], ed.kind[k], ed.weight[k])):
                        m = eng.tensor_copy(dst_[:, :], tab[:, k, :, c])
                m.then_inc(s["count"], 1)
                eng.wait_ge(s["count"], 2)
                eng.tensor_copy(lineT[:, :, :], t_ps[0:ET, :, :]).then_inc(s["wide"], 1)
                eng.wait_ge(s["count"], 3)
                for k in range(KEYS):
                    m = eng.tensor_tensor(same[:, k, :], ed.key[k][:, :], t_ps[:, k, 0:ET], ALU.is_equal)
                m.then_inc(s["roll"], 1)
                eng.wait_ge(s["roll"], 1)
                for k in range(KEYS):
                    eng.scalar_tensor_tensor(ed.target[k][:, :], same[:, k, :], NO_ROW, ed.key[k][:, :], ALU.mult, ALU.add)

            @block.tensor
            def _(eng):
                eng.wait_ge(s["hot"], 1)
                for k in range(KEYS):
                    def hist(t, start, stop):
                        return eng.matmul(h_ps[:, k, :], hot_hi[k].ap()[:, ds1(t), :].rearrange("a one p -> a (one p)"),
                                          hot_lo[k].ap()[:, ds1(t), :].rearrange("a one p -> a (one p)"), start=start, stop=stop)
                    hist(0, True, False)
                    with eng.Fori(1, ET - 1) as t:
                        hist(t, False, False)
                    m = hist(ET - 1, False, True)
                m.then_inc(s["hist"], 1)
                eng.wait_ge(s["scan"], 1)
                for k in range(KEYS):
                    m = eng.matmul(o_ps[:, k:k + 1], cst.after[0:HI, 0:HI], incl[:, k, P - 1:P], start=True, stop=True)
                m.then_inc(s["off"], 1)

                def counts(t, h, q, last):
                    wait(eng, s["put"], t)
                    for k in range(KEYS):
                        m = eng.matmul(c_ps[q][:, k, :], hot_hi[k].ap()[:, ds1(t), :].rearrange("a one p -> a (one p)"),
                                       hot_lo[k].ap()[:, ds1(t), :].rearrange("a one p -> a (one p)"), start=True, stop=True)
                    m.then_inc(s["tile"], 1)

                def look(t, h, q, last):
                    wait(eng, s["val"], t - 1)
                    eng.wait_ge(s["ohT"], t + 1)
                    eng.wait_ge(s["put"], t + 1)
                    for k in range(KEYS):
                        m = eng.matmul(l_ps[q][:, k, :], ohT[q][:, k, :], place[q][:, k, :], start=True, stop=True)
                    m.then_inc(s["look"], 1)
                pipeline(eng, [(0, counts), (1, look)], count=ET, short_last=False, ways=W)
                eng.wait_ge(s["count"], 1)
                for k in range(KEYS):
                    m = eng.transpose(t_ps[0:ET, k, :], ed.key[k][:, :], cst.ident[:, :])
                m.then_inc(s["count"], 1)
                eng.wait_ge(s["fin3"], 32)
                eng.wait_ge(s["wide"], 1)
                for k in range(KEYS):
                    m = eng.transpose(t_ps[:, k, 0:ET], nextT[:, k, :], cst.ident[0:ET, 0:ET])
                m.then_inc(s["count"], 1)


class Constants:

    def __init__(self, core, early):
        nc = core.nc

        def early_sbuf(n, shape, dt=F32):
            return early.enter_context(nc.sbuf_tensor(f"cst_{n}", shape, dt))

        def sbuf(n, shape, dt=F32):
            return nc.alloc_sbuf_tensor(f"cst_{n}", shape, dt)

        self.half = sbuf("half", [P, KC])
        self.ident = sbuf("ident", [P, P])
        self.ident_b = sbuf("ident_b", [P, P], BF16)
        self.last_row = sbuf("last_row", [P, 1])
        self.iota = early_sbuf("iota", [P, P])
        self.index = early_sbuf("index", [P, 1])
        self.before = early_sbuf("before", [P, P])
        self.after = early_sbuf("after", [P, P])
        with core.phase("const", "a b") as (s, _, _), nc.Block() as block:
            @block.gpsimd
            def _(eng):
                eng.memset(self.half[:, :], -0.5)
                eng.iota(self.iota[:, :], [[1, P]], base=0, channel_multiplier=0, allow_small_or_imprecise_dtypes=True)
                eng.iota(self.index[:, :], [[1, 1]], base=0, channel_multiplier=1, allow_small_or_imprecise_dtypes=True).then_inc(s["a"], 1)

            @block.vector
            def _(eng):
                eng.wait_ge(s["a"], 1)
                for m, op in ((self.before, ALU.is_lt), (self.after, ALU.is_gt), (self.ident, ALU.is_equal),
                              (self.ident_b, ALU.is_equal)):
                    eng.tensor_scalar(m[:, :], self.iota[:, :], self.index[:, :], None, op)
                eng.tensor_scalar(self.last_row[:, :], self.index[:, :], float(P - 1), None, ALU.is_equal)


class Split:

    def __init__(self, s, raw, value, hi, lo):
        self.s, self.raw, self.value, self.hi, self.lo = s, raw, value, hi, lo

    def load(self, eng):
        eng.dma_start(self.raw[:, :, :], self.value).then_inc(self.s["w"], 16)

    def high(self, eng):
        eng.wait_ge(self.s["w"], 16)
        eng.activation(self.hi[:, :, :], self.raw[:, :, :], ACT.Copy).then_inc(self.s["whi"], 1)

    def low(self, eng):
        eng.wait_ge(self.s["whi"], 1)
        eng.tensor_tensor(self.lo[:, :, :], self.raw[:, :, :], self.hi[:, :, :].bitcast(F32), ALU.subtract).then_inc(self.s["wlo"], 1)


def chunked(w):
    return w.rearrange("(c p) n -> p c n", p=P)


def combine_phase(core, cst, basis, att, w_hi, w_lo):
    nc = core.nc
    W = 4
    TE = KC - 1
    with core.phase("combine", "att ld0 ld1 ld2 ld3 diag te ve hi lo") as (s, sbuf, psum):
        b_t = [sbuf(f"basis{q}", [P, KC, D]) for q in range(W)]
        att_t = sbuf("att", [P, RELATIONS * BASES])
        diag = [sbuf(f"diag{q}", [P, P]) for q in range(W)]
        acc = sbuf("acc", [P, KC + 1, D])
        rest = psum("rest", [P, TE, D])
        ld = [s[f"ld{q}"] for q in range(W)]
        with nc.Block() as block:
            @block.sync
            def _(eng):
                eng.dma_start(att_t[:, :], att.rearrange("r b -> (r b)").partition_broadcast(P)).then_inc(s["att"], 16)

                def load(b, h, q, last):
                    wait(eng, s["te"], b - W + 1)
                    wait(eng, s["ve"], b - W + 1)
                    eng.dma_start(b_t[q][:, :, :], chunked(basis[ds1(b), :, :].rearrange("one i o -> (one i) o"))).then_inc(ld[q], 16)
                pipeline(eng, [(0, load)], count=BASES, short_last=False, ways=W)

            @block.scalar
            def _(eng):
                eng.wait_ge(s["att"], 16)

                def diagonal(b, h, q, last):
                    wait(eng, s["te"], b - W + 1)
                    a = BASES + b
                    eng.activation(diag[q][:, :], cst.ident[:, :], ACT.Copy, scale=att_t[:, ds1(a)]).then_inc(s["diag"], 1)
                pipeline(eng, [(0, diagonal)], count=BASES, short_last=False, ways=W)
                eng.wait_ge(s["ve"], BASES)
                eng.activation(w_hi[:, 0:KC, :], acc[:, 0:KC, :], ACT.Copy)
                eng.activation(w_hi[:, 2 * KC - 1, :], acc[:, KC, :], ACT.Copy)
                eng.wait_ge(s["te"], BASES)
                eng.activation(w_hi[:, KC:KC + TE, :], rest[:, :, :], ACT.Copy).then_inc(s["hi"], 1)

            @block.vector
            def _(eng):
                eng.memset(acc[:, :, :], 0.0).then_inc(s["lo"], 1)
                eng.wait_ge(s["lo"], 1)
                eng.wait_ge(s["att"], 16)

                def add(b, h, q, last):
                    eng.wait_ge(ld[q], (h + 1) * 16)
                    wait(eng, s["ve"], b)
                    eng.scalar_tensor_tensor(acc[:, 0:KC, :], b_t[q][:, :, :], att_t[:, ds1(b)], acc[:, 0:KC, :], ALU.mult, ALU.add)
                    a = BASES + b
                    eng.scalar_tensor_tensor(acc[:, KC, :], b_t[q][:, TE, :], att_t[:, ds1(a)], acc[:, KC, :],
                                             ALU.mult, ALU.add).then_inc(s["ve"], 1)
                pipeline(eng, [(0, add)], count=BASES, short_last=False, ways=W)
                eng.wait_ge(s["hi"], 1)
                eng.tensor_tensor(w_lo[:, 0:KC, :], acc[:, 0:KC, :], w_hi[:, 0:KC, :].bitcast(F32), ALU.subtract)
                eng.tensor_tensor(w_lo[:, 2 * KC - 1, :], acc[:, KC, :], w_hi[:, 2 * KC - 1, :].bitcast(F32), ALU.subtract)
                eng.tensor_tensor(w_lo[:, KC:KC + TE, :], rest[:, :, :], w_hi[:, KC:KC + TE, :].bitcast(F32), ALU.subtract)

            @block.tensor
            def _(eng):
                def term(b, h, q, last):
                    eng.wait_ge(ld[q], (h + 1) * 16)
                    eng.wait_ge(s["diag"], b + 1)
                    for c in range(TE):
                        m = eng.matmul(rest[:, c, :], diag[q][:, :], b_t[q][:, c, :],
                                       start=isinstance(b, int) and b == 0, stop=isinstance(b, int) and b == BASES - 1)
                    m.then_inc(s["te"], 1)
                pipeline(eng, [(0, term)], count=BASES, short_last=False, ways=W)


def three(eng, out, a_hi, a_lo, b_hi, b_lo, start, stop):
    eng.matmul(out, a_hi, b_hi, start=start, stop=False)
    eng.matmul(out, a_lo, b_hi, start=False, stop=False)
    return eng.matmul(out, a_hi, b_lo, start=False, stop=stop)


def relation_phase(core, cst, ed, table, gate_w, w_hi, w_lo, root, clear):
    nc = core.nc
    W = 4
    names = ("w whi wlo gw krow mask zeroed clear hk hix ends ix swg0 swg1 swg2 swg3 z sig copy lo coef ch sel A pth ptl B res tix hd H hres "
             "sws0 sws1 sws2 sws3")
    with core.phase("relation", names) as (s, sbuf, psum):
        gw = sbuf("gw", [P, RELATIONS, D])
        krow = sbuf("krow", [P, EP])
        mask = sbuf("mask", [P, RELATIONS, ET])
        ix = [sbuf(f"ix{q}", [P, 1], U32) for q in range(W)]
        tix = [sbuf(f"tix{q}", [P, 1], U32) for q in range(W)]
        x = [sbuf(f"x{q}", [P, D]) for q in range(W)]
        xh = [sbuf(f"xh{q}", [P, D], F32R) for q in range(W)]
        xl = [sbuf(f"xl{q}", [P, D], F32R) for q in range(W)]
        junk = [sbuf(f"junk{q}", [P, RELATIONS, D]) for q in range(W)]
        z = [sbuf(f"z{q}", [P, RELATIONS]) for q in range(W)]
        sig = [sbuf(f"sig{q}", [P, RELATIONS]) for q in range(W)]
        cf = [sbuf(f"cf{q}", [P, RELATIONS]) for q in range(W)]
        ch = [sbuf(f"ch{q}", [P, RELATIONS], F32R) for q in range(W)]
        cl = [sbuf(f"cl{q}", [P, RELATIONS]) for q in range(W)]
        sh = [sbuf(f"sh{q}", [P, RELATIONS, P], F32R) for q in range(W)]
        sl = [sbuf(f"sl{q}", [P, RELATIONS, P], F32R) for q in range(W)]
        hd = [sbuf(f"hd{q}", [P, ET]) for q in range(W)]
        zeros = sbuf("zeros", [P, TILES, D])
        split = Split(s, sbuf("root_raw", [P, KC, D]), *root)
        ends = sbuf("ends", [P, ET])
        hkey = sbuf("hkey", [ET, 2])
        hsame = sbuf("hsame", [ET, 1])
        hix = sbuf("hix", [ET, 1], U32)
        hres = sbuf("hres", [ET, D])
        pth = [sbuf(f"pth{q}", [P, KC, RELATIONS, P], F32R) for q in range(2)]
        ptl = [sbuf(f"ptl{q}", [P, KC, RELATIONS, P], F32R) for q in range(2)]
        res = [sbuf(f"res{q}", [P, D]) for q in range(W)]
        A = [psum(f"A{q}", [P, KC, RELATIONS, P]) for q in range(2)]
        B = [psum(f"B{q}", [P, D]) for q in range(2)]
        H = psum("H", [ET, D])
        heads = krow.ap().rearrange("a (t p) -> a p t", p=P)[:, 0, :]
        ga, sc = [s[f"swg{q}"] for q in range(W)], [s[f"sws{q}"] for q in range(W)]

        def run(eng, *stages):
            pipeline(eng, stages, count=ET, short_last=False, ways=W)

        with nc.Block() as block:
            @block.sync
            def _(eng):
                eng.dma_start(krow[:, :], ed.key_row[0][0:EP].partition_broadcast(P)).then_inc(s["krow"], 16)
                eng.dma_start(gw[:, :, :], gate_w.rearrange("r i one -> (r i one)").partition_broadcast(P)
                              .rearrange("a (r i) -> a r i", r=RELATIONS)).then_inc(s["gw"], 16)
                for j in range(2):
                    eng.dma_start(hkey[:, j:j + 1], ed.key_row[0][j * P:j * P + EP].rearrange("(t p) -> t p", p=P)[:, 0:1],
                                  allow_slow_non_contiguous=True).then_inc(s["hk"], 16)

                split.load(eng)
                def zero_rows(g, h, q, last):
                    wait_apart(eng, s["sel"], g)
                    eng.dma_start(clear[bass.ds(g * GROUP, GROUP), :].rearrange("(t p) d -> p t d", p=P),
                                  zeros[:, :, :]).then_inc(s["clear"], 16)
                if clear is not None:
                    assert NG == ET
                    eng.wait_ge(s["zeroed"], 1)
                    run(eng, (0, zero_rows))
                    eng.wait_ge(s["clear"], 16 * NG)

            @block.gpsimd
            def _(eng):
                eng.memset(zeros[:, :, :], 0.0).then_inc(s["zeroed"], 1)

                def gather(t, h, q, last):
                    wait(eng, s["lo"], t - W + 1)
                    wait(eng, s["z"], t - W + 1)
                    wait_apart(eng, s["ix"], t + 1)
                    eng.indirect_dma_start(x[q][:, :], None, table, bass.IndirectOffsetOnAxis(ap=ix[q][:, :], axis=0)).then_inc(ga[q], 16)

                def scatter(t, h, q, last):
                    eng.wait_ge(s["tix"], t + 1)
                    wait_apart(eng, s["res"], t + 1)
                    eng.indirect_dma_start(ed.sums[0], bass.IndirectOffsetOnAxis(ap=tix[q][:, :], axis=0), res[q][:, :], None,
                                           bounds_check=ROWS - 1, oob_is_err=False).then_inc(sc[q], 16)
                run(eng, (0, gather), (4, scatter))
                for q in range(W):
                    eng.wait_ge(sc[q], 16 * (ET // W))
                eng.wait_ge(s["hres"], 1)
                eng.indirect_dma_start(ed.sums[0], bass.IndirectOffsetOnAxis(ap=hix[:, :], axis=0), hres[:, :], None,
                                       bounds_check=ROWS - 1, oob_is_err=False).then_inc(sc[0], 16)
                eng.wait_ge(sc[0], 16 * (ET // W) + 16)

            @block.vector
            def _(eng):
                for r in range(RELATIONS):
                    if r == 0:
                        m = eng.tensor_scalar(mask[:, 0, :], ed.kind[0][:, :], 0.0, None, ALU.is_equal)
                    else:
                        m = eng.tensor_scalar(mask[:, 1, :], ed.kind[0][:, :], 0.0, None, ALU.not_equal)
                m.then_inc(s["mask"], 1)
                eng.wait_ge(s["hk"], 32)
                eng.tensor_tensor(hsame[:, :], hkey[:, 0:1], hkey[:, 1:2], ALU.is_equal).then_inc(s["hix"], 1)
                eng.wait_ge(s["hix"], 1)
                eng.scalar_tensor_tensor(hix[:, :], hsame[:, :], NO_ROW, hkey[:, 0:1], ALU.mult, ALU.add).then_inc(s["hix"], 1)
                eng.tensor_scalar(ends[:, :], ed.target[0][:, :], NO_ROW, cst.last_row[:, :], ALU.is_lt, ALU.max).then_inc(s["ends"], 1)

                def index(t, h, q, last):
                    wait(eng, ga[q], h * 16)
                    eng.tensor_copy(ix[q][:, :], ed.partner[0][:, ds1(t)]).then_inc(s["ix"], 1)

                def gates(t, h, q, last):
                    eng.wait_ge(ga[q], (h + 1) * 16)
                    wait(eng, s["sig"], t - W + 1)
                    for r in range(RELATIONS):
                        m = eng.scalar_tensor_tensor(junk[q][:, r, :], x[q][:, :], 1.0, gw[:, r, :], ALU.mult, ALU.mult,
                                                     accum_out=z[q][:, r:r + 1])
                    m.then_inc(s["z"], 1)
                    eng.wait_ge(s["copy"], t + 1)
                    wait(eng, s["A"], t - W + 1)
                    eng.tensor_tensor(xl[q][:, :], x[q][:, :], xh[q][:, :].bitcast(F32), ALU.subtract).then_inc(s["lo"], 1)

                def select(t, h, q, last):
                    eng.wait_ge(s["sig"], t + 1)
                    eng.tensor_tensor(cf[q][:, :], sig[q][:, :], mask[:, :, ds1(t)].rearrange("a r one -> a (r one)"),
                                      ALU.mult).then_inc(s["coef"], 1)
                    wait(eng, s["H"], t - W + 1)
                    eng.tensor_scalar(hd[q][:, :], heads, ed.key[0][:, ds1(t)], ends[:, ds1(t)], ALU.is_equal, ALU.mult).then_inc(s["hd"], 1)
                    wait(eng, sc[q], h * 16)
                    eng.tensor_copy(tix[q][:, :], ed.target[0][:, ds1(t)]).then_inc(s["tix"], 1)
                    eng.wait_ge(s["coef"], t + 1)
                    eng.tensor_copy(ch[q][:, :], cf[q][:, :]).then_inc(s["ch"], 1)
                    eng.wait_ge(s["ch"], t * 2 + 1)
                    eng.tensor_tensor(cl[q][:, :], cf[q][:, :], ch[q][:, :].bitcast(F32), ALU.subtract).then_inc(s["ch"], 1)
                    eng.wait_ge(s["ch"], t * 2 + 2)
                    for r in range(RELATIONS):
                        eng.tensor_scalar(sh[q][:, r, :], krow[:, bass.ts(t, P)], ed.key[0][:, ds1(t)],
                                          ch[q][:, r:r + 1].bitcast(F32), ALU.is_equal, ALU.mult)
                        m = eng.tensor_scalar(sl[q][:, r, :], krow[:, bass.ts(t, P)], ed.key[0][:, ds1(t)],
                                              cl[q][:, r:r + 1], ALU.is_equal, ALU.mult)
                    m.then_inc(s["sel"], 1)

                def low(t, h, q, last):
                    eng.wait_ge(s["pth"], t + 1)
                    eng.tensor_tensor(ptl[q % 2][:, :, :, :], A[q % 2][:, :, :, :], pth[q % 2][:, :, :, :].bitcast(F32),
                                      ALU.subtract).then_inc(s["ptl"], 1)
                eng.wait_ge(s["krow"], 16)
                eng.wait_ge(s["gw"], 16)
                eng.wait_ge(s["mask"], 1)
                eng.wait_ge(s["ends"], 1)
                run(eng, (0, index), (1, gates), (2, select), (3, low))
                split.low(eng)
                eng.wait_ge(s["H"], ET)
                eng.wait_ge(s["hix"], 2)
                eng.tensor_copy(hres[:, :], H[:, :]).then_inc(s["hres"], 1)

            @block.scalar
            def _(eng):
                def copy(t, h, q, last):
                    eng.wait_ge(ga[q], (h + 1) * 16)
                    wait(eng, s["A"], t - W + 1)
                    eng.activation(xh[q][:, :], x[q][:, :], ACT.Copy).then_inc(s["copy"], 1)
                    eng.wait_ge(s["z"], t + 1)
                    wait(eng, s["coef"], t - W + 1)
                    eng.activation(sig[q][:, :], z[q][:, :], ACT.Sigmoid).then_inc(s["sig"], 1)

                def high(t, h, q, last):
                    eng.wait_ge(s["A"], t + 1)
                    wait(eng, s["B"], t - 1)
                    eng.activation(pth[q % 2][:, :, :, :], A[q % 2][:, :, :, :], ACT.Copy).then_inc(s["pth"], 1)

                def result(t, h, q, last):
                    eng.wait_ge(s["B"], t + 1)
                    wait(eng, sc[q], h * 16)
                    wait(eng, s["H"], t - W + 1)
                    eng.activation(res[q][:, :], B[q % 2][:, :], ACT.Copy).then_inc(s["res"], 1)
                run(eng, (1, copy), (3, high), (4, result))
                split.high(eng)

            @block.tensor
            def _(eng):
                def sums(t, h, q, last):
                    eng.wait_ge(s["lo"], t + 1)
                    eng.wait_ge(s["sel"], t + 1)
                    wait(eng, s["ptl"], t - 1)
                    for c in range(KC):
                        cs = slice(c * P, (c + 1) * P)
                        m = three(eng, A[q % 2][:, c, :, :], xh[q][:, cs], xl[q][:, cs], sh[q][:, :, :], sl[q][:, :, :], True, True)
                    m.then_inc(s["A"], 1)

                def product(t, h, q, last):
                    eng.wait_ge(s["ptl"], t + 1)
                    wait(eng, s["res"], t - 1)
                    for r in range(RELATIONS):
                        for c in range(KC):
                            m = three(eng, B[q % 2][:, :], pth[q % 2][:, c, r, :], ptl[q % 2][:, c, r, :], w_hi[:, r * KC + c, :],
                                      w_lo[:, r * KC + c, :], r == 0 and c == 0, r == RELATIONS - 1 and c == KC - 1)
                    m.then_inc(s["B"], 1)

                def head(t, h, q, last):
                    eng.wait_ge(s["res"], t + 1)
                    eng.wait_ge(s["hd"], t + 1)
                    eng.matmul(H[:, :], hd[q][:, :], res[q][:, :], start=isinstance(t, int) and t == 0,
                               stop=isinstance(t, int) and t == ET - 1).then_inc(s["H"], 1)
                run(eng, (2, sums), (3, product), (4, head))


def root_phase(core, cst, ed, rows_in, root, bias, half, rows_out, skip=None, normed=None):
    nc = core.nc
    fin = skip is not None
    root_hi, root_lo = root
    names = ("bias ld0 ld1 la0 la1 lx0 lx1 T hi lo M pa pb pc y r st0 st1 sn0 sn1 stats aggr var rstd norm")
    with core.phase("root", names) as (s, sbuf, psum):
        bt = sbuf("bias", [P, D])
        xin = [sbuf(f"xin{q}", [P, TILES, D]) for q in range(2)]
        agg = [sbuf(f"agg{q}", [P, TILES, D]) for q in range(2)]
        skp = [sbuf(f"skp{q}", [P, TILES, D]) for q in range(2)] if fin else None
        xh = [sbuf(f"xh{q}", [P, KC, GROUP], F32R) for q in range(2)]
        xl = [sbuf(f"xl{q}", [P, KC, GROUP], F32R) for q in range(2)]
        y = [sbuf(f"y{q}", [P, TILES, D]) for q in range(2)]
        nrm = [sbuf(f"nrm{q}", [P, TILES, D]) for q in range(2)] if fin else None
        bn = [sbuf(f"bn{q}", [P, TILES, 6]) for q in range(2)]
        mv = [sbuf(f"mv{q}", [P, TILES, 2]) for q in range(2)]
        rs = [sbuf(f"rs{q}", [P, TILES]) for q in range(2)]
        T = [psum(f"T{q}", [P, KC, GROUP]) for q in range(2)]
        O = [psum(f"O{q}", [P, TILES, D]) for q in range(2)]
        ld, la, lx = (s["ld0"], s["ld1"]), (s["la0"], s["la1"]), (s["lx0"], s["lx1"])
        st, sn = (s["st0"], s["st1"]), (s["sn0"], s["sn1"])
        with nc.Block() as block:
            @block.sync
            def _(eng):
                eng.dma_start(bt[:, :], bias.partition_broadcast(P)).then_inc(s["bias"], 16)

                def load(g, h, q, last):
                    wait(eng, s["T"], g - 1)
                    eng.dma_start(part(xin[q], last), rows(rows_in, g, last)).then_inc(ld[q], 16)
                    wait(eng, s["y"], g - 1)
                    eng.dma_start(part(agg[q], last), rows(ed.sums[0], g, last)).then_inc(la[q], 16)
                    if fin:
                        eng.dma_start(part(skp[q], last), rows(skip, g, last)).then_inc(lx[q], 16)
                pipeline(eng, [(0, load)])

            @block.tensor
            def _(eng):
                root_T = lambda g, h, q, last: turn(eng, s, g, h, q, last, ld, xin, T, cst.ident)

                def product(g, h, q, last):
                    eng.wait_ge(s["lo"], g + 1)
                    wait(eng, s["y"], g - 1)
                    for t, n in tiles_of(last):
                        ts = slice(t * P, t * P + n)
                        for c in range(KC):
                            m = three(eng, O[q][0:n, t, :], xh[q][:, c, ts], xl[q][:, c, ts], root_hi[:, c, :], root_lo[:, c, :],
                                      c == 0, c == KC - 1)
                    m.then_inc(s["M"], 1)
                pipeline(eng, [(0, root_T), (1, product)])

            @block.gpsimd
            def _(eng):
                def add_bias(g, h, q, last):
                    n = REST if last else P
                    eng.wait_ge(la[q], (h + 1) * 16)
                    k = 1 if last else TILES
                    eng.tensor_tensor(agg[q][0:n, 0:k, :], agg[q][0:n, 0:k, :], bt[0:n, :].unsqueeze(1).to_broadcast([n, k, D]),
                                      ALU.add).then_inc(s["pa"], 1)
                    if fin:
                        eng.wait_ge(lx[q], (h + 1) * 16)
                        eng.wait_ge(s["pa"], g + 1)
                        eng.tensor_tensor(agg[q][0:n, 0:k, :], agg[q][0:n, 0:k, :], skp[q][0:n, 0:k, :], ALU.add).then_inc(s["pb"], 1)
                eng.wait_ge(s["bias"], 16)
                stages = [(0, add_bias)]
                if fin:
                    stages.append((2, lambda g, h, q, last: row_rstd(eng, s, g, mv[q], half, rs[q], last)))
                pipeline(eng, stages)

            @block.scalar
            def _(eng):
                def high(g, h, q, last):
                    split_hi(eng, s, g, q, last, T, xh)

                def finish(g, h, q, last):
                    eng.wait_ge(s["y"], g + 1)
                    if not fin:
                        eng.activation(part(y[q], last), part(y[q], last), ACT.Relu).then_inc(s["r"], 1)
                        eng.wait_ge(s["r"], g + 1)
                    eng.dma_start(rows(rows_out, g, last), part(y[q], last)).then_inc(st[q], 16)
                    if fin:
                        eng.wait_ge(s["norm"], g + 1)
                        eng.dma_start(rows(normed, g, last), part(nrm[q], last)).then_inc(sn[q], 16)
                pipeline(eng, [(0, high), (2, finish)])
                for q in range(2):
                    eng.wait_ge(st[q], 16 * (NG // 2))
                    if fin:
                        eng.wait_ge(sn[q], 16 * (NG // 2))

            @block.vector
            def _(eng):
                def low(g, h, q, last):
                    split_lo(eng, s, g, q, last, T, xh, xl)

                def total(g, h, q, last):
                    eng.wait_ge(s["M"], g + 1)
                    eng.wait_ge(s["pb" if fin else "pa"], g + 1)
                    wait(eng, st[q], h * 16)
                    if fin:
                        wait(eng, s["norm"], g - 1)
                    eng.tensor_tensor(part(y[q], last), part(O[q], last), part(agg[q], last), ALU.add).then_inc(s["y"], 1)
                    if fin:
                        eng.wait_ge(s["y"], g + 1)
                        row_stats(eng, s, g, y[q], bn[q], mv[q], last)

                def norm(g, h, q, last):
                    eng.wait_ge(s["rstd"], g + 1)
                    wait(eng, sn[q], h * 16)
                    row_norm(eng, y[q], nrm[q], mv[q], rs[q], last).then_inc(s["norm"], 1)
                pipeline(eng, [(0, low), (1, total)] + ([(2, norm)] if fin else []))


def turn(eng, s, g, h, q, last, ready, x, T, ident):
    if ready is None:
        eng.wait_ge(s["pre"], g + 1)
    else:
        eng.wait_ge(ready[q], (h + 1) * 16)
    wait(eng, s["lo"], g - 1)
    for t, n in tiles_of(last):
        for c in range(KC):
            m = eng.transpose(T[q][:, c, t * P:t * P + n], x[q][0:n, t, c * P:(c + 1) * P], ident[0:n, 0:n])
    m.then_inc(s["T"], 1)


def split_hi(eng, s, g, q, last, T, xh):
    w = width_of(last)
    eng.wait_ge(s["T"], g + 1)
    wait(eng, s["M"], g - 1)
    eng.activation(xh[q][:, :, 0:w], T[q][:, :, 0:w], ACT.Copy).then_inc(s["hi"], 1)


def split_lo(eng, s, g, q, last, T, xh, xl):
    w = width_of(last)
    eng.wait_ge(s["hi"], g + 1)
    eng.tensor_tensor(xl[q][:, :, 0:w], T[q][:, :, 0:w], xh[q][:, :, 0:w].bitcast(F32), ALU.subtract).then_inc(s["lo"], 1)


SUB = P // EXPERTS
SUB_BITS = SUB.bit_length() - 1
LINE = N // SUB
TPE = 5
SL = CAP // TPE
ST = EXPERTS * TPE
BLOCK = 125
NB = N // BLOCK
BITS = 30


def tokens_phase(core, cst, rows_in, residual, gate_w, w1, b1, w2, b2, probs, rows_out):
    nc = core.nc
    K = HID + 1
    M = HID + EXPERTS
    W = 4
    names = ("w whi wlo ld0 ld1 ld2 ld3 lr0 lr1 lr2 lr3 T hi lo hm act gh gl M y st0 st1 st2 st3 one "
             "LT L mx sub exp sum rec pr pt ptc st")
    with core.phase("tokens", names) as (s, sbuf, psum):
        def ring(n, shape, dt=F32):
            return [sbuf(f"{n}{q}", shape, dt) for q in range(2)] * 2

        xin, rsd, y = ([sbuf(f"{n}{q}", [P, TILES, D]) for q in range(W)] for n in ("xin", "rsd", "y"))
        xh, xl = ring("xh", [P, KC, GROUP], F32R), ring("xl", [P, KC, GROUP], F32R)
        w1r, w1h, w1l = (sbuf(n, [P, KC, M], dt) for n, dt in (("w1r", F32), ("w1h", F32R), ("w1l", F32R)))
        w2r, w2h, w2l = (sbuf(n, [K, D], dt) for n, dt in (("w2r", F32), ("w2h", F32R), ("w2l", F32R)))
        b1r = sbuf("b1r", [HID, 1])
        act, gh, gl = ring("act", [K, GROUP]), ring("gh", [K, GROUP], F32R), ring("gl", [K, GROUP], F32R)
        lt = ring("lt", [EXPERTS, GROUP])
        mx, sm, rc = (ring(n, [P, TILES]) for n in ("mx", "sm", "rc"))
        lg, ex, pr = (ring(n, [P, TILES, EXPERTS]) for n in ("lg", "ex", "pr"))
        pT = sbuf("pT", [EXPERTS, NG * GROUP])
        T = psum("T", [P, KC, GROUP])
        Hp = [psum(f"Hp{q}", [M, 512]) for q in range(2)] * 2
        O = psum("O", [P, TILES, D])
        L = psum("L", [P, TILES, EXPERTS])
        Q = psum("Q", [EXPERTS, GROUP])
        ld, lr, st = ([s[f"{n}{q}"] for q in range(W)] for n in ("ld", "lr", "st"))
        with nc.Block() as block:
            @block.sync
            def _(eng):
                eng.dma_start(w1r[:, :, 0:HID], chunked(w1)).then_inc(s["w"], 16)
                eng.dma_start(w1r[:, :, HID:M], chunked(gate_w)).then_inc(s["w"], 16)
                eng.dma_start(w2r[0:HID, :], w2).then_inc(s["w"], 16)
                eng.dma_start(w2r[HID:K, :], b2.unsqueeze(0)).then_inc(s["w"], 16)
                eng.dma_start(b1r[:, :], b1.unsqueeze(1)).then_inc(s["w"], 16)

                def load(g, h, q, last):
                    wait_apart(eng, s["T"], g - W + 1)
                    eng.dma_start(part(xin[q], last), rows(rows_in, g, last)).then_inc(ld[q], 16)

                def load_residual(g, h, q, last):
                    wait_apart(eng, s["y"], g - W + 1)
                    eng.dma_start(part(rsd[q], last), rows(residual, g, last)).then_inc(lr[q], 16)
                pipeline(eng, [(0, load), (1, load_residual)], ways=W)
                eng.wait_ge(s["ptc"], NG)
                eng.dma_start(probs, pT[:, 0:N]).then_inc(s["st"], 16)
                eng.wait_ge(s["st"], 16)

            @block.tensor
            def _(eng):
                def turn_rows(g, h, q, last):
                    eng.wait_ge(ld[q], (h + 1) * 16)
                    wait(eng, s["lo"], g)
                    for t, n in tiles_of(last):
                        for c in range(KC):
                            m = eng.transpose(T[:, c, t * P:t * P + n], xin[q][0:n, t, c * P:(c + 1) * P], cst.ident[0:n, 0:n])
                    m.then_inc(s["T"], 1)

                def up(g, h, q, last):
                    w_ = width_of(last)
                    eng.wait_ge(s["lo"], g + 1)
                    wait(eng, s["act"], g - 1)
                    wait(eng, s["LT"], g - 1)
                    for c in range(KC):
                        m = three(eng, Hp[q][:, 0:w_], w1h[:, c, :], w1l[:, c, :], xh[q][:, c, 0:w_], xl[q][:, c, 0:w_], c == 0, c == KC - 1)
                    m.then_inc(s["hm"], 1)

                def down(g, h, q, last):
                    eng.wait_ge(s["gl"], g + 1)
                    wait(eng, s["y"], g)
                    for t, n in tiles_of(last):
                        ts = slice(t * P, t * P + n)
                        m = three(eng, O[0:n, t, :], gh[q][:, ts], gl[q][:, ts], w2h[:, :], w2l[:, :], True, True)
                    m.then_inc(s["M"], 1)

                def turn_logits(g, h, q, last):
                    eng.wait_ge(s["LT"], g + 1)
                    wait_apart(eng, s["sub"], g)
                    for t, n in tiles_of(last):
                        m = eng.transpose(L[0:n, t, :], lt[q][:, t * P:t * P + n], cst.ident[0:EXPERTS, 0:EXPERTS])
                    m.then_inc(s["L"], 1)

                def turn_probs(g, h, q, last):
                    eng.wait_ge(s["pr"], g + 1)
                    wait(eng, s["ptc"], g)
                    for t, n in tiles_of(last):
                        m = eng.transpose(Q[:, t * P:t * P + n], pr[q][0:n, t, :], cst.ident[0:n, 0:n])
                    m.then_inc(s["pt"], 1)
                eng.wait_ge(s["wlo"], 1)
                pipeline(eng, [(0, turn_rows), (3, turn_logits), (6, turn_probs), (3, down), (1, up)], ways=W)

            @block.scalar
            def _(eng):
                def high(g, h, q, last):
                    w_ = width_of(last)
                    eng.wait_ge(s["T"], g + 1)
                    wait(eng, s["hm"], g - 1)
                    eng.activation(xh[q][:, :, 0:w_], T[:, :, 0:w_], ACT.Copy).then_inc(s["hi"], 1)

                def acts(g, h, q, last):
                    w_ = width_of(last)
                    eng.wait_ge(s["hm"], g + 1)
                    wait(eng, s["gl"], g - 1)
                    eng.activation(act[q][0:HID, 0:w_], Hp[q][0:HID, 0:w_], ACT.Gelu_apprx_tanh, bias=b1r[:, :]).then_inc(s["act"], 1)
                    eng.wait_ge(s["act"], g + 1)
                    wait(eng, s["M"], g - 1)
                    eng.activation(gh[q][:, 0:w_], act[q][:, 0:w_], ACT.Copy).then_inc(s["gh"], 1)

                def copy_logits(g, h, q, last):
                    w = width_of(last)
                    eng.wait_ge(s["hm"], g + 1)
                    wait(eng, s["L"], g - 1)
                    eng.activation(lt[q][:, 0:w], Hp[q][HID:M, 0:w], ACT.Copy).then_inc(s["LT"], 1)

                def exps(g, h, q, last):
                    n, k = (REST, 1) if last else (P, TILES)
                    eng.wait_ge(s["sub"], g + 1)
                    wait(eng, s["pr"], g - 1)
                    eng.activation(ex[q][0:n, 0:k, :], lg[q][0:n, 0:k, :], ACT.Exp).then_inc(s["exp"], 1)

                def out(g, h, q, last):
                    wait_apart(eng, s["pt"], g + 1)
                    w = width_of(last)
                    at = slice(g * GROUP, g * GROUP + w) if isinstance(g, int) else bass.ds(g * GROUP, w)
                    eng.activation(pT[:, at], Q[:, 0:w], ACT.Copy).then_inc(s["ptc"], 1)

                def store(g, h, q, last):
                    eng.wait_ge(s["y"], g + 1)
                    eng.dma_start(rows(rows_out, g, last), part(y[q], last)).then_inc(st[q], 16)
                eng.wait_ge(s["w"], 80)
                eng.activation(w1h[:, :, :], w1r[:, :, :], ACT.Copy)
                eng.activation(w2h[:, :], w2r[:, :], ACT.Copy).then_inc(s["whi"], 1)
                eng.wait_ge(s["one"], 1)
                pipeline(eng, [(0, high), (2, copy_logits), (2, acts), (4, exps), (6, out), (5, store)], ways=W)
                for q in range(W):
                    eng.wait_ge(st[q], 16 * (NG // W))

            @block.vector
            def _(eng):
                def low(g, h, q, last):
                    w_ = width_of(last)
                    eng.wait_ge(s["hi"], g + 1)
                    eng.tensor_tensor(xl[q][:, :, 0:w_], T[:, :, 0:w_], xh[q][:, :, 0:w_].bitcast(F32), ALU.subtract).then_inc(s["lo"], 1)

                def low_units(g, h, q, last):
                    w_ = width_of(last)
                    eng.wait_ge(s["gh"], g + 1)
                    eng.tensor_tensor(gl[q][:, 0:w_], act[q][:, 0:w_], gh[q][:, 0:w_].bitcast(F32), ALU.subtract).then_inc(s["gl"], 1)

                def total(g, h, q, last):
                    eng.wait_ge(s["M"], g + 1)
                    eng.wait_ge(lr[q], (h + 1) * 16)
                    wait(eng, st[q], h * 16)
                    eng.tensor_tensor(part(y[q], last), part(O, last), part(rsd[q], last), ALU.add).then_inc(s["y"], 1)

                def shift(g, h, q, last):
                    n, k = (REST, 1) if last else (P, TILES)
                    eng.wait_ge(s["L"], g + 1)
                    eng.tensor_reduce(mx[q][0:n, 0:k], L[0:n, 0:k, :], AX.X, ALU.max).then_inc(s["mx"], 1)
                    eng.wait_ge(s["mx"], g + 1)
                    wait(eng, s["exp"], g - 1)
                    eng.tensor_tensor(lg[q][0:n, 0:k, :], L[0:n, 0:k, :], mx[q][0:n, 0:k].unsqueeze(2).to_broadcast([n, k, EXPERTS]),
                                      ALU.subtract).then_inc(s["sub"], 1)

                def divide(g, h, q, last):
                    n, k = (REST, 1) if last else (P, TILES)
                    eng.wait_ge(s["exp"], g + 1)
                    eng.tensor_reduce(sm[q][0:n, 0:k], ex[q][0:n, 0:k, :], AX.X, ALU.add).then_inc(s["sum"], 1)
                    eng.wait_ge(s["sum"], g + 1)
                    eng.reciprocal(rc[q][0:n, 0:k], sm[q][0:n, 0:k]).then_inc(s["rec"], 1)
                    eng.wait_ge(s["rec"], g + 1)
                    wait(eng, s["pt"], g - 1)
                    eng.tensor_tensor(pr[q][0:n, 0:k, :], ex[q][0:n, 0:k, :], rc[q][0:n, 0:k].unsqueeze(2).to_broadcast([n, k, EXPERTS]),
                                      ALU.mult).then_inc(s["pr"], 1)
                for q in range(2):
                    m = eng.memset(act[q][HID:K, :], 1.0)
                m.then_inc(s["one"], 1)
                eng.wait_ge(s["whi"], 1)
                eng.tensor_tensor(w1l[:, :, :], w1r[:, :, :], w1h[:, :, :].bitcast(F32), ALU.subtract)
                eng.tensor_tensor(w2l[:, :], w2r[:, :], w2h[:, :].bitcast(F32), ALU.subtract).then_inc(s["wlo"], 1)
                pipeline(eng, [(4, total), (4, shift), (0, low), (5, divide), (2, low_units)], ways=W)


def select_phase(core, cst, probs, table, ends):
    nc = core.nc
    names = "ld blk ibit cand cnt tot keep th gt eq sc tg off need okr pick count val rank st one"
    with core.phase("select", names) as (s, sbuf, psum):
        p = sbuf("p", [P, LINE])
        same = sbuf("same", [P, P])
        prior = sbuf("prior", [P, P])
        grp = sbuf("grp", [P, P])
        grp_i = sbuf("grp_i", [P, P], I32)
        own_i = sbuf("own_i", [P, 1], I32)
        own = sbuf("own", [P, 1])
        thr = [sbuf(f"thr{q}", [P, 1], I32) for q in range(2)]
        cand = [sbuf(f"cand{q}", [P, 1], I32) for q in range(2)]
        cnt = [sbuf(f"cnt{q}", [P, 1]) for q in range(2)]
        junk = [sbuf(f"junk{q}", [P, LINE]) for q in range(2)]
        gt = sbuf("gt", [P, LINE])
        eq = sbuf("eq", [P, LINE])
        scan = sbuf("scan", [P, LINE])
        need = sbuf("need", [P, 2])
        before = sbuf("before", [P, 1])
        last = sbuf("last", [P, LINE // BLOCK])
        two = sbuf("two", [P, 2])
        tot = [psum(f"tot{q}", [P, 1]) for q in range(2)]
        off = psum("off", [P, 2])
        sums = psum("sums", [P, 1])
        with nc.Block() as block:
            @block.sync
            def _(eng):
                eng.dma_start(p[:, :], probs.rearrange("e (k n) -> (e k) n", k=SUB)).then_inc(s["ld"], 16)
                lines = table.rearrange("(a b) w -> a b w", a=P)
                eng.wait_ge(s["val"], 1)
                eng.dma_start(lines[:, :, BLOCK:2 * BLOCK], eq.ap().rearrange("a (b n) -> a b n", n=BLOCK)).then_inc(s["st"], 16)
                eng.wait_ge(s["rank"], 1)
                eng.dma_start(lines[:, :, 0:BLOCK], scan.ap().rearrange("a (b n) -> a b n", n=BLOCK)).then_inc(s["st"], 16)
                eng.dma_start(ends.rearrange("(a b) -> a b", a=P), last[:, :]).then_inc(s["st"], 16)
                eng.wait_ge(s["st"], 48)

            @block.gpsimd
            def _(eng):
                eng.iota(grp_i[:, :], [[1, P]], base=0, channel_multiplier=0)
                eng.iota(own_i[:, :], [[1, 1]], base=0, channel_multiplier=1).then_inc(s["ibit"], 1)

            @block.tensor
            def _(eng):
                eng.wait_ge(s["blk"], 1)
                for b in range(BITS):
                    q = b % 2
                    eng.wait_ge(s["cnt"], b + 1)
                    eng.matmul(tot[q][:, :], same[:, :], cnt[q][:, :], start=True, stop=True).then_inc(s["tot"], 1)
                eng.wait_ge(s["tg"], 1)
                eng.matmul(sums[:, :], same[:, :], two[:, 0:1], start=True, stop=True)
                eng.matmul(off[:, 0:1], prior[:, :], two[:, 1:2], start=True, stop=True).then_inc(s["off"], 1)
                eng.wait_ge(s["tg"], 2)
                eng.matmul(off[:, 1:2], prior[:, :], two[:, 1:2], start=True, stop=True).then_inc(s["off"], 1)

            @block.vector
            def _(eng):
                eng.wait_ge(s["ibit"], 1)
                eng.tensor_scalar(grp_i[:, :], grp_i[:, :], SUB_BITS, None, ALU.logical_shift_right)
                eng.tensor_scalar(own_i[:, :], own_i[:, :], SUB_BITS, None, ALU.logical_shift_right)
                eng.memset(thr[0][:, :], 0).then_inc(s["one"], 1)
                eng.wait_ge(s["one"], 1)
                eng.tensor_copy(grp[:, :], grp_i[:, :])
                eng.tensor_copy(own[:, :], own_i[:, :]).then_inc(s["one"], 1)
                eng.wait_ge(s["one"], 2)
                eng.tensor_scalar(same[:, :], grp[:, :], own[:, :], None, ALU.is_equal).then_inc(s["one"], 1)
                eng.wait_ge(s["one"], 3)
                eng.tensor_tensor(prior[:, :], same[:, :], cst.after[:, :], ALU.mult).then_inc(s["blk"], 1)
                eng.wait_ge(s["ld"], 16)
                for b in range(BITS):
                    q = b % 2
                    wait(eng, s["th"], b)
                    eng.tensor_scalar(cand[q][:, :], thr[q][:, :], 1 << (BITS - 1 - b), None, ALU.bitwise_or).then_inc(s["cand"], 1)
                    eng.wait_ge(s["cand"], b + 1)
                    eng.tensor_scalar(junk[q][:, :], p[:, :], cand[q][:, :].bitcast(F32), 0.0, ALU.is_ge, ALU.add,
                                      accum_out=cnt[q][:, :]).then_inc(s["cnt"], 1)
                    eng.wait_ge(s["tot"], b + 1)
                    eng.scalar_tensor_tensor(two[:, 0:1], tot[q][:, :], float(CAP), cand[q][:, :].bitcast(F32),
                                             ALU.is_ge, ALU.mult).then_inc(s["keep"], 1)
                    eng.wait_ge(s["keep"], b + 1)
                    eng.tensor_tensor(thr[1 - q][:, :].bitcast(F32), two[:, 0:1], thr[q][:, :].bitcast(F32), ALU.max).then_inc(s["th"], 1)
                border = thr[BITS % 2][:, :].bitcast(F32)
                eng.wait_ge(s["th"], BITS)
                eng.tensor_scalar(gt[:, :], p[:, :], border, 0.0, ALU.is_gt, ALU.add, accum_out=two[:, 0:1])
                eng.tensor_scalar(eq[:, :], p[:, :], border, None, ALU.is_equal).then_inc(s["gt"], 1)
                eng.wait_ge(s["gt"], 1)
                eng.tensor_tensor_scan(scan[:, :], eq[:, :], eq[:, :], 0.0, ALU.add, ALU.bypass).then_inc(s["sc"], 1)
                eng.wait_ge(s["sc"], 1)
                eng.tensor_copy(two[:, 1:2], scan[:, LINE - 1:LINE]).then_inc(s["tg"], 1)
                eng.wait_ge(s["off"], 1)
                eng.tensor_scalar(need[:, 0:1], sums[:, :], -1.0, float(CAP), ALU.mult, ALU.add).then_inc(s["need"], 1)
                eng.wait_ge(s["need"], 1)
                eng.tensor_tensor(need[:, 1:2], need[:, 0:1], off[:, 0:1], ALU.subtract).then_inc(s["need"], 1)
                eng.wait_ge(s["need"], 2)
                eng.scalar_tensor_tensor(eq[:, :], scan[:, :], need[:, 1:2], eq[:, :], ALU.is_le, ALU.mult).then_inc(s["okr"], 1)
                eng.wait_ge(s["okr"], 1)
                eng.tensor_tensor(gt[:, :], gt[:, :], eq[:, :], ALU.add).then_inc(s["pick"], 1)
                eng.wait_ge(s["pick"], 1)
                eng.tensor_tensor_scan(scan[:, :], gt[:, :], gt[:, :], 0.0, ALU.add, ALU.bypass).then_inc(s["count"], 1)
                eng.tensor_tensor(eq[:, :], gt[:, :], p[:, :], ALU.mult).then_inc(s["val"], 1)
                eng.wait_ge(s["count"], 1)
                eng.tensor_copy(two[:, 1:2], scan[:, LINE - 1:LINE]).then_inc(s["tg"], 1)
                eng.wait_ge(s["off"], 2)
                eng.tensor_copy(before[:, :], off[:, 1:2]).then_inc(s["count"], 1)
                eng.wait_ge(s["count"], 2)
                eng.tensor_scalar(last[:, :], scan.ap().rearrange("a (b n) -> a n b", n=BLOCK)[:, BLOCK - 1, :], before[:, :], None, ALU.add).then_inc(s["count"], 1)
                eng.wait_ge(s["count"], 3)
                eng.tensor_scalar(scan[:, :], scan[:, :], before[:, :], None, ALU.add).then_inc(s["rank"], 1)


def slots_phase(core, table, ends, token, score):
    nc = core.nc
    W = 4
    names = "io r ends cmp blk row ix swr0 swr1 swr2 swr3 cnt put tok"
    with core.phase("slots", names) as (s, sbuf, psum):
        r_i = sbuf("r_i", [SL, ST], I32)
        r0 = sbuf("r0", [SL, ST])
        r1 = sbuf("r1", [SL, ST])
        row0_i = sbuf("row0_i", [SL, ST], I32)
        row0 = sbuf("row0", [SL, ST])
        end = sbuf("end", [SL, EXPERTS, NB])
        cmp = [sbuf(f"cmp{i}", [SL, EXPERTS, NB]) for i in range(TPE)]
        blk = sbuf("blk", [SL, EXPERTS, TPE])
        row = sbuf("row", [SL, ST], U32)
        ix = [sbuf(f"ix{q}", [SL, 1], U32) for q in range(W)]
        line = [sbuf(f"line{q}", [SL, 2 * BLOCK]) for q in range(W)]
        junk = [sbuf(f"junk{q}", [SL, 2, BLOCK]) for q in range(W)]
        found = [sbuf(f"found{q}", [SL, 2]) for q in range(W)]
        both = sbuf("both", [SL, 2, ST])
        ga = [s[f"swr{q}"] for q in range(W)]
        blk_flat = blk.ap().rearrange("a e i -> a (e i)")

        def run(eng, *stages):
            pipeline(eng, stages, count=ST, short_last=False, ways=W)

        with nc.Block() as block:
            @block.sync
            def _(eng):
                eng.dma_start(end[:, :, :], ends.partition_broadcast(SL).rearrange("a (e b) -> a e b", e=EXPERTS)).then_inc(s["ends"], 16)

            @block.gpsimd
            def _(eng):
                eng.iota(r_i[:, :], [[0, EXPERTS], [SL, TPE]], base=0, channel_multiplier=1)
                eng.iota(row0_i[:, :], [[NB, EXPERTS], [0, TPE]], base=0, channel_multiplier=0).then_inc(s["io"], 1)

                def gather(t, h, q, last):
                    wait(eng, s["cnt"], t - W + 1)
                    wait_apart(eng, s["ix"], t + 1)
                    eng.indirect_dma_start(line[q][:, :], None, table, bass.IndirectOffsetOnAxis(ap=ix[q][:, :], axis=0)).then_inc(ga[q], 16)
                run(eng, (0, gather))

            @block.vector
            def _(eng):
                eng.wait_ge(s["io"], 1)
                eng.tensor_copy(r0[:, :], r_i[:, :])
                eng.tensor_copy(row0[:, :], row0_i[:, :]).then_inc(s["r"], 1)
                eng.wait_ge(s["r"], 1)
                eng.tensor_scalar(r1[:, :], r0[:, :], 1.0, None, ALU.add).then_inc(s["r"], 1)
                eng.wait_ge(s["ends"], 16)
                for i in range(TPE):
                    eng.tensor_scalar(cmp[i][:, :, :], end[:, :, :], r0[:, i:i + 1], None, ALU.is_le).then_inc(s["cmp"], 1)
                for i in range(TPE):
                    eng.wait_ge(s["cmp"], i + 1)
                    m = eng.tensor_reduce(blk[:, :, i], cmp[i][:, :, :], AX.X, ALU.add)
                m.then_inc(s["blk"], 1)
                eng.wait_ge(s["blk"], 1)
                eng.tensor_tensor(row[:, :], blk_flat, row0[:, :], ALU.add).then_inc(s["row"], 1)
                eng.wait_ge(s["row"], 1)
                eng.wait_ge(s["r"], 2)

                def index(t, h, q, last):
                    wait(eng, ga[q], h * 16)
                    eng.tensor_copy(ix[q][:, :], row[:, ds1(t)]).then_inc(s["ix"], 1)

                def find(t, h, q, last):
                    eng.wait_ge(ga[q], (h + 1) * 16)
                    wait(eng, s["put"], t - W + 1)
                    eng.tensor_scalar(junk[q][:, 0, :], line[q][:, 0:BLOCK], r0[:, ds1(t)], 0.0, ALU.is_le, ALU.add,
                                      accum_out=found[q][:, 0:1])
                    eng.scalar_tensor_tensor(junk[q][:, 1, :], line[q][:, 0:BLOCK], r1[:, ds1(t)], line[q][:, BLOCK:2 * BLOCK],
                                             ALU.is_equal, ALU.mult, accum_out=found[q][:, 1:2]).then_inc(s["cnt"], 1)

                def put(t, h, q, last):
                    eng.wait_ge(s["cnt"], t + 1)
                    eng.tensor_copy(both[:, :, ds1(t)].rearrange("a c one -> a (c one)"), found[q][:, :]).then_inc(s["put"], 1)
                run(eng, (0, index), (3, find), (4, put))
                eng.wait_ge(s["put"], ST)
                eng.tensor_copy(score[:, :], both[:, 1, :])
                eng.scalar_tensor_tensor(token[:, :], blk_flat, float(BLOCK), both[:, 0, :], ALU.mult, ALU.add)


def routed_phase(core, cst, rows_in, w1, b1, w2, b2, token, score, routed):
    nc = core.nc
    R = 2
    K = HID + 1
    HALF = SL * TPE // 2 + 2 - SL * TPE // 2 % 2
    names = ("w whi wlo ix T hi lo hm act gh gl one O ev "
             + " ".join(f"swg{i}" for i in range(TPE)) + " " + " ".join(f"sws{i}" for i in range(TPE)))
    with core.phase("routed", names) as (s, sbuf, psum):
        def ring(n, shape, dt=F32):
            return [sbuf(f"{n}{q}", shape, dt) for q in range(R)] * 2

        w1r, w1h, w1l = ring("w1r", [P, KC, HID]), ring("w1h", [P, KC, HID], F32R), ring("w1l", [P, KC, HID], F32R)
        w2r, w2h, w2l = ring("w2r", [K, D]), ring("w2h", [K, D], F32R), ring("w2l", [K, D], F32R)
        b1r = ring("b1r", [HID, 1])
        ix = [sbuf(f"ix{q}", [SL, TPE], U32) for q in range(4)]
        sc = [sbuf(f"sc{q}", [SL, TPE]) for q in range(4)]
        x = ring("x", [SL, TPE, D])
        xh, xl = ring("xh", [P, KC, 2 * HALF], F32R), ring("xl", [P, KC, 2 * HALF], F32R)
        act = sbuf("act", [K, 2, HALF])
        gh, gl = sbuf("gh", [K, 2, HALF], F32R), sbuf("gl", [K, 2, HALF], F32R)
        zero = sbuf("zero", [P, KC, 2 * HALF - SL * TPE])
        res = [sbuf(f"res{i}", [SL, D]) for i in range(TPE)]
        T = [psum(f"T{j}", [P, KC, P]) for j in range(3)]
        Hp = psum("Hp", [HID, 2, 512])
        O = [psum(f"O{j}", [SL, D]) for j in range(3)]
        ga, sc_ = [s[f"swg{i}"] for i in range(TPE)], [s[f"sws{i}"] for i in range(TPE)]
        gh_f, gl_f = (v.ap().rearrange("a b n -> a (b n)") for v in (gh, gl))

        def run(eng, *stages):
            pipeline(eng, stages, count=EXPERTS, short_last=False, ways=4)

        def tiles(*stages):
            return [(lag, step(i)) for i in range(TPE) for lag, step in stages]

        def used(i, n):
            return n - 1 if i < 2 else n - 2

        with nc.Block() as block:
            @block.sync
            def _(eng):
                def load(e, h, q, last):
                    wait_apart(eng, s["wlo"], (e - R + 1) * 2)
                    wait_apart(eng, s["act"], e - R + 1)
                    wait_apart(eng, s["whi"], e * 2)
                    eng.dma_start(w1r[q][:, :, :], chunked(w1[ds1(e)].rearrange("one i o -> (one i) o"))).then_inc(s["w"], 16)
                    eng.dma_start(w2r[q][0:HID, :], w2[ds1(e)].rearrange("one i o -> (one i) o")).then_inc(s["w"], 16)
                    eng.dma_start(w2r[q][HID:K, :], b2[ds1(e), :]).then_inc(s["w"], 16)
                    eng.dma_start(b1r[q][:, :], b1[ds1(e), :].rearrange("one h -> h one"), allow_slow_non_contiguous=True).then_inc(s["w"], 16)
                run(eng, (0, load))

            @block.gpsimd
            def _(eng):
                def gather(e, h, q, last):
                    for i in range(TPE):
                        wait(eng, s["T"], (e - 1) * TPE + i + 1)
                        wait_apart(eng, s["ix"], e + 1)
                        eng.indirect_dma_start(x[q][:, i, :], None, rows_in,
                                               bass.IndirectOffsetOnAxis(ap=ix[q][:, i:i + 1], axis=0)).then_inc(ga[i], 16)

                def scatter(e, h, q, last):
                    for i in range(TPE):
                        wait(eng, sc_[i], e * 16)
                    for i in range(TPE):
                        wait_apart(eng, s["ev"], e * TPE + i + 1)
                        eng.indirect_dma_start(routed, bass.IndirectOffsetOnAxis(ap=ix[q][:, i:i + 1], axis=0), res[i][:, :], None,
                                               compute_op=ALU.add).then_inc(sc_[i], 16)
                run(eng, (3, scatter), (0, gather))
                for i in range(TPE):
                    eng.wait_ge(sc_[i], EXPERTS * 16)

            @block.tensor
            def _(eng):
                def turn_slots(i):
                    def step(e, h, q, last):
                        n = e * TPE + i
                        eng.wait_ge(ga[i], (e + 1) * 16)
                        wait(eng, s["lo"], used(i, n))
                        for c in range(KC):
                            m = eng.transpose(T[i % 3][:, c, 0:SL], x[q][:, i, c * P:(c + 1) * P], cst.ident[0:SL, 0:SL])
                        m.then_inc(s["T"], 1)
                    return step

                def up(e, h, q, last):
                    eng.wait_ge(s["lo"], (e + 1) * TPE)
                    eng.wait_ge(s["wlo"], (e + 1) * 2)
                    wait(eng, s["act"], e)
                    for b in range(2):
                        cols = slice(b * HALF, (b + 1) * HALF)
                        for c in range(KC):
                            m = three(eng, Hp[:, b, 0:HALF], w1h[q][:, c, :], w1l[q][:, c, :], xh[q][:, c, cols], xl[q][:, c, cols],
                                      c == 0, c == KC - 1)
                    m.then_inc(s["hm"], 1)

                def down(i):
                    def step(e, h, q, last):
                        n = e * TPE + i
                        eng.wait_ge(s["gl"], e + 1)
                        wait(eng, s["ev"], used(i, n))
                        cols = slice(i * SL, (i + 1) * SL)
                        three(eng, O[i % 3][:, :], gh_f[:, cols], gl_f[:, cols], w2h[q][:, :], w2l[q][:, :], True, True).then_inc(s["O"], 1)
                    return step
                eng.wait_ge(s["one"], 2)
                run(eng, *tiles((1, turn_slots), (2, down)), (1, up))

            @block.scalar
            def _(eng):
                def weights(e, h, q, last):
                    eng.wait_ge(s["w"], (e + 1) * 64)
                    wait(eng, s["O"], (e - R + 1) * TPE)
                    eng.activation(w1h[q][:, :, :], w1r[q][:, :, :], ACT.Copy).then_inc(s["whi"], 1)
                    eng.activation(w2h[q][:, :], w2r[q][:, :], ACT.Copy).then_inc(s["whi"], 1)

                def high(e, h, q, last):
                    wait(eng, s["hm"], e - R + 1)
                    for i in range(TPE):
                        eng.wait_ge(s["T"], e * TPE + i + 1)
                        eng.activation(xh[q][:, :, i * SL:(i + 1) * SL], T[i % 3][:, :, 0:SL], ACT.Copy).then_inc(s["hi"], 1)

                def acts(e, h, q, last):
                    eng.wait_ge(s["hm"], e + 1)
                    wait(eng, s["gl"], e)
                    eng.activation(act[0:HID, :, :], Hp[:, :, 0:HALF], ACT.Gelu_apprx_tanh, bias=b1r[q][:, :]).then_inc(s["act"], 1)
                    eng.wait_ge(s["act"], e + 1)
                    wait(eng, s["O"], e * TPE)
                    eng.activation(gh[:, :, :], act[:, :, :], ACT.Copy).then_inc(s["gh"], 1)
                eng.wait_ge(s["one"], 1)
                for q in range(R):
                    eng.activation(xh[q][:, :, SL * TPE:2 * HALF], zero[:, :, :], ACT.Copy)
                    m = eng.activation(xl[q][:, :, SL * TPE:2 * HALF], zero[:, :, :], ACT.Copy)
                m.then_inc(s["one"], 1)
                run(eng, (1, high), (1, acts), (0, weights))

            @block.vector
            def _(eng):
                def index(e, h, q, last):
                    for i in range(TPE):
                        wait(eng, sc_[i], h * 16)
                    at = slice(e * TPE, e * TPE + TPE) if isinstance(e, int) else bass.ds(e * TPE, TPE)
                    eng.tensor_copy(sc[q][:, :], score[:, at])
                    eng.tensor_copy(ix[q][:, :], token[:, at]).then_inc(s["ix"], 1)

                def weights(e, h, q, last):
                    eng.wait_ge(s["whi"], e * 2 + 1)
                    eng.tensor_tensor(w1l[q][:, :, :], w1r[q][:, :, :], w1h[q][:, :, :].bitcast(F32), ALU.subtract).then_inc(s["wlo"], 1)
                    eng.wait_ge(s["whi"], e * 2 + 2)
                    eng.tensor_tensor(w2l[q][:, :], w2r[q][:, :], w2h[q][:, :].bitcast(F32), ALU.subtract).then_inc(s["wlo"], 1)

                def low(i):
                    def step(e, h, q, last):
                        cols = slice(i * SL, (i + 1) * SL)
                        eng.wait_ge(s["hi"], e * TPE + i + 1)
                        eng.tensor_tensor(xl[q][:, :, cols], T[i % 3][:, :, 0:SL], xh[q][:, :, cols].bitcast(F32), ALU.subtract).then_inc(s["lo"], 1)
                    return step

                def weigh(i):
                    def step(e, h, q, last):
                        eng.wait_ge(s["ix"], e + 1)
                        wait(eng, sc_[i], e * 16)
                        eng.wait_ge(s["O"], e * TPE + i + 1)
                        eng.tensor_scalar(res[i][:, :], O[i % 3][:, :], sc[q][:, i:i + 1], None, ALU.mult).then_inc(s["ev"], 1)
                    return step

                def low_units(e, h, q, last):
                    eng.wait_ge(s["gh"], e + 1)
                    eng.tensor_tensor(gl[:, :, :], act[:, :, :], gh[:, :, :].bitcast(F32), ALU.subtract).then_inc(s["gl"], 1)
                eng.memset(zero[:, :, :], 0.0)
                eng.memset(act[HID:K, :, :], 1.0).then_inc(s["one"], 1)
                run(eng, (0, index), *tiles((1, low), (2, weigh)), (1, low_units), (0, weights))


def norm_phase(core, src, dst, half):
    nc = core.nc
    W = 4
    with core.phase("norm", "ld0 ld1 ld2 ld3 stats aggr var rstd norm st0 st1 st2 st3") as (s, sbuf, _):
        x, y = ([sbuf(f"{n}{q}", [P, TILES, D]) for q in range(W)] for n in ("x", "y"))
        bn = [sbuf(f"bn{q}", [P, TILES, 6]) for q in range(W)]
        mv = [sbuf(f"mv{q}", [P, TILES, 2]) for q in range(W)]
        rs = [sbuf(f"rs{q}", [P, TILES]) for q in range(W)]
        ld, st = ([s[f"{n}{q}"] for q in range(W)] for n in ("ld", "st"))
        with nc.Block() as block:
            @block.sync
            def _(eng):
                def load(g, h, q, last):
                    wait_apart(eng, s["norm"], g - W + 1)
                    eng.dma_start(part(x[q], last), rows(src, g, last)).then_inc(ld[q], 16)
                pipeline(eng, [(0, load)], ways=W)

            @block.vector
            def _(eng):
                def stats(g, h, q, last):
                    eng.wait_ge(ld[q], (h + 1) * 16)
                    row_stats(eng, s, g, x[q], bn[q], mv[q], last)

                def norm(g, h, q, last):
                    eng.wait_ge(s["rstd"], g + 1)
                    wait(eng, st[q], h * 16)
                    row_norm(eng, x[q], y[q], mv[q], rs[q], last).then_inc(s["norm"], 1)
                pipeline(eng, [(0, stats), (1, norm)], ways=W)

            @block.gpsimd
            def _(eng):
                pipeline(eng, [(0, lambda g, h, q, last: row_rstd(eng, s, g, mv[q], half, rs[q], last))], ways=W)

            @block.scalar
            def _(eng):
                def store(g, h, q, last):
                    eng.wait_ge(s["norm"], g + 1)
                    eng.dma_start(rows(dst, g, last), part(y[q], last)).then_inc(st[q], 16)
                pipeline(eng, [(0, store)], ways=W)
                for q in range(W):
                    eng.wait_ge(st[q], 16 * (NG // W))


def layer_of(a, layer):
    v = a[bass.ds(layer, 1)]
    names = " ".join("abc"[:len(a.shape) - 1])
    return v.rearrange(f"one {names} -> (one {names.split()[0]}) {' '.join(names.split()[1:])}")


def message_phase(core, cst, ed, table, We, be, layer, weight):
    nc = core.nc
    W = 4
    names = ("w whi wlo krow we hk hix ix swg0 swg1 swg2 swg3 mix sum mh ml sel tix B res hres head sws0 sws1 sws2 sws3")
    with core.phase("message", names) as (s, sbuf, psum):
        krow = sbuf("krow", [P, EP])
        split = Split(s, sbuf("weight_raw", [P, KC, D]), *weight)
        We_b = sbuf("We", [P, D])
        be_b = sbuf("be", [P, D])
        ix = [sbuf(f"ix{q}", [P, 1], U32) for q in range(W)]
        tix = [sbuf(f"tix{q}", [P, 1], U32) for q in range(W)]
        x = [sbuf(f"x{q}", [P, D]) for q in range(W)]
        y = [sbuf(f"y{q}", [P, D]) for q in range(W)]
        z = [sbuf(f"z{q}", [P, D]) for q in range(W)]
        mh = [sbuf(f"mh{q}", [P, D], F32R) for q in range(W)]
        ml = [sbuf(f"ml{q}", [P, D], F32R) for q in range(W)]
        sel = [sbuf(f"sel{q}", [P, P], F32R) for q in range(W)]
        hd = [sbuf(f"hd{q}", [P, ET], F32R) for q in range(W)]
        hkey = sbuf("hkey", [ET, 2])
        hsame = sbuf("hsame", [ET, 1])
        hix = sbuf("hix", [ET, 1], U32)
        hres = sbuf("hres", [ET, D])
        res = [sbuf(f"res{q}", [P, D]) for q in range(W)]
        B = [psum(f"B{q}", [P, D]) for q in range(2)]
        H = psum("H", [ET, D])
        ga, sc = [s[f"swg{q}"] for q in range(W)], [s[f"sws{q}"] for q in range(W)]

        heads = krow.ap().rearrange("a (t p) -> a p t", p=P)[:, 0, :]

        def run(eng, *stages):
            pipeline(eng, stages, count=ET, short_last=False, ways=W)

        with nc.Block() as block:
            @block.sync
            def _(eng):
                eng.dma_start(krow[:, :], ed.key_row[1][0:EP].partition_broadcast(P)).then_inc(s["krow"], 16)
                eng.dma_start(We_b[:, :], layer_of(We, layer).rearrange("one d -> (one d)").partition_broadcast(P)).then_inc(s["we"], 16)
                eng.dma_start(be_b[:, :], be[bass.ds(layer, 1), :].rearrange("one d -> (one d)").partition_broadcast(P)).then_inc(s["we"], 16)
                for j in range(2):
                    eng.dma_start(hkey[:, j:j + 1], ed.key_row[1][j * P:j * P + EP].rearrange("(t p) -> t p", p=P)[:, 0:1],
                                  allow_slow_non_contiguous=True).then_inc(s["hk"], 16)

                split.load(eng)

            @block.gpsimd
            def _(eng):
                def gather(t, h, q, last):
                    wait(eng, s["mix"], t - W + 1)
                    wait_apart(eng, s["ix"], t + 1)
                    eng.indirect_dma_start(x[q][:, :], None, table, bass.IndirectOffsetOnAxis(ap=ix[q][:, :], axis=0)).then_inc(ga[q], 16)

                def scatter(t, h, q, last):
                    eng.wait_ge(s["tix"], t + 1)
                    wait_apart(eng, s["res"], t + 1)
                    eng.indirect_dma_start(ed.sums[1], bass.IndirectOffsetOnAxis(ap=tix[q][:, :], axis=0), res[q][:, :], None,
                                           bounds_check=ROWS - 1, oob_is_err=False).then_inc(sc[q], 16)
                run(eng, (0, gather), (5, scatter))
                for q in range(W):
                    eng.wait_ge(sc[q], 16 * (ET // W))
                eng.wait_ge(s["hres"], 1)
                eng.indirect_dma_start(ed.sums[1], bass.IndirectOffsetOnAxis(ap=hix[:, :], axis=0), hres[:, :], None,
                                       bounds_check=ROWS - 1, oob_is_err=False).then_inc(sc[0], 16)
                eng.wait_ge(sc[0], 16 * (ET // W) + 16)

            @block.vector
            def _(eng):
                eng.wait_ge(s["krow"], 16)
                eng.wait_ge(s["we"], 32)
                eng.wait_ge(s["hk"], 32)
                eng.tensor_tensor(hsame[:, :], hkey[:, 0:1], hkey[:, 1:2], ALU.is_equal).then_inc(s["hix"], 1)
                eng.wait_ge(s["hix"], 1)
                eng.scalar_tensor_tensor(hix[:, :], hsame[:, :], NO_ROW, hkey[:, 0:1], ALU.mult, ALU.add).then_inc(s["hix"], 1)

                def index(t, h, q, last):
                    wait(eng, ga[q], h * 16)
                    eng.tensor_copy(ix[q][:, :], ed.partner[1][:, ds1(t)]).then_inc(s["ix"], 1)

                def select(t, h, q, last):
                    wait(eng, s["B"], t - W + 1)
                    eng.tensor_scalar(hd[q][:, :], heads, ed.key[1][:, ds1(t)], None, ALU.is_equal).then_inc(s["head"], 1)
                    eng.tensor_scalar(sel[q][:, :], krow[:, bass.ts(t, P)], ed.key[1][:, ds1(t)], None, ALU.is_equal).then_inc(s["sel"], 1)

                def target(t, h, q, last):
                    wait(eng, sc[q], h * 16)
                    eng.tensor_copy(tix[q][:, :], ed.target[1][:, ds1(t)]).then_inc(s["tix"], 1)

                def add(t, h, q, last):
                    eng.wait_ge(ga[q], (h + 1) * 16)
                    eng.scalar_tensor_tensor(y[q][:, :], We_b[:, :], ed.weight[1][:, ds1(t)], x[q][:, :], ALU.mult, ALU.add).then_inc(s["mix"], 1)
                    eng.wait_ge(s["mix"], t + 1)
                    wait(eng, s["ml"], t - W + 1)
                    eng.tensor_tensor(z[q][:, :], y[q][:, :], be_b[:, :], ALU.add).then_inc(s["sum"], 1)

                def low(t, h, q, last):
                    eng.wait_ge(s["mh"], t + 1)
                    wait(eng, s["B"], t - W + 1)
                    eng.scalar_tensor_tensor(ml[q][:, :], z[q][:, :], 0.0, mh[q][:, :].bitcast(F32), ALU.max, ALU.subtract).then_inc(s["ml"], 1)
                run(eng, (0, index), (3, add), (4, low), (3, select), (4, target))
                split.low(eng)
                eng.wait_ge(s["B"], ET)
                eng.wait_ge(s["hix"], 2)
                eng.tensor_copy(hres[:, :], H[:, :]).then_inc(s["hres"], 1)

            @block.scalar
            def _(eng):
                def high(t, h, q, last):
                    eng.wait_ge(s["sum"], t + 1)
                    wait(eng, s["B"], t - W + 1)
                    eng.activation(mh[q][:, :], z[q][:, :], ACT.Relu).then_inc(s["mh"], 1)

                def result(t, h, q, last):
                    eng.wait_ge(s["B"], t + 1)
                    wait(eng, sc[q], h * 16)
                    eng.activation(res[q][:, :], B[q % 2][:, :], ACT.Copy).then_inc(s["res"], 1)
                run(eng, (3, high), (5, result))
                split.high(eng)

            @block.tensor
            def _(eng):
                def sums(t, h, q, last):
                    eng.wait_ge(s["ml"], t + 1)
                    eng.wait_ge(s["sel"], t + 1)
                    wait(eng, s["res"], t - 1)
                    eng.matmul(B[q % 2][:, :], sel[q][:, :], mh[q][:, :], start=True, stop=False)
                    eng.matmul(B[q % 2][:, :], sel[q][:, :], ml[q][:, :], start=False, stop=True)
                    eng.wait_ge(s["head"], t + 1)
                    first, end = (isinstance(t, int) and t == 0), (isinstance(t, int) and t == ET - 1)
                    eng.matmul(H[:, :], hd[q][:, :], mh[q][:, :], start=first, stop=False)
                    eng.matmul(H[:, :], hd[q][:, :], ml[q][:, :], start=False, stop=end).then_inc(s["B"], 1)
                run(eng, (4, sums))


def hidden_phase(core, cst, ed, table, eps, b1, w, layer, hT, stats):
    nc = core.nc
    wh, wl = w
    names = "eps eps1 b1 ld0 ld1 la pre T hi lo M ev bn"
    with core.phase("hidden", names) as (s, sbuf, psum):
        e_t = sbuf("eps", [P, 1])
        b1t = sbuf("b1", [P, KC])
        xin = [sbuf(f"xin{q}", [P, TILES, D]) for q in range(2)]
        agg = sbuf("agg", [P, TILES, D])
        xh = [sbuf(f"xh{q}", [P, KC, GROUP], F32R) for q in range(2)]
        xl = [sbuf(f"xl{q}", [P, KC, GROUP], F32R) for q in range(2)]
        T = [psum(f"T{q}", [P, KC, GROUP]) for q in range(2)]
        O = [psum(f"O{q}", [P, KC, GROUP]) for q in range(2)]
        ld = (s["ld0"], s["ld1"])
        at = lambda g, w_: slice(g * GROUP, g * GROUP + w_) if isinstance(g, int) else bass.ds(g * GROUP, w_)
        with nc.Block() as block:
            @block.sync
            def _(eng):
                eng.dma_start(e_t[:, :], eps[bass.ds(layer, 1)].partition_broadcast(P)).then_inc(s["eps"], 16)
                eng.dma_start(b1t[:, :], b1[bass.ds(layer, 1), :].rearrange("one (c p) -> (one p) c", p=P),
                              allow_slow_non_contiguous=True).then_inc(s["b1"], 16)

                def load(g, h, q, last):
                    wait_apart(eng, s["T"], g - 1)
                    eng.dma_start(part(xin[q], last), rows(table, g, last)).then_inc(ld[q], 16)
                    wait_apart(eng, s["pre"], g)
                    eng.dma_start(part(agg, last), rows(ed.sums[1], g, last)).then_inc(s["la"], 16)
                pipeline(eng, [(0, load)])

            @block.tensor
            def _(eng):
                def product(g, h, q, last):
                    w_ = width_of(last)
                    eng.wait_ge(s["lo"], g + 1)
                    wait(eng, s["ev"], g - 1)
                    for o in range(KC):
                        for c in range(KC):
                            cs = slice(o * P, (o + 1) * P)
                            m = three(eng, O[q][:, o, 0:w_], wh[:, c, cs], wl[:, c, cs], xh[q][:, c, 0:w_], xl[q][:, c, 0:w_],
                                      c == 0, c == KC - 1)
                    m.then_inc(s["M"], 1)
                pipeline(eng, [(0, lambda g, h, q, last: turn(eng, s, g, h, q, last, None, xin, T, cst.ident)), (1, product)])

            @block.scalar
            def _(eng):
                def evacuate(g, h, q, last):
                    w_ = width_of(last)
                    wait_apart(eng, s["M"], g + 1)
                    for o in range(KC):
                        m = eng.activation(hT[:, o, at(g, w_)], O[q][:, o, 0:w_], ACT.Identity, bias=b1t[:, o:o + 1])
                    m.then_inc(s["ev"], 1)
                eng.wait_ge(s["b1"], 16)
                pipeline(eng, [(0, lambda g, h, q, last: split_hi(eng, s, g, q, last, T, xh)), (1, evacuate)])

            @block.vector
            def _(eng):
                eng.wait_ge(s["eps"], 16)
                eng.tensor_scalar(e_t[:, :], e_t[:, :], 1.0, None, ALU.add).then_inc(s["eps1"], 1)
                eng.wait_ge(s["eps1"], 1)

                def mix(g, h, q, last):
                    eng.wait_ge(ld[q], (h + 1) * 16)
                    eng.wait_ge(s["la"], (g + 1) * 16)
                    eng.scalar_tensor_tensor(part(xin[q], last), part(xin[q], last), e_t[0:REST if last else P, :], part(agg, last),
                                             ALU.mult, ALU.add).then_inc(s["pre"], 1)

                def statistics(g, h, q, last):
                    w_ = width_of(last)
                    wait_apart(eng, s["ev"], g + 1)
                    for o in range(KC):
                        m = eng.bn_stats(stats[:, o, ds1(g), :].rearrange("a one k -> a (one k)"), hT[:, o, at(g, w_)])
                    m.then_inc(s["bn"], 1)
                pipeline(eng, [(0, mix), (1, lambda g, h, q, last: split_lo(eng, s, g, q, last, T, xh, xl)), (2, statistics)])


def output_phase(core, cst, table, gamma, beta, b2, weight, layer, hT, stats):
    nc = core.nc
    names = "w whi wlo ld b2 agg var rstd sc mean aff nrm hi lo M add y st0 st1"
    with core.phase("output", names) as (s, sbuf, psum):
        _, wh, wl = weight
        gm = sbuf("gm", [P, KC])
        bt = sbuf("bt", [P, KC])
        b2t = sbuf("b2t", [P, D])
        mv = sbuf("mv", [P, KC, 2])
        rs = sbuf("rs", [P, KC])
        scl = sbuf("scl", [P, KC])
        ms = sbuf("ms", [P, KC])
        shf = sbuf("shf", [P, KC])
        hh = [sbuf(f"hh{q}", [P, KC, GROUP], F32R) for q in range(2)]
        hl = [sbuf(f"hl{q}", [P, KC, GROUP], F32R) for q in range(2)]
        y_both = sbuf("y", [P, 2, TILES, D])
        y = [y_both[:, q] for q in range(2)]
        split = Split(s, y_both.ap().rearrange("a q t d -> a (q t) d"), *weight)
        O = [psum(f"O{q}", [P, TILES, D]) for q in range(2)]
        st = (s["st0"], s["st1"])
        at = lambda g, w_: slice(g * GROUP, g * GROUP + w_) if isinstance(g, int) else bass.ds(g * GROUP, w_)
        with nc.Block() as block:
            @block.sync
            def _(eng):
                split.load(eng)
                for t, a in ((gm, gamma), (bt, beta)):
                    eng.dma_start(t[:, :], a[bass.ds(layer, 1), :].rearrange("one (c p) -> (one p) c", p=P),
                                  allow_slow_non_contiguous=True).then_inc(s["ld"], 16)
                eng.dma_start(b2t[:, :], b2[bass.ds(layer, 1), :].rearrange("one d -> (one d)").partition_broadcast(P)).then_inc(s["b2"], 16)

                def store(g, h, q, last):
                    wait_apart(eng, s["y"], g + 1)
                    eng.dma_start(rows(table, g, last), part(y[q], last)).then_inc(st[q], 16)
                pipeline(eng, [(0, store)])
                for q in range(2):
                    eng.wait_ge(st[q], 16 * (NG // 2))

            @block.gpsimd
            def _(eng):
                eng.wait_ge(s["var"], 1)
                eng.tensor_tensor(rs[:, :], mv[:, :, 1], cst.half[:, :], ALU.pow).then_inc(s["rstd"], 1)

            @block.vector
            def _(eng):
                for o in range(KC):
                    m = eng.bn_aggr(mv[:, o, :], stats[:, o, :, :].rearrange("a g k -> a (g k)"))
                m.then_inc(s["agg"], 1)
                eng.wait_ge(s["agg"], 1)
                eng.tensor_scalar(mv[:, :, 1], mv[:, :, 1], EPS, None, ALU.add).then_inc(s["var"], 1)
                eng.wait_ge(s["rstd"], 1)
                eng.wait_ge(s["ld"], 32)
                eng.tensor_tensor(scl[:, :], rs[:, :], gm[:, :], ALU.mult).then_inc(s["sc"], 1)
                eng.wait_ge(s["sc"], 1)
                eng.tensor_tensor(ms[:, :], mv[:, :, 0], scl[:, :], ALU.mult).then_inc(s["mean"], 1)
                eng.wait_ge(s["mean"], 1)
                eng.tensor_tensor(shf[:, :], bt[:, :], ms[:, :], ALU.subtract).then_inc(s["aff"], 1)
                eng.wait_ge(s["b2"], 16)

                def low(g, h, q, last):
                    w_ = width_of(last)
                    eng.wait_ge(s["hi"], g + 1)
                    eng.tensor_tensor(hl[q][:, :, 0:w_], hT[:, :, at(g, w_)], hh[q][:, :, 0:w_].bitcast(F32), ALU.subtract).then_inc(s["lo"], 1)

                def add(g, h, q, last):
                    n, k = (REST, 1) if last else (P, TILES)
                    eng.wait_ge(s["M"], g + 1)
                    wait(eng, st[q], h * 16)
                    eng.tensor_tensor(part(y[q], last), part(O[q], last), b2t[0:n, :].unsqueeze(1).to_broadcast([n, k, D]),
                                      ALU.add).then_inc(s["add"], 1)
                split.low(eng)
                pipeline(eng, [(0, low), (1, add)])

            @block.scalar
            def _(eng):
                def normal(g, h, q, last):
                    w_ = width_of(last)
                    for o in range(KC):
                        m = eng.activation(hT[:, o, at(g, w_)], hT[:, o, at(g, w_)], ACT.Relu, bias=shf[:, o:o + 1], scale=scl[:, o:o + 1])
                    m.then_inc(s["nrm"], 1)
                    eng.wait_ge(s["nrm"], g + 1)
                    wait_apart(eng, s["M"], g - 1)
                    eng.activation(hh[q][:, :, 0:w_], hT[:, :, at(g, w_)], ACT.Copy).then_inc(s["hi"], 1)

                def finish(g, h, q, last):
                    eng.wait_ge(s["add"], g + 1)
                    eng.activation(part(y[q], last), part(y[q], last), ACT.Relu).then_inc(s["y"], 1)
                split.high(eng)
                eng.wait_ge(s["aff"], 1)
                pipeline(eng, [(0, normal), (2, finish)])

            @block.tensor
            def _(eng):
                def product(g, h, q, last):
                    eng.wait_ge(s["lo"], g + 1)
                    wait(eng, s["add"], g - 1)
                    for t, n in tiles_of(last):
                        ts = slice(t * P, t * P + n)
                        for c in range(KC):
                            m = three(eng, O[q][0:n, t, :], hh[q][:, c, ts], hl[q][:, c, ts], wh[:, c, :], wl[:, c, :], c == 0, c == KC - 1)
                    m.then_inc(s["M"], 1)
                eng.wait_ge(s["wlo"], 1)
                pipeline(eng, [(0, product)])


def ternary_phase(core, cst, w_up, w_down, up, down, scales):
    nc = core.nc
    names = "ld abs sum mean clip rec sc rnd q cp T"
    with core.phase("ternary", names) as (s, sbuf, psum):
        wu = sbuf("wu", [HID, D])
        wd = sbuf("wd", [P, KC, HID])
        qu = sbuf("qu", [HID, D])
        qd = sbuf("qd", [P, KC, HID])
        bu = sbuf("bu", [HID, D], BF16)
        bd = sbuf("bd", [P, KC, HID], BF16)
        total = sbuf("total", [P, 2])
        ones = sbuf("ones", [P, P])
        inv = sbuf("inv", [P, 2])
        S = psum("S", [P, 2])
        Tu = psum("Tu", [P, KC, HID], BF16)
        Td = psum("Td", [HID, KC, P], BF16)
        with nc.Block() as block:
            @block.sync
            def _(eng):
                eng.dma_start(wu[:, :], w_up).then_inc(s["ld"], 16)
                eng.dma_start(wd[:, :, :], w_down.rearrange("(c p) h -> p c h", p=P)).then_inc(s["ld"], 16)

            @block.vector
            def _(eng):
                eng.memset(total[:, :], 0.0).then_inc(s["abs"], 1)
                eng.memset(ones[:, :], 1.0)
                eng.wait_ge(s["ld"], 32)
                eng.wait_ge(s["abs"], 1)
                eng.tensor_reduce(total[0:HID, 0:1], wu[:, :], AX.X, ALU.add, apply_absolute_value=True)
                eng.tensor_reduce(total[:, 1:2], wd.ap().rearrange("a c h -> a (c h)"), AX.X, ALU.add, apply_absolute_value=True).then_inc(s["sum"], 1)
                eng.wait_ge(s["mean"], 1)
                eng.tensor_scalar(scales[:, :], S[:, :], 1.0 / (HID * D), EPS, ALU.mult, ALU.max).then_inc(s["clip"], 1)
                eng.wait_ge(s["clip"], 1)
                eng.reciprocal(inv[:, :], scales[:, :]).then_inc(s["rec"], 1)
                eng.wait_ge(s["rec"], 1)
                eng.tensor_scalar(qu[:, :], wu[:, :], inv[0:HID, 0:1], MAGIC, ALU.mult, ALU.add)
                eng.tensor_scalar(qd[:, :, :], wd[:, :, :], inv[:, 1:2], MAGIC, ALU.mult, ALU.add).then_inc(s["rnd"], 1)
                eng.wait_ge(s["rnd"], 1)
                eng.tensor_scalar(qu[:, :], qu[:, :], MAGIC, 1.0, ALU.subtract, ALU.min)
                eng.tensor_scalar(qd[:, :, :], qd[:, :, :], MAGIC, 1.0, ALU.subtract, ALU.min).then_inc(s["rnd"], 1)
                eng.wait_ge(s["rnd"], 2)
                eng.tensor_scalar(bu[:, :], qu[:, :], -1.0, None, ALU.max)
                eng.tensor_scalar(bd[:, :, :], qd[:, :, :], -1.0, None, ALU.max).then_inc(s["q"], 1)
                eng.wait_ge(s["T"], 1)
                eng.tensor_copy(up[:, :, :], Tu[:, :, :])
                eng.tensor_copy(down[:, :], Td.ap().rearrange("h c o -> h (c o)"))

            @block.tensor
            def _(eng):
                eng.wait_ge(s["sum"], 1)
                eng.matmul(S[:, :], ones[:, :], total[:, :], start=True, stop=True).then_inc(s["mean"], 1)
                eng.wait_ge(s["q"], 1)
                for c in range(KC):
                    eng.transpose(Tu[:, c, :], bu[:, c * P:(c + 1) * P], cst.ident_b[0:HID, 0:HID])
                for c in range(KC):
                    m = eng.transpose(Td[:, c, :], bd[:, c, :], cst.ident_b[:, :])
                m.then_inc(s["T"], 1)


def quantized_phase(core, cst, x2, gnn, up, down, scales, half, out):
    nc = core.nc
    LVL = 127.0
    W, R = 8, 4
    names = ("ld0 ld1 ld2 ld3 lg0 lg1 lg2 lg3 st0 st1 st2 st3 x3 stats aggr var neg rstd nb nrm amax unit k0 "
             "lvl magic rnd clip q T qT U h0 h1 h2 am2 u2 lv2 s1 s2 q2 T2 q2T O y k")
    with core.phase("quant", names) as (s, sbuf, psum):
        def ring(n, shape, dt=F32):
            return [sbuf(f"{n}{q}", shape, dt) for q in range(R)] * (W // R)

        x3 = [sbuf(f"x3{q}", [P, TILES, D]) for q in range(W)]
        gn, nr, rd, yo = (ring(n, [P, TILES, D]) for n in ("gn", "nr", "rd", "yo"))
        xq, xqT = ring("xq", [P, TILES, D], BF16), ring("xqT", [P, KC, GROUP], BF16)
        bn, mv = ring("bn", [P, TILES, 6]), ring("mv", [P, TILES, 2])
        rs, ng, nb = (ring(n, [P, TILES]) for n in ("rs", "ng", "nb"))
        am, un, lv, k0, am2, un2, lv2, k1 = (ring(n, [P, TILES]) for n in ("am", "un", "lv", "k0", "am2", "un2", "lv2", "k1"))
        hf, hr, hs = (ring(n, [P, TILES, HID]) for n in ("hf", "hr", "hs"))
        magic = sbuf("magic", [P, 1])
        hq, hqT = ring("hq", [P, TILES, HID], BF16), ring("hqT", [HID, GROUP], BF16)
        T = psum("T", [P, KC, GROUP], BF16)
        U = psum("U", [P, TILES, HID])
        T2 = psum("T2", [HID, GROUP], BF16)
        O = psum("O", [P, TILES, D])
        ld, lg, st = ([s[f"{n}{q}"] for q in range(R)] * (W // R) for n in ("ld", "lg", "st"))
        H = lambda h, q: h * (W // R) + q // R
        nk = lambda last: (REST, 1) if last else (P, TILES)

        with nc.Block() as block:
            @block.sync
            def _(eng):
                def load(g, h, q, last):
                    wait_apart(eng, s["y"], g - W + 1)
                    wait_apart(eng, s["x3"], g - R + 1)
                    eng.dma_start(part(x3[q], last), rows(x2, g, last)).then_inc(ld[q], 16)
                    eng.dma_start(part(gn[q], last), rows(gnn, g, last)).then_inc(lg[q], 16)
                pipeline(eng, [(0, load)], ways=W)

            @block.gpsimd
            def _(eng):
                eng.memset(magic[:, :], MAGIC).then_inc(s["magic"], 1)

                def rstd(g, h, q, last):
                    n, k = nk(last)
                    row_rstd(eng, s, g, mv[q], half, rs[q], last)
                    eng.wait_ge(s["rstd"], g + 1)
                    eng.tensor_tensor(nb[q][0:n, 0:k], ng[q][0:n, 0:k], rs[q][0:n, 0:k], ALU.mult).then_inc(s["nb"], 1)

                def add(g, h, q, last):
                    eng.wait_ge(ld[q], (H(h, q) + 1) * 16)
                    eng.wait_ge(lg[q], (H(h, q) + 1) * 16)
                    eng.tensor_tensor(part(x3[q], last), part(x3[q], last), part(gn[q], last), ALU.add).then_inc(s["x3"], 1)
                pipeline(eng, [(2, rstd), (1, add)], ways=W)

            @block.vector
            def _(eng):
                def rows_stats(t):
                    def step(g, h, q, last):
                        if t == 0:
                            eng.wait_ge(s["x3"], g + 1)
                            wait(eng, s["nb"], g - R + 1)
                        for j, n in tiles_of(last):
                            if j == t:
                                m = eng.bn_stats(bn[q][0:n, t, :], x3[q][0:n, t, :])
                        if t == TILES - 1 and not last or t == 0 and last:
                            m.then_inc(s["stats"], 1)
                    return step

                def mean_and_variance(g, h, q, last):
                    wait_apart(eng, s["stats"], g + 1)
                    for t, n in tiles_of(last):
                        m = eng.bn_aggr(mv[q][0:n, t, :], bn[q][0:n, t, :])
                    m.then_inc(s["aggr"], 1)

                def variance_eps(g, h, q, last):
                    n, k = nk(last)
                    eng.wait_ge(s["aggr"], g + 1)
                    eng.tensor_scalar(ng[q][0:n, 0:k], mv[q][0:n, 0:k, 0], -1.0, None, ALU.mult)
                    eng.tensor_scalar(mv[q][0:n, 0:k, 1], mv[q][0:n, 0:k, 1], EPS, None, ALU.add).then_inc(s["var"], 1)

                def largest(g, h, q, last):
                    n, k = nk(last)
                    eng.wait_ge(s["nrm"], g + 1)
                    eng.tensor_reduce(am[q][0:n, 0:k], nr[q][0:n, 0:k, :], AX.X, ALU.max, apply_absolute_value=True).then_inc(s["amax"], 1)

                def unit(g, h, q, last):
                    n, k = nk(last)
                    eng.wait_ge(s["amax"], g + 1)
                    eng.tensor_scalar(un[q][0:n, 0:k], am[q][0:n, 0:k], EPS, 1.0 / LVL, ALU.max, ALU.mult).then_inc(s["unit"], 1)

                def levels(g, h, q, last):
                    n, k = nk(last)
                    eng.wait_ge(s["unit"], g + 1)
                    eng.reciprocal(lv[q][0:n, 0:k], un[q][0:n, 0:k]).then_inc(s["lvl"], 1)
                    eng.tensor_scalar(k0[q][0:n, 0:k], un[q][0:n, 0:k], scales[0:n, 0:1], None, ALU.mult).then_inc(s["k0"], 1)

                def clamp(g, h, q, last):
                    n, k = nk(last)
                    eng.wait_ge(s["rnd"], g + 1)
                    eng.tensor_scalar(rd[q][0:n, 0:k, :], rd[q][0:n, 0:k, :], MAGIC + LVL, MAGIC - LVL - 1, ALU.min, ALU.max).then_inc(s["clip"], 1)

                def hidden_round(g, h, q, last):
                    n, k = nk(last)
                    eng.wait_ge(s["h0"], g + 1)
                    eng.tensor_scalar(hr[q][0:n, 0:k, :], hf[q][0:n, 0:k, :], MAGIC, MAGIC, ALU.add, ALU.subtract).then_inc(s["h1"], 1)

                def hidden_clamp(g, h, q, last):
                    n, k = nk(last)
                    eng.wait_ge(s["h1"], g + 1)
                    eng.tensor_scalar(hf[q][0:n, 0:k, :], hr[q][0:n, 0:k, :], LVL, -LVL - 1, ALU.min, ALU.max).then_inc(s["h2"], 1)

                def hidden_largest(g, h, q, last):
                    n, k = nk(last)
                    eng.wait_ge(s["h2"], g + 1)
                    eng.tensor_reduce(am2[q][0:n, 0:k], hf[q][0:n, 0:k, :], AX.X, ALU.max, apply_absolute_value=True).then_inc(s["am2"], 1)

                def hidden_unit(g, h, q, last):
                    n, k = nk(last)
                    eng.wait_ge(s["am2"], g + 1)
                    eng.tensor_scalar(un2[q][0:n, 0:k], am2[q][0:n, 0:k], EPS, 1.0 / LVL, ALU.max, ALU.mult).then_inc(s["u2"], 1)

                def hidden_levels(g, h, q, last):
                    n, k = nk(last)
                    eng.wait_ge(s["u2"], g + 1)
                    eng.reciprocal(lv2[q][0:n, 0:k], un2[q][0:n, 0:k]).then_inc(s["lv2"], 1)
                    eng.tensor_scalar(k1[q][0:n, 0:k], un2[q][0:n, 0:k], scales[0:n, 1:2], None, ALU.mult).then_inc(s["k"], 1)

                def hidden_scale(g, h, q, last):
                    eng.wait_ge(s["lv2"], g + 1)
                    for t, r in tiles_of(last):
                        m = eng.tensor_scalar(hs[q][0:r, t, :], hf[q][0:r, t, :], lv2[q][0:r, t:t + 1], MAGIC, ALU.mult, ALU.add)
                    m.then_inc(s["s1"], 1)

                def hidden_level_clamp(g, h, q, last):
                    n, k = nk(last)
                    eng.wait_ge(s["s1"], g + 1)
                    eng.tensor_scalar(hr[q][0:n, 0:k, :], hs[q][0:n, 0:k, :], MAGIC + LVL, MAGIC - LVL - 1, ALU.min, ALU.max).then_inc(s["s2"], 1)

                def hidden_integers(g, h, q, last):
                    n, k = nk(last)
                    eng.wait_ge(s["s2"], g + 1)
                    wait(eng, s["T2"], g - R + 1)
                    eng.tensor_scalar(hq[q][0:n, 0:k, :], hr[q][0:n, 0:k, :], MAGIC, None, ALU.subtract).then_inc(s["q2"], 1)

                def final(t):
                    def step(g, h, q, last):
                        if t == 0:
                            eng.wait_ge(s["O"], g + 1)
                            wait(eng, st[q], H(h, q) * 16)
                            eng.wait_ge(s["k"], g + 1)
                        for j, n in tiles_of(last):
                            if j == t:
                                m = eng.scalar_tensor_tensor(yo[q][0:n, t, :], O[0:n, t, :], k1[q][0:n, t:t + 1], x3[q][0:n, t, :],
                                                             ALU.mult, ALU.add)
                        if t == TILES - 1 and not last or t == 0 and last:
                            m.then_inc(s["y"], 1)
                    return step
                pipeline(eng, [(8, final(0)), (8, final(1)), (6, hidden_round), (5, clamp), (6, hidden_clamp),
                               (2, rows_stats(0)), (6, hidden_largest), (6, hidden_unit), (2, rows_stats(1)), (6, hidden_levels), (4, largest),
                               (6, hidden_scale), (2, mean_and_variance), (4, unit), (6, hidden_level_clamp), (2, variance_eps),
                               (4, levels), (6, hidden_integers)], ways=W)

            @block.scalar
            def _(eng):
                def integers(g, h, q, last):
                    n, k = nk(last)
                    eng.wait_ge(s["clip"], g + 1)
                    wait(eng, s["T"], g - R + 1)
                    eng.activation(xq[q][0:n, 0:k, :], rd[q][0:n, 0:k, :], ACT.Copy, bias=-MAGIC).then_inc(s["q"], 1)

                def norm(g, h, q, last):
                    eng.wait_ge(s["nb"], g + 1)
                    wait(eng, s["rnd"], g - R + 1)
                    for t, r in tiles_of(last):
                        m = eng.activation(nr[q][0:r, t, :], x3[q][0:r, t, :], ACT.Identity, bias=nb[q][0:r, t:t + 1], scale=rs[q][0:r, t:t + 1])
                    m.then_inc(s["nrm"], 1)

                def scale(g, h, q, last):
                    eng.wait_ge(s["lvl"], g + 1)
                    wait(eng, s["q"], g - R + 1)
                    for t, r in tiles_of(last):
                        m = eng.activation(rd[q][0:r, t, :], nr[q][0:r, t, :], ACT.Identity, bias=magic[0:r, :], scale=lv[q][0:r, t:t + 1])
                    m.then_inc(s["rnd"], 1)

                def copy_rows(g, h, q, last):
                    w_ = width_of(last)
                    eng.wait_ge(s["T"], g + 1)
                    wait(eng, s["U"], g - R + 1)
                    eng.activation(xqT[q][:, :, 0:w_], T[:, :, 0:w_], ACT.Copy).then_inc(s["qT"], 1)

                def copy_hidden(g, h, q, last):
                    w_ = width_of(last)
                    eng.wait_ge(s["T2"], g + 1)
                    wait(eng, s["O"], g - R + 1)
                    eng.activation(hqT[q][:, 0:w_], T2[:, 0:w_], ACT.Copy).then_inc(s["q2T"], 1)

                def relu(g, h, q, last):
                    eng.wait_ge(s["U"], g + 1)
                    wait(eng, s["q2"], g - R + 1)
                    eng.wait_ge(s["k0"], g + 1)
                    for t, r in tiles_of(last):
                        m = eng.activation(hf[q][0:r, t, :], U[0:r, t, :], ACT.Relu, scale=k0[q][0:r, t:t + 1])
                    m.then_inc(s["h0"], 1)

                def store(g, h, q, last):
                    eng.wait_ge(s["y"], g + 1)
                    eng.dma_start(rows(out, g, last), part(yo[q], last)).then_inc(st[q], 16)
                eng.wait_ge(s["magic"], 1)
                pipeline(eng, [(5, integers), (7, copy_hidden), (3, norm), (5, copy_rows), (4, scale), (5, relu), (8, store)], ways=W)
                for q in range(R):
                    eng.wait_ge(st[q], 16 * (NG // R))

            @block.tensor
            def _(eng):
                def turn_hidden(g, h, q, last):
                    eng.wait_ge(s["q2"], g + 1)
                    wait_apart(eng, s["q2T"], g)
                    for t, n in tiles_of(last):
                        m = eng.transpose(T2[:, t * P:t * P + n], hq[q][0:n, t, :], cst.ident_b[0:n, 0:n])
                    m.then_inc(s["T2"], 1)

                def down_(g, h, q, last):
                    eng.wait_ge(s["q2T"], g + 1)
                    wait(eng, s["y"], g)
                    for t, n in tiles_of(last):
                        m = eng.matmul(O[0:n, t, :], hqT[q][:, t * P:t * P + n], down[:, :], start=True, stop=True)
                    m.then_inc(s["O"], 1)

                def turn_rows(g, h, q, last):
                    eng.wait_ge(s["q"], g + 1)
                    wait(eng, s["qT"], g)
                    for t, n in tiles_of(last):
                        for c in range(KC):
                            m = eng.transpose(T[:, c, t * P:t * P + n], xq[q][0:n, t, c * P:(c + 1) * P], cst.ident_b[0:n, 0:n])
                    m.then_inc(s["T"], 1)

                def up_(g, h, q, last):
                    eng.wait_ge(s["qT"], g + 1)
                    wait(eng, s["h0"], g)
                    for t, n in tiles_of(last):
                        for c in range(KC):
                            m = eng.matmul(U[0:n, t, :], xqT[q][:, c, t * P:t * P + n], up[:, c, :], start=c == 0, stop=c == KC - 1)
                    m.then_inc(s["U"], 1)
                pipeline(eng, [(7, turn_hidden), (7, down_), (5, turn_rows), (5, up_)], ways=W)


def scratch(nc, name, shape):
    return nc.dram_tensor(name, shape, F32).ap()


def first_gnn(core, cst, ed, a, x, normed, hidden, rows_out, normed_out):
    nc = core.nc
    for n, table in ((1, normed), (2, hidden)):
        with nc.sbuf_tensor(f"root_hi{n}", [P, KC, D], F32R) as hi, nc.sbuf_tensor(f"root_lo{n}", [P, KC, D], F32R) as lo:
            with nc.sbuf_tensor(f"w_hi{n}", [P, RELATIONS * KC, D], F32R) as w_hi, \
                    nc.sbuf_tensor(f"w_lo{n}", [P, RELATIONS * KC, D], F32R) as w_lo:
                combine_phase(core, cst, a[f"L0_gnn_basis{n}"], a[f"L0_gnn_att{n}"], w_hi, w_lo)
                relation_phase(core, cst, ed, table, a[f"L0_gnn_gate_w{n}"], w_hi, w_lo,
                               (chunked(a[f"L0_gnn_root{n}"]), hi, lo), ed.sums[1] if n == 1 else None)
            if n == 1:
                root_phase(core, cst, ed, normed, (hi, lo), a["L0_gnn_bias1"], cst.half, hidden)
            else:
                root_phase(core, cst, ed, hidden, (hi, lo), a["L0_gnn_bias2"], cst.half, rows_out, x, normed_out)


def first_ffn(core, cst, a, x, normed, probs, rows_out, normed_out):
    nc = core.nc
    table, ends = scratch(nc, "slot_table", (EXPERTS * NB, 2 * BLOCK)), scratch(nc, "slot_ends", (EXPERTS * NB,))
    tokens_phase(core, cst, normed, x, a["L0_ffn_gate_w"], a["L0_ffn_sw1"], a["L0_ffn_sb1"], a["L0_ffn_sw2"], a["L0_ffn_sb2"],
                 probs, rows_out)
    select_phase(core, cst, probs, table, ends)
    with nc.sbuf_tensor("slot_token", [SL, ST], U32) as token, nc.sbuf_tensor("slot_score", [SL, ST], F32) as score:
        slots_phase(core, table, ends, token, score)
        routed_phase(core, cst, normed, a["L0_ffn_w1"], a["L0_ffn_b1"], a["L0_ffn_w2"], a["L0_ffn_b2"], token, score, rows_out)
    norm_phase(core, rows_out, normed_out, cst.half)


def second_gnn(core, cst, ed, a, g):
    nc = core.nc
    with nc.Fori(0, LAYERS) as layer:
        def weight(name):
            return a[name][bass.ds(layer, 1)].rearrange("one (c p) n -> (one p) c n", p=P)

        with nc.sbuf_tensor("w_hi", [P, KC, D], F32R) as hi, nc.sbuf_tensor("w_lo", [P, KC, D], F32R) as lo:
            message_phase(core, cst, ed, g, a["L1_gnn_We"], a["L1_gnn_be"], layer, (weight("L1_gnn_W1"), hi, lo))
            with nc.sbuf_tensor("hT", [P, KC, N], F32) as hT, nc.sbuf_tensor("h_stats", [P, KC, NG, 6], F32) as stats:
                hidden_phase(core, cst, ed, g, a["L1_gnn_eps"], a["L1_gnn_b1"], (hi, lo), layer, hT, stats)
                output_phase(core, cst, g, a["L1_gnn_gamma"], a["L1_gnn_beta"], a["L1_gnn_b2"],
                             (weight("L1_gnn_W2"), hi, lo), layer, hT, stats)


def second_ffn(core, cst, a, x, g, out):
    nc = core.nc
    with nc.sbuf_tensor("up", [P, KC, HID], BF16) as up, nc.sbuf_tensor("down", [HID, D], BF16) as down, \
            nc.sbuf_tensor("scales", [P, 2], F32) as scales:
        ternary_phase(core, cst, a["L1_ffn_w_up"], a["L1_ffn_w_down"], up, down, scales)
        quantized_phase(core, cst, x, g, up, down, scales, cst.half, out)


def build(nc, a, out):
    core = Core(nc)
    ed = Edges(nc)
    normed0, hidden, x1, normed1 = (scratch(nc, n, (N, D)) for n in ("normed0", "hidden", "x1", "normed1"))
    x2, g = scratch(nc, "x2", (N, D)), scratch(nc, "g", (N, D))
    probs = scratch(nc, "probs", (EXPERTS, N))
    with ExitStack() as early:
        cst = Constants(core, early)
        order_phase(core, ed, cst, a["src"], a["dst"], a["edge_type_2"], a["edge_weight1"], a["x"], normed0)
        first_gnn(core, cst, ed, a, a["x"], normed0, hidden, x1, normed1)
        first_ffn(core, cst, a, x1, normed1, probs, x2, g)
    second_gnn(core, cst, ed, a, g)
    second_ffn(core, cst, a, x2, g, out)


_INS = """x src dst edge_type_2 edge_weight1 L0_gnn_basis1 L0_gnn_att1 L0_gnn_gate_w1 L0_gnn_root1 L0_gnn_bias1
    L0_gnn_basis2 L0_gnn_att2 L0_gnn_gate_w2 L0_gnn_root2 L0_gnn_bias2 L0_ffn_gate_w L0_ffn_w1 L0_ffn_b1 L0_ffn_w2
    L0_ffn_b2 L0_ffn_sw1 L0_ffn_sb1 L0_ffn_sw2 L0_ffn_sb2 L1_gnn_eps L1_gnn_We L1_gnn_be L1_gnn_W1 L1_gnn_b1
    L1_gnn_gamma L1_gnn_beta L1_gnn_W2 L1_gnn_b2 L1_ffn_w_up L1_ffn_w_down""".split()


def kernel(**inputs):
    import numpy as np
    import concourse.bacc as bacc
    from concourse.bass_utils import run_bass_kernel_spmd

    nc = bacc.Bacc("TRN2", target_bir_lowering=False, num_devices=1)
    arrays, args = {}, {}
    for name in _INS:
        v = np.ascontiguousarray(inputs[name])
        arrays[f"in_{name}"] = v
        args[name] = nc.dram_tensor(f"in_{name}", v.shape, mybir.dt.from_np(v.dtype), kind="ExternalInput").ap()
    out = nc.dram_tensor("out", (N, D), F32, kind="ExternalOutput").ap()
    build(nc, args, out)
    r = run_bass_kernel_spmd(nc, [arrays], core_ids=[0])
    return r.results[0]["out"]
```
